# Optimizing a Trainium2 kernel written in Bass

```python
import numpy as np
import jax
import jax.numpy as jnp

def _softmax(x, axis=-1):
    return jax.nn.softmax(x, axis=axis)

def _gelu(x):
    return jax.nn.gelu(x, approximate=True)

def _silu(x):
    return jax.nn.silu(x)

def _sigmoid(x):
    return jax.nn.sigmoid(x)

def _layernorm(x, axis=-1, eps=1e-05):
    m = jnp.mean(x, axis=axis, keepdims=True)
    v = jnp.var(x, axis=axis, keepdims=True)
    return (x - m) / jnp.sqrt(v + eps)

def _scatter_add(tgt, idx, src, axis=0):
    return tgt.at[idx].add(src)

def _segment_sum(src, seg, n):
    return jax.ops.segment_sum(src, seg, n)
kernel_name = 'mk_prb_d2_jaxref_r4_3f01c6'

def setup_inputs(seed: int=0):
    np.random.seed(seed)
    _w = jnp.asarray

    def _L0_attn_setup():
        import jax, jax.numpy as jnp
        import numpy as np
        D_MODEL = 256
        D_QK = 256
        H = 16
        HEAD_DIM = D_QK // H
        V_DIM = D_MODEL // H
        B, S = (2, 512)
        key = jax.random.key(seed)
        ks = jax.random.split(key, 9)
        sd = 1.0 / np.sqrt(D_MODEL)
        return {'x': jax.random.normal(ks[0], (B, S, D_MODEL), dtype=jnp.float32), 'Wqk_w': jax.random.normal(ks[1], (2 * D_QK, D_MODEL), dtype=jnp.float32) * sd, 'Wqk_b': jax.random.normal(ks[2], (2 * D_QK,), dtype=jnp.float32) * 0.01, 'Wv_w': jax.random.normal(ks[3], (D_MODEL, D_MODEL), dtype=jnp.float32) * sd, 'Wv_b': jax.random.normal(ks[4], (D_MODEL,), dtype=jnp.float32) * 0.01, 'Wn_w': jax.random.normal(ks[5], (H, D_MODEL), dtype=jnp.float32) * sd, 'Wn_b': jax.random.normal(ks[6], (H,), dtype=jnp.float32) * 0.01, 'Wo_w': jax.random.normal(ks[7], (D_MODEL, D_MODEL), dtype=jnp.float32) * sd, 'Wo_b': jax.random.normal(ks[8], (D_MODEL,), dtype=jnp.float32) * 0.01}
    _L0_attn_in = _L0_attn_setup()

    def _L0_ffn_setup():
        import jax, jax.numpy as jnp
        import numpy as np
        E = 32
        K = 4
        H = 256
        I = 128
        B, S = (2, 512)
        T = B * S
        C = 256
        ROUTED_SCALE = 1.0

        def _silu_and_mul(gu):
            g, u = jnp.split(gu, 2, axis=-1)
            return jax.nn.silu(g) * u
        key = jax.random.key(seed)
        ks = jax.random.split(key, 6)
        s = 0.02
        return {'hidden_states': jax.random.normal(ks[0], (B, S, H), jnp.float32), 'gate_w': jax.random.normal(ks[1], (E, H), jnp.float32) * s, 'w_gate_up': jax.random.normal(ks[2], (E, H, 2 * I), jnp.float32) * s, 'w_down': jax.random.normal(ks[3], (E, I, H), jnp.float32) * s, 'shared_w_gate_up': jax.random.normal(ks[4], (H, 2 * I), jnp.float32) * s, 'shared_w_down': jax.random.normal(ks[5], (I, H), jnp.float32) * s}
    _L0_ffn_in = _L0_ffn_setup()

    def _L1_attn_setup():
        import jax, jax.numpy as jnp
        import numpy as np
        B, T, D = (4, 2048, 256)
        H = 16
        HD = D // H
        TOP_K = 64
        key = jax.random.key(seed)
        ks = jax.random.split(key, 6)
        x = jax.random.normal(ks[0], (B, T, D), dtype=jnp.float32)
        Wq = jax.random.normal(ks[1], (D, D), dtype=jnp.float32) * 0.02
        Wk = jax.random.normal(ks[2], (D, D), dtype=jnp.float32) * 0.02
        Wv = jax.random.normal(ks[3], (D, D), dtype=jnp.float32) * 0.02
        Wo = jax.random.normal(ks[4], (D, D), dtype=jnp.float32) * 0.02
        w_score = jax.random.normal(ks[5], (HD,), dtype=jnp.float32) * 0.02
        return {'x': x, 'Wq': Wq, 'Wk': Wk, 'Wv': Wv, 'Wo': Wo, 'w_score': w_score}
    _L1_attn_in = _L1_attn_setup()

    def _L1_ffn_setup():
        import jax, jax.numpy as jnp
        import numpy as np
        DIM = 256
        HIDDEN = 768
        SCALE = 1.0 / 127.0

        def _dequant(w_int, dtype):
            return w_int.astype(dtype) * jnp.asarray(SCALE, dtype)
        key = jax.random.key(seed)
        k_x, k_g, k_u, k_d = jax.random.split(key, 4)
        x = jax.random.normal(k_x, (4, 512, DIM), dtype=jnp.float32)
        w_gate = jax.random.randint(k_g, (HIDDEN, DIM), -127, 128, dtype=jnp.int32)
        w_up = jax.random.randint(k_u, (HIDDEN, DIM), -127, 128, dtype=jnp.int32)
        w_down = jax.random.randint(k_d, (DIM, HIDDEN), -127, 128, dtype=jnp.int32)
        return {'x': x, 'w_gate': w_gate, 'w_up': w_up, 'w_down': w_down}
    _L1_ffn_in = _L1_ffn_setup()
    _d = {'L0_attn_x': _L0_attn_in['x'], 'L0_attn_Wqk_w': _L0_attn_in['Wqk_w'], 'L0_attn_Wqk_b': _L0_attn_in['Wqk_b'], 'L0_attn_Wv_w': _L0_attn_in['Wv_w'], 'L0_attn_Wv_b': _L0_attn_in['Wv_b'], 'L0_attn_Wn_w': _L0_attn_in['Wn_w'], 'L0_attn_Wn_b': _L0_attn_in['Wn_b'], 'L0_attn_Wo_w': _L0_attn_in['Wo_w'], 'L0_attn_Wo_b': _L0_attn_in['Wo_b'], 'L0_ffn_gate_w': _L0_ffn_in['gate_w'], 'L0_ffn_w_gate_up': _L0_ffn_in['w_gate_up'], 'L0_ffn_w_down': _L0_ffn_in['w_down'], 'L0_ffn_shared_w_gate_up': _L0_ffn_in['shared_w_gate_up'], 'L0_ffn_shared_w_down': _L0_ffn_in['shared_w_down'], 'L1_attn_Wq': _L1_attn_in['Wq'], 'L1_attn_Wk': _L1_attn_in['Wk'], 'L1_attn_Wv': _L1_attn_in['Wv'], 'L1_attn_Wo': _L1_attn_in['Wo'], 'L1_attn_w_score': _L1_attn_in['w_score'], 'L1_ffn_w_gate': _L1_ffn_in['w_gate'], 'L1_ffn_w_up': _L1_ffn_in['w_up'], 'L1_ffn_w_down': _L1_ffn_in['w_down']}
    _x0 = _d['L0_attn_x']
    _d['L0_attn_x'] = jax.random.normal(jax.random.fold_in(jax.random.key(seed), 1), (8, 1024, 256), dtype=_x0.dtype)
    del _x0
    return _d

def reference(L0_attn_x, L0_attn_Wqk_w, L0_attn_Wqk_b, L0_attn_Wv_w, L0_attn_Wv_b, L0_attn_Wn_w, L0_attn_Wn_b, L0_attn_Wo_w, L0_attn_Wo_b, L0_ffn_gate_w, L0_ffn_w_gate_up, L0_ffn_w_down, L0_ffn_shared_w_gate_up, L0_ffn_shared_w_down, L1_attn_Wq, L1_attn_Wk, L1_attn_Wv, L1_attn_Wo, L1_attn_w_score, L1_ffn_w_gate, L1_ffn_w_up, L1_ffn_w_down):

    def _L0_attn_ref(x, Wqk_w, Wqk_b, Wv_w, Wv_b, Wn_w, Wn_b, Wo_w, Wo_b):
        import jax, jax.numpy as jnp
        import numpy as np
        D_MODEL = 256
        D_QK = 256
        H = 16
        HEAD_DIM = D_QK // H
        V_DIM = D_MODEL // H
        B, S = (2, 512)
        b, s, _ = x.shape
        qk = x @ Wqk_w.T + Wqk_b
        qk = qk.reshape(b, s, 2, H, HEAD_DIM)
        q, k = (qk[:, :, 0], qk[:, :, 1])
        v = (x @ Wv_w.T + Wv_b).reshape(b, s, H, V_DIM)
        n = jnp.exp(-(x @ Wn_w.T + Wn_b))
        kv = jnp.einsum('bshd,bsht->bshdt', k, v)
        kv = jnp.cumsum(kv, axis=1)
        out = jnp.einsum('bshd,bshdt->bsht', q, kv)
        out = n[..., None] * out
        out = out.reshape(b, s, D_MODEL)
        return out @ Wo_w.T + Wo_b

    def _L0_ffn_ref(hidden_states, gate_w, w_gate_up, w_down, shared_w_gate_up, shared_w_down):
        import jax, jax.numpy as jnp
        import numpy as np
        E = 32
        K = 4
        H = 256
        I = 128
        B, S = (2, 512)
        T = B * S
        C = 256
        ROUTED_SCALE = 1.0

        def _silu_and_mul(gu):
            g, u = jnp.split(gu, 2, axis=-1)
            return jax.nn.silu(g) * u
        b, s, h = hidden_states.shape
        x = hidden_states.reshape(-1, h)
        t = x.shape[0]
        logits = x @ gate_w.T
        probs = jax.nn.softmax(logits, axis=-1)
        topk_w, topk_idx = jax.lax.top_k(probs, K)
        topk_w = topk_w / jnp.sum(topk_w, axis=-1, keepdims=True)
        topk_w = topk_w * ROUTED_SCALE
        e_flat = topk_idx.reshape(-1)
        w_flat = topk_w.reshape(-1)
        t_flat = jnp.repeat(jnp.arange(t), K)
        order = jnp.argsort(e_flat)
        e_s, w_s, t_s = (e_flat[order], w_flat[order], t_flat[order])
        counts = jax.ops.segment_sum(jnp.ones_like(e_s), e_s, num_segments=E)
        starts = jnp.cumsum(counts) - counts
        pos = jnp.arange(t * K) - starts[e_s]
        slot = jnp.minimum(pos, C)
        buf = jnp.zeros((E, C + 1, h), x.dtype).at[e_s, slot].set(x[t_s])
        gu = jnp.einsum('ech,ehi->eci', buf[:, :C], w_gate_up)
        expert_out = jnp.einsum('eci,eih->ech', _silu_and_mul(gu), w_down)
        expert_out = jnp.pad(expert_out, ((0, 0), (0, 1), (0, 0)))
        gate = jnp.where(pos < C, w_s, 0.0)[:, None]
        routed = jnp.zeros_like(x).at[t_s].add(expert_out[e_s, slot] * gate)
        shared = _silu_and_mul(x @ shared_w_gate_up) @ shared_w_down
        return (routed + shared).reshape(b, s, h)

    def _L1_attn_ref(x, Wq, Wk, Wv, Wo, w_score):
        import jax, jax.numpy as jnp
        import numpy as np
        B, T, D = (4, 2048, 256)
        H = 16
        HD = D // H
        TOP_K = 64
        b, t, d = x.shape
        top_k = min(TOP_K, t)

        def proj(W):
            return jnp.einsum('btd,ed->bte', x, W).reshape(b, t, H, HD).transpose(0, 2, 1, 3)
        q = proj(Wq)
        k = proj(Wk)
        v = proj(Wv)
        idx_scores = jnp.einsum('bhtd,d->bht', k, w_score)
        _, top_idx = jax.lax.top_k(idx_scores, top_k)
        idx = top_idx[..., None]
        k_sparse = jnp.take_along_axis(k, idx, axis=2)
        v_sparse = jnp.take_along_axis(v, idx, axis=2)
        scale = HD ** (-0.5)
        scores = jnp.einsum('bhtd,bhkd->bhtk', q, k_sparse) * scale
        attn = jax.nn.softmax(scores, axis=-1)
        out = jnp.einsum('bhtk,bhkd->bhtd', attn, v_sparse)
        out = out.transpose(0, 2, 1, 3).reshape(b, t, d)
        return jnp.einsum('btd,ed->bte', out, Wo)

    def _L1_ffn_ref(x, w_gate, w_up, w_down):
        import jax, jax.numpy as jnp
        import numpy as np
        DIM = 256
        HIDDEN = 768
        SCALE = 1.0 / 127.0

        def _dequant(w_int, dtype):
            return w_int.astype(dtype) * jnp.asarray(SCALE, dtype)
        wg = _dequant(w_gate, x.dtype)
        wu = _dequant(w_up, x.dtype)
        wd = _dequant(w_down, x.dtype)
        gate = jnp.einsum('bsd,hd->bsh', x, wg)
        up = jnp.einsum('bsd,hd->bsh', x, wu)
        h = jax.nn.silu(gate) * up
        return jnp.einsum('bsh,dh->bsd', h, wd)
    x = L0_attn_x
    xn = _layernorm(x, axis=-1)
    x = x + _L0_attn_ref(xn, L0_attn_Wqk_w, L0_attn_Wqk_b, L0_attn_Wv_w, L0_attn_Wv_b, L0_attn_Wn_w, L0_attn_Wn_b, L0_attn_Wo_w, L0_attn_Wo_b) + _L0_ffn_ref(xn, L0_ffn_gate_w, L0_ffn_w_gate_up, L0_ffn_w_down, L0_ffn_shared_w_gate_up, L0_ffn_shared_w_down)
    xn = _layernorm(x, axis=-1)
    x = x + _L1_attn_ref(xn, L1_attn_Wq, L1_attn_Wk, L1_attn_Wv, L1_attn_Wo, L1_attn_w_score) + _L1_ffn_ref(xn, L1_ffn_w_gate, L1_ffn_w_up, L1_ffn_w_down)
    return x

_drawn_inputs = setup_inputs


def setup_inputs(seed=0):
    import zlib

    import numpy as np

    out = dict(_drawn_inputs(seed))
    spreads = {}
    factors = {'L0_attn_Wqk_b': 3.432,
     'L0_attn_Wv_b': 6.641,
     'L0_attn_Wn_b': 5.039,
     'L0_attn_Wo_b': 64.0,
     'L0_ffn_gate_w': 8.0,
     'L0_ffn_w_gate_up': 8.0,
     'L0_ffn_w_down': 8.0,
     'L0_ffn_shared_w_gate_up': 8.0,
     'L0_ffn_shared_w_down': 8.0,
     'L1_attn_Wq': 64.0,
     'L1_attn_Wk': 64.0,
     'L1_attn_Wv': 64.0,
     'L1_attn_Wo': 64.0,
     'L1_attn_w_score': 64.0}
    for name, (base, spread) in spreads.items():
        noise = np.random.default_rng([zlib.crc32(name.encode()), seed]).standard_normal(out[name].shape)
        drawn = base * np.exp(spread * noise) if base else spread * noise
        out[name] = jnp.asarray(drawn.astype(out[name].dtype))
    for name, factor in factors.items():
        out[name] = (out[name] * factor).astype(out[name].dtype)
    return out
```

```python
from contextlib import ExitStack

import numpy as np

import concourse.bass as bass
from concourse import mybir

ALU = mybir.AluOpType
ACT = mybir.ActivationFunctionType
AX_X = mybir.AxisListType.X
F32 = mybir.dt.float32
BF16 = mybir.dt.bfloat16
I32 = mybir.dt.int32

P = 128
BATCH, SEQ, D = 8, 1024, 256
TOKENS = BATCH * SEQ
NT = TOKENS // P
BT = SEQ // P
KC = D // P
H, HD = 16, 16
NE, TOPE, CAP = 32, 4, 256
EPS = 1e-5
BIG = 3.0e38

PK, PV, PQ, PN, PL, PW = 0, 256, 512, 768, 784, 816
XW = D + NE
DUMP = TOKENS
ROWS = TOKENS + P

_C = {}
_w = 0
for _name, _n in (("ident", P), ("causal", P), ("strict", P), ("block", P), ("even", 1), ("odd", 1),
                  ("part", 1), ("dump", 1), ("tile1", NT), ("iota16", 16), ("ediag", 8), ("lowkeys", 1),
                  ("highkeys", 1), ("keybase", 1)):
    _C[_name] = (_w, _w + _n)
    _w += _n
CW = _w


def shape_constants():
    c = np.zeros((P, CW), np.float32)
    i, j = np.arange(P)[:, None], np.arange(P)[None, :]

    def put(name, v):
        a, b = _C[name]
        c[:, a:b] = v

    put("ident", i == j)
    put("causal", i <= j)
    put("strict", i < j)
    put("block", i // HD == j // HD)
    put("even", i // HD % 2 == 0)
    put("odd", i // HD % 2 == 1)
    put("part", i)
    put("dump", DUMP + i + P)
    put("tile1", np.arange(NT)[None, :] + 1)
    put("iota16", np.arange(16)[None, :])
    put("ediag", i // 16 == np.arange(8)[None, :])
    put("lowkeys", i < 64)
    put("highkeys", i >= 64)
    put("keybase", i // H * (SEQ * H) + i % H)
    return c


class Chain:

    def __init__(self, eng, sem, base=0):
        self.eng, self.sem, self.base, self.k = eng, sem, base, 0

    def mark(self, ins):
        self.k += 1
        ins.then_inc(self.sem, 1)
        return self.k

    def wait(self, k=None):
        self.eng.wait_ge(self.sem, self.base + (self.k if k is None else k))


LN_MARKS = 15


def layernorm_stats(dve, step, x_all, ln, tile0, n):
    ve, r, t = ln["ve"][:, 0:n], ln["r"][:, 0:n], ln["t"][:, 0:n]
    for k in range(n):
        last = dve.bn_stats(ln["st"][:, k, :], x_all[:, tile0 + k, :])
    step.mark(last)
    step.wait()
    step.mark(dve.memset(ve, EPS))
    for k in range(n):
        last = dve.bn_aggr(ln["mv"][:, k, :], ln["st"][:, k, :])
    step.mark(last)
    step.wait()
    step.mark(dve.tensor_tensor(ve, ve, ln["mv"][:, 0:n, 1], ALU.add))
    step.wait()
    step.mark(dve.tensor_scalar(t.bitcast(I32), ve.bitcast(I32), 1, None, ALU.arith_shift_right))
    step.wait()
    step.mark(dve.tensor_scalar(r.bitcast(I32), t.bitcast(I32), -1, 0x5F3759DF, ALU.mult, ALU.add))
    step.wait()
    for k in range(3):
        dst = r if k < 2 else ln["rstd"][:, bass.ds(tile0, n)]
        step.mark(dve.tensor_tensor(t, r, r, ALU.mult))
        step.wait()
        step.mark(dve.scalar_tensor_tensor(out=t, in0=t, scalar=-0.5, in1=ve, op0=ALU.mult, op1=ALU.mult))
        step.wait()
        last = dve.scalar_tensor_tensor(out=dst, in0=t, scalar=1.5, in1=r, op0=ALU.add, op1=ALU.mult)
        if k < 2:
            step.mark(last)
            step.wait()
    step.mark(last)
    step.wait()
    return dve.scalar_tensor_tensor(out=ln["nmr"][:, bass.ds(tile0, n)], in0=ln["mv"][:, 0:n, 0], scalar=-1.0,
                                    in1=ln["rstd"][:, bass.ds(tile0, n)], op0=ALU.mult, op1=ALU.mult)


def bcast(ap, axis, n):
    return ap.unsqueeze(axis).broadcast_to([*ap.shape[:axis], n, *ap.shape[axis:]])


def layer0_dense(nc, g, ins, dram):
    with ExitStack() as ctx:
        def sb(name, shape, dt=F32):
            return ctx.enter_context(nc.sbuf_tensor(name, shape, dt))

        def sem(name):
            return ctx.enter_context(nc.semaphore(name))

        cst, x_all, ln, place = g["cst"], g["x_all"], g["ln"], g["place"]
        wproj = sb("wproj", [P, KC, PW])
        bproj = sb("bproj", [P, PW])
        wo = sb("wo", [P, KC, D])
        bo = sb("bo", [P, D])
        wsu = sb("wsu", [P, KC, D])
        wsd = sb("wsd", [P, D])
        xn = sb("xn", [P, 2, XW])
        xnT = sb("xnT", [P, 2, KC, P])
        k_sb = sb("k_sb", [P, 2, D])
        vz = sb("vz", [P, 2, H // 2, 64])
        q_in = sb("q_in", [P, 2, 308])
        qs = sb("qs", [P, 2, D])
        qkT = sb("qkT", [P, 2, 4, P])
        qbd = sb("qbd", [P, 2, KC, 8, P])
        at = sb("at", [P, 2, H, P])
        sbd = sb("sbd", [P, 2, KC, P])
        oT = sb("oT", [P, 2, KC, P])
        hT = sb("hT", [P, 2, P])
        th = sb("th", [P, P])
        hg = sb("hg", [P, P])
        nexp = sb("nexp", [P, H])
        elog = sb("elog", [P, NE])
        ewm = sb("ewm", [P, NE])
        top8 = sb("top8", [P, 8])
        negmax = sb("negmax", [P, 1])
        rep = sb("rep", [P, NE + 4])
        ssum = sb("ssum", [P, 1])
        rsum = sb("rsum", [P, 1])
        far = sb("far", [P, NE])
        maskb = sb("maskb", [P, 2, NE], BF16)
        msum = sb("msum", [P, 8, NE], BF16)
        strictb = sb("strictb", [P, P], BF16)
        onesb = sb("onesb", [P, P], BF16)
        zrow = sb("zrow", [P, XW])
        b_tg, b_kv, b_q, b_t2, b_a0, b_a1, b_o, b_s = g["banks"]
        b_a = (b_a0, b_a1)

        w_loaded = sem("w_loaded")
        x_loaded = sem("x_loaded")
        consts_ready = sem("consts_ready")
        zeros_stored = sem("zeros_stored")
        ln_done = sem("ln_done")
        xn_done = sem("xn_done")
        xn_stored = [sem("xn_stored0"), sem("xn_stored1")]
        x1_stored = sem("x1_stored")
        xb_done = sem("xb_done")
        t1_done = sem("t1_done")
        xnT_done = sem("xnT_done")
        kvp_done = sem("kvp_done")
        qp_done = sem("qp_done")
        kv_done = sem("kv_done")
        qin_done = sem("qin_done")
        negmax_done = sem("negmax_done")
        mask_done = sem("mask_done")
        nexp_done = sem("nexp_done")
        elog_done = sem("elog_done")
        qs_done = sem("qs_done")
        weights_done = sem("weights_done")
        t2_done = sem("t2_done")
        qkT_done = sem("qkT_done")
        spread_done = sem("spread_done")
        s_done = sem("s_done")
        sbd_done = sem("sbd_done")
        a_done = sem("a_done")
        am_done = sem("am_done")
        gu_done = sem("gu_done")
        tanh_done = sem("tanh_done")
        h_done = sem("h_done")
        o_done = sem("o_done")
        oT_done = sem("oT_done")
        pos_done = sem("pos_done")
        place_done = sem("place_done")
        y_done = sem("y_done")
        x1_done = sem("x1_done")
        dstep = sem("dstep")
        block = ctx.enter_context(nc.Block())

        xt = ins["x"].rearrange("b (c p) d -> b p c d", p=P)
        rows_v = dram["xrows"].rearrange("(t p) w -> t p w", p=P)
        x1_v = dram["x1"].rearrange("(t p) w -> t p w", p=P)
        ident = cst[:, _C["ident"][0]:_C["ident"][1]]
        causal = cst[:, _C["causal"][0]:_C["causal"][1]]
        blockm = cst[:, _C["block"][0]:_C["block"][1]]
        headm = cst[:, _C["ediag"][0]:_C["ediag"][1]]

        def batches(eng, body):
            with eng.Fori(0, BATCH - 1) as b:
                body(b, False)
            body(BATCH - 1, True)

        @block.sync
        def _(sp):
            sp.dma_start(cst[:, :], ins["cst"]).then_inc(w_loaded, 16)
            sp.dma_start(x_all[:, 0:BT, :], xt[0]).then_inc(x_loaded, 16)
            for dst, src in ((wproj, "wproj"), (wo, "wo"), (wsu, "wsu")):
                sp.dma_start(dst[:, :, :], ins[src].rearrange("(k p) n -> p k n", p=P)).then_inc(w_loaded, 16)
            for dst, src in ((bproj, "bproj"), (bo, "bo"), (wsd, "wsd")):
                sp.dma_start(dst[:, :], ins[src]).then_inc(w_loaded, 16)
            for b in range(1, BATCH):
                sp.wait_ge(x_loaded, 16 * b)
                sp.dma_start(x_all[:, b * BT:(b + 1) * BT, :], xt[b]).then_inc(x_loaded, 16)
            sp.wait_ge(consts_ready, 1)
            sp.dma_start(rows_v[NT], zrow[:, :]).then_inc(zeros_stored, 16)
            sp.dma_start(x1_v[NT], zrow[:, 0:D]).then_inc(zeros_stored, 16)

            def store_row(m, par, half):
                sp.wait_ge(weights_done, m + 1)
                sp.dma_start(rows_v[m], xn[:, par, :]).then_inc(xn_stored[par], 16)

            store_row(0, 0, 0)

            def body(b, last):
                for c in range(BT):
                    n = b * BT + c
                    if not (last and c == BT - 1):
                        store_row(n + 1, (c + 1) % 2, 0)
                    sp.wait_ge(x1_done, n + 1)
                    sp.dma_start(x1_v[n], x_all[:, n, :]).then_inc(x1_stored, 16)

            batches(sp, body)
            for par in range(2):
                sp.wait_ge(xn_stored[par], 16 * NT // 2)
            sp.wait_ge(x1_stored, 16 * NT)
            sp.wait_ge(zeros_stored, 32)

        @block.gpsimd
        def _(pool):
            def spread_heads(n, par):
                pool.wait_ge(qkT_done, n + 1)
                for hf in range(KC):
                    pool.tensor_tensor(qbd[:, par, hf, :, :], bcast(qkT[:, par, hf, :], 1, 8), bcast(headm, 2, P),
                                       ALU.mult).then_inc(spread_done, 1)

            def add_out_bias(n):
                pool.wait_ge(xn_done, n + 1)
                pool.tensor_tensor(x_all[:, n, :], x_all[:, n, :], bo[:, :], ALU.add).then_inc(xb_done, 1)

            pool.wait_ge(w_loaded, 16 * 7)
            pool.wait_ge(consts_ready, 1)

            def body(b, last):
                for c in range(BT):
                    n = b * BT + c
                    add_out_bias(n)
                    spread_heads(n, c % 2)

            batches(pool, body)

        @block.scalar
        def _(act):
            def norm(k, par, first):
                if not first:
                    act.wait_ge(t1_done, k - 1)
                    act.wait_ge(xn_stored[par], 16 * (k // 2) if isinstance(k, int) else 0)
                act.activation(xn[:, par, 0:D], x_all[:, k, :], ACT.Identity, bias=ln["nmr"][:, bass.ds(k, 1)],
                               scale=ln["rstd"][:, bass.ds(k, 1)]).then_inc(xn_done, 1)

            def put_xnT(m, par):
                act.wait_ge(t1_done, m + 1)
                act.copy(xnT[:, par, :, :], b_tg[:, 0:256].rearrange("p (k t) -> p k t", k=KC)).then_inc(xnT_done, 1)

            def put_qkT(n, par):
                act.wait_ge(t2_done, n + 1)
                act.copy(qkT[:, par, :, :], b_t2[:, :].rearrange("p (k t) -> p k t", k=4)).then_inc(qkT_done, 1)

            def exps(m, par):
                act.wait_ge(qin_done, m + 1)
                act.activation(nexp[:, :], q_in[:, par, 256:272], ACT.Exp, scale=-1.0).then_inc(nexp_done, 1)
                act.wait_ge(negmax_done, m + 1)
                act.activation(elog[:, :], q_in[:, par, 272:304], ACT.Exp, bias=negmax[:, :]).then_inc(elog_done, 1)

            def gate_tanh(m):
                act.wait_ge(gu_done, m + 1)
                act.activation(th[:, :], b_tg[:, 256:384], ACT.Tanh, scale=0.5).then_inc(tanh_done, 1)

            def put_oT(n, par):
                act.wait_ge(o_done, n + 1)
                act.copy(oT[:, par, :, :], b_o[:, 0:256].rearrange("p (k t) -> p k t", k=KC)).then_inc(oT_done, 1)

            act.wait_ge(ln_done, 1)
            norm(0, 0, True)
            norm(1, 1, True)
            put_xnT(0, 0)
            exps(0, 0)
            gate_tanh(0)

            def body(b, last):
                for c in range(BT):
                    n = b * BT + c
                    if not (last and c == BT - 1):
                        put_xnT(n + 1, (c + 1) % 2)
                    put_qkT(n, c % 2)
                    if not (last and c == BT - 1):
                        exps(n + 1, (c + 1) % 2)
                    if not (last and c >= BT - 2):
                        if c == BT - 2:
                            act.wait_ge(ln_done, b + 2)
                        act.wait_ge(xn_stored[c % 2], b * (16 * BT // 2) + 16 * (c // 2 + 1))
                        act.wait_ge(t1_done, n + 1)
                        act.activation(xn[:, c % 2, 0:D], x_all[:, n + 2, :], ACT.Identity,
                                       bias=ln["nmr"][:, bass.ds(n + 2, 1)],
                                       scale=ln["rstd"][:, bass.ds(n + 2, 1)]).then_inc(xn_done, 1)
                    if not (last and c == BT - 1):
                        gate_tanh(n + 1)
                    put_oT(n, c % 2)

            batches(act, body)

        @block.vector
        def _(dve):
            LN, KVQ, ROUTE = LN_MARKS, 0, 9
            setup = Chain(dve, dstep)
            dve.wait_ge(w_loaded, 16 * 7)
            dve.memset(vz[:, :, :, :], 0.0)
            dve.memset(q_in[:, :, 304:308], BIG)
            dve.memset(msum[:, 0, :], 0.0)
            dve.memset(onesb[:, :], 1.0)
            dve.memset(zrow[:, :], 0.0)
            dve.tensor_copy(strictb[:, :], cst[:, _C["strict"][0]:_C["strict"][1]]).then_inc(am_done, 2)
            setup.mark(dve.memset(ssum[:, :], 0.0))
            setup.wait()
            dve.memset(rsum[:, :], 0.0).then_inc(consts_ready, 1)
            dve.wait_ge(x_loaded, 16)
            layernorm_stats(dve, setup, x_all, ln, 0, BT).then_inc(ln_done, 1)
            fixed = setup.k
            PER_TILE = 8

            def project(m, par):
                dve.wait_ge(kvp_done, m + 1)
                dve.tensor_tensor(k_sb[:, par, :], b_kv[:, 0:D], bproj[:, PK:PK + D], ALU.add)
                dve.tensor_tensor(vz[:, par, :, :].rearrange("p a (x e) -> p a x e", e=HD)[:, :, 0::3, :],
                                  b_kv[:, D:2 * D].rearrange("p (a x e) -> p a x e", x=2, e=HD),
                                  bproj[:, PV:PV + D].rearrange("p (a x e) -> p a x e", x=2, e=HD),
                                  ALU.add).then_inc(kv_done, 1)
                dve.wait_ge(qp_done, m + 1)
                dve.tensor_tensor(q_in[:, par, 0:304], b_q[:, 0:304], bproj[:, PQ:PW], ALU.add).then_inc(qin_done, 1)

            def route(m, par, cm, step):
                logits = q_in[:, par, 272:308]
                step.mark(dve.max(top8[:, :], logits))
                step.wait()
                dve.tensor_scalar(negmax[:, :], top8[:, 4:5], -1.0, None, ALU.mult).then_inc(negmax_done, 1)
                step.mark(dve.match_replace(rep[:, :], top8[:, :], logits, -BIG))
                step.wait()
                step.mark(dve.tensor_scalar(maskb[:, par, :], rep[:, 0:NE], -1e38, None, ALU.is_lt))
                dve.tensor_scalar(far[:, :], rep[:, 0:NE], -1e38, 1024.0, ALU.is_ge, ALU.mult)
                step.wait()
                dve.tensor_tensor(msum[:, (cm + 1) % 8, :], msum[:, cm, :], maskb[:, par, :],
                                  ALU.add).then_inc(mask_done, 1)
                dve.wait_ge(nexp_done, m + 1)
                dve.tensor_tensor(qs[:, par, :].rearrange("p (h e) -> p h e", h=H),
                                  q_in[:, par, 0:D].rearrange("p (h e) -> p h e", h=H),
                                  bcast(nexp[:, :], 2, HD), ALU.mult).then_inc(qs_done, 1)
                dve.wait_ge(elog_done, m + 1)
                step.mark(dve.tensor_tensor(ewm[:, :], elog[:, :], maskb[:, par, :], ALU.mult))
                step.wait()
                step.mark(dve.tensor_reduce(ssum[:, :], ewm[:, :], AX_X, ALU.add))
                step.wait()
                step.mark(dve.reciprocal(rsum[:, :], ssum[:, :]))
                step.wait()
                dve.tensor_scalar(xn[:, par, D:XW], ewm[:, :], rsum[:, :], None, ALU.mult).then_inc(weights_done, 1)

            def shared_act(m, par, step):
                dve.wait_ge(tanh_done, m + 1)
                step.mark(dve.scalar_tensor_tensor(out=hg[:, :], in0=th[:, :], scalar=1.0, in1=b_tg[:, 256:384],
                                                   op0=ALU.add, op1=ALU.mult))
                step.wait()
                dve.scalar_tensor_tensor(out=hT[:, par, :], in0=hg[:, :], scalar=0.5, in1=b_tg[:, 384:512],
                                         op0=ALU.mult, op1=ALU.mult).then_inc(h_done, 1)

            def places(m):
                dve.wait_ge(pos_done, m + 1)
                dve.tensor_tensor(place[:, m, :], b_q[:, 304:336], far[:, :], ALU.add).then_inc(place_done, 1)

            def state(s, nxt):
                dve.wait_ge(s_done, s)
                dve.tensor_tensor(sbd[:, nxt, :, :], b_s[:, 0:256].rearrange("p (k t) -> p k t", k=KC),
                                  bcast(blockm, 1, KC), ALU.mult).then_inc(sbd_done, 1)

            def mask_scores(n, par, j):
                dve.wait_ge(a_done, 4 * n + j + 1)
                dve.tensor_tensor(at[:, par, 4 * j:4 * j + 4, :], b_a[j % 2][:, :].rearrange("p (h t) -> p h t", h=4),
                                  bcast(causal, 1, 4), ALU.mult).then_inc(am_done, 1)

            def residual(n):
                dve.wait_ge(xb_done, n + 1)
                dve.wait_ge(y_done, n + 1)
                dve.tensor_tensor(x_all[:, n, :], x_all[:, n, :], b_o[:, 256:512], ALU.add).then_inc(x1_done, 1)

            first = Chain(dve, dstep, fixed)
            project(0, 0)
            dve.wait_ge(qin_done, 1)
            route(0, 0, 0, first)
            shared_act(0, 0, first)
            places(0)
            fixed += first.k
            per_tile = first.k
            per_batch = per_tile * BT + LN_MARKS

            def body(b, last):
                step = Chain(dve, dstep, fixed + b * per_batch)
                for c in range(BT):
                    n = b * BT + c
                    more = not (last and c == BT - 1)
                    par = (c + 1) % 2
                    if c < BT - 1:
                        state(b * (BT - 1) + c + 1, (c + 1) % 2)
                    if more:
                        project(n + 1, par)
                        dve.wait_ge(qin_done, n + 2)
                    for j in range(4):
                        mask_scores(n, c % 2, j)
                    if more:
                        route(n + 1, par, (c + 1) % 8, step)
                        shared_act(n + 1, par, step)
                        places(n + 1)
                    if c == 4 and not last:
                        dve.wait_ge(x_loaded, b * 16 + 32)
                        layernorm_stats(dve, step, x_all, ln, (b + 1) * BT, BT).then_inc(ln_done, 1)
                    residual(n)
                if not last:
                    assert step.k == per_batch, (step.k, per_batch)

            batches(dve, body)

        @block.tensor
        def _(pe):
            def transpose_norm(m, par):
                pe.wait_ge(xn_done, m + 1)
                for k in range(KC):
                    last = pe.transpose(b_tg[:, k * P:(k + 1) * P], xn[:, par, k * P:(k + 1) * P], ident)
                last.then_inc(t1_done, 1)

            def project(m, par, first):
                pe.wait_ge(xnT_done, m + 1)
                if not first:
                    pe.wait_ge(kv_done, m)
                for k in range(KC):
                    last = pe.matmul(b_kv[:, :], xnT[:, par, k, :], wproj[:, k, 0:512], start=(k == 0),
                                     stop=(k == KC - 1))
                last.then_inc(kvp_done, 1)
                if not first:
                    pe.wait_ge(place_done, m)
                for k in range(KC):
                    last = pe.matmul(b_q[:, 0:304], xnT[:, par, k, :], wproj[:, k, 512:PW], start=(k == 0),
                                     stop=(k == KC - 1))
                last.then_inc(qp_done, 1)

            def shared_up(m, par):
                for gu in range(2):
                    for k in range(KC):
                        last = pe.matmul(b_tg[:, 256 + gu * P:256 + (gu + 1) * P], wsu[:, k, gu * P:(gu + 1) * P],
                                         xnT[:, par, k, :], start=(k == 0), stop=(k == KC - 1))
                last.then_inc(gu_done, 1)

            def positions(m, par, cm):
                pe.wait_ge(mask_done, m + 1)
                pe.matmul(b_q[:, 304:336], strictb[:, :], maskb[:, par, :], start=True, stop=False)
                pe.matmul(b_q[:, 304:336], onesb[:, :], msum[:, cm, :], start=False, stop=True).then_inc(pos_done, 1)

            def transpose_qk(n, par):
                pe.wait_ge(qs_done, n + 1)
                for k in range(KC):
                    pe.transpose(b_t2[:, k * P:(k + 1) * P], qs[:, par, k * P:(k + 1) * P], ident)
                for k in range(KC):
                    last = pe.transpose(b_t2[:, (2 + k) * P:(3 + k) * P], k_sb[:, par, k * P:(k + 1) * P], ident)
                last.then_inc(t2_done, 1)

            def v_pairs(par, hf):
                return vz[:, par, 4 * hf:4 * hf + 4, :].rearrange("p a (x e) -> p a x e", e=HD)[:, :, 0::3, :]

            def state(par, c):
                for k in range(KC):
                    last = pe.matmul(b_s[:, k * P:(k + 1) * P].rearrange("p (a x e) -> p a x e", x=2, e=HD),
                                     k_sb[:, par, k * P:(k + 1) * P], v_pairs(par, k),
                                     start=(c == 0 and k == 0), stop=(k == 1), skip_group_check=True)
                last.then_inc(s_done, 1)

            def head_scores(n, par):
                for j in range(4):
                    if j % 2 == 0:
                        pe.wait_ge(spread_done, 2 * n + j // 2 + 1)
                    pe.wait_ge(am_done, 4 * n + j + 1)
                    pe.matmul(b_a[j % 2][:, :], qkT[:, par, 2 + j // 2, :],
                              qbd[:, par, j // 2, 4 * (j % 2):4 * (j % 2) + 4, :], start=True,
                              stop=True).then_inc(a_done, 1)

            def attend(n, par, c):
                pe.wait_ge(am_done, 4 * n + 6)
                for hf in range(KC):
                    cols = slice(hf * P, (hf + 1) * P)
                    if c > 0:
                        pe.matmul(b_o[:, cols], sbd[:, par, hf, :], qkT[:, par, hf, :], start=True, stop=False,
                                  skip_group_check=True)
                    for eo in range(2):
                        for pr in range(4):
                            last = pe.matmul(b_o[32 * pr:32 * pr + 32, cols],
                                             vz[:, par, 4 * hf + pr, 32 * eo:32 * eo + 32],
                                             at[:, par, 8 * hf + 2 * pr + eo, :], start=(c == 0 and eo == 0),
                                             stop=(eo == 1), skip_group_check=True)
                last.then_inc(o_done, 1)

            def output(n, par):
                pe.wait_ge(oT_done, n + 1)
                for k in range(KC):
                    pe.matmul(b_o[:, 256:512], oT[:, par, k, :], wo[:, k, :], start=(k == 0), stop=False)
                pe.matmul(b_o[:, 256:512], hT[:, par, :], wsd[:, :], start=False, stop=True).then_inc(y_done, 1)

            pe.wait_ge(w_loaded, 16 * 7)
            pe.wait_ge(consts_ready, 1)
            transpose_norm(0, 0)
            project(0, 0, True)
            shared_up(0, 0)
            positions(0, 0, 0)

            def body(b, last):
                for c in range(BT):
                    n = b * BT + c
                    more = not (last and c == BT - 1)
                    par = (c + 1) % 2
                    pe.wait_ge(h_done, n + 1)
                    if more:
                        transpose_norm(n + 1, par)
                    transpose_qk(n, c % 2)
                    if c > 0:
                        pe.wait_ge(sbd_done, b * (BT - 1) + c)
                    if c < BT - 1:
                        state(c % 2, c)
                    if more:
                        project(n + 1, par, False)
                    head_scores(n, c % 2)
                    if more:
                        shared_up(n + 1, par)
                    attend(n, c % 2, c)
                    if more:
                        positions(n + 1, par, (c + 1) % 8)
                    output(n, c % 2)

            batches(pe, body)


def wait(eng, sem, value):
    if not isinstance(value, int) or value > 0:
        eng.wait_ge(sem, value)


def expert_slots(nc, g, dram):
    with ExitStack() as ctx:
        def sb(name, shape, dt=F32):
            return ctx.enter_context(nc.sbuf_tensor(name, shape, dt))

        def sem(name):
            return ctx.enter_context(nc.semaphore(name))

        cst, place, slot_rows = g["cst"], g["place"], g["slot_rows"]
        banks = g["banks"]
        place_i = sb("place_i", [P, NT, NE], I32)
        part_i = sb("part_i", [P, NT, NE], I32)
        lo = sb("lo", [P, NT, NE], BF16)
        hi = sb("hi", [P, NT, NE], BF16)
        iota_b = sb("iota_b", [P, 16], BF16)
        hot_hi = sb("hot_hi", [P, 2, NE, 16], BF16)
        hot_lo = sb("hot_lo", [P, 2, NE, 16], BF16)
        carry = sb("carry", [P, 2, 2, NE, 16], BF16)
        own = sb("own", [P, 4, 2, 8, 16])
        parts = sb("parts", [P, 4, 2, 16])
        table = sb("table", [P, 4, 16])
        slots_t = sb("slots_t", [2 * NE, P])
        empty = sb("empty", [P, 2 * NE])

        digits_done = sem("digits_done")
        hot_hi_done = sem("hot_hi_done")
        hot_lo_done = sem("hot_lo_done")
        carry_done = sem("carry_done")
        slots_done = sem("slots_done")
        own_done = sem("own_done")
        table_done = sem("table_done")
        table_moved = sem("table_moved")
        turned = sem("turned")
        rows_done = sem("rows_done")
        bstep = sem("bstep")
        block = ctx.enter_context(nc.Block())

        partc = cst[:, _C["part"][0]:_C["part"][1]]
        tile1 = _C["tile1"][0]
        ediag = cst[:, _C["ediag"][0]:_C["ediag"][1]]
        slots_v = dram["slots"].rearrange("(g q l) -> q g l", g=4, q=P)
        slots_back = dram["slots"].rearrange("(e s) -> e s", s=P)

        def tiles(eng, body):
            body(0, True)
            with eng.Fori(1, NT // 2) as i:
                body(i, False)

        @block.vector
        def _(dve):
            step = Chain(dve, bstep)
            step.mark(dve.tensor_scalar(place_i[:, :, :], place[:, :, :], float(CAP), None, ALU.min))
            dve.tensor_copy(iota_b[:, :], cst[:, _C["iota16"][0]:_C["iota16"][1]])
            step.wait()
            step.mark(dve.tensor_scalar(part_i[:, :, :], place_i[:, :, :], 4, None, ALU.arith_shift_right))
            step.wait()
            step.mark(dve.tensor_copy(hi[:, :, :], part_i[:, :, :]))
            step.mark(dve.tensor_scalar(place_i[:, :, :], place_i[:, :, :], 15, None, ALU.bitwise_and))
            step.wait()
            dve.tensor_copy(lo[:, :, :], place_i[:, :, :]).then_inc(digits_done, 1)
            dve.wait_ge(digits_done, 1)
            fixed = step.k

            def body(i, first):
                for par in range(2):
                    t = i * 2 + par
                    wait(dve, slots_done, t - 1)
                    dve.tensor_tensor(hot_lo[:, par, :, :], bcast(lo[:, t, :], 2, 16), bcast(iota_b[:, :], 1, NE),
                                      ALU.is_equal).then_inc(hot_lo_done, 1)
                    dve.tensor_tensor(hot_hi[:, par, :, :], bcast(hi[:, t, :], 2, 16), bcast(iota_b[:, :], 1, NE),
                                      ALU.is_equal).then_inc(hot_hi_done, 1)
                    dve.wait_ge(hot_lo_done, t + 1)
                    dve.tensor_scalar(carry[:, par, 0, :, :], hot_lo[:, par, :, :], partc, None, ALU.mult)
                    dve.tensor_scalar(carry[:, par, 1, :, :], hot_lo[:, par, :, :], cst[:, bass.ds(t + tile1, 1)],
                                      None, ALU.mult).then_inc(carry_done, 1)

            tiles(dve, body)
            step = Chain(dve, bstep, fixed)
            dve.wait_ge(slots_done, NT)
            for gr in range(4):
                last = dve.tensor_tensor(own[:, gr, :, :, :],
                                         banks[gr][:, 0:256].rearrange("p (x e l) -> p x e l", x=2, e=8),
                                         bcast(bcast(ediag, 2, 16), 1, 2), ALU.mult)
            step.mark(last)
            step.wait()
            for gr in range(4):
                last = dve.tensor_reduce(parts[:, gr, :, :], own[:, gr, :, :, :].rearrange("p x e l -> p x l e"), AX_X,
                                         ALU.add)
            step.mark(last)
            step.wait()
            step.mark(dve.scalar_tensor_tensor(out=table[:, :, :], in0=parts[:, :, 1, :], scalar=float(P),
                                               in1=parts[:, :, 0, :], op0=ALU.mult, op1=ALU.add))
            step.wait()
            dve.tensor_scalar(table[:, :, :], table[:, :, :], float(-P), None, ALU.add).then_inc(table_done, 1)
            dve.wait_ge(turned, 1)
            step.mark(dve.tensor_scalar(empty[:, :], banks[4][:, 0:2 * NE], 0.0,
                                        cst[:, _C["dump"][0]:_C["dump"][1]], ALU.is_lt, ALU.mult))
            step.wait()
            dve.tensor_tensor(slot_rows[:, :], banks[4][:, 0:2 * NE], empty[:, :], ALU.add).then_inc(rows_done, 1)
            dve.wait_ge(rows_done, 1)

        @block.tensor
        def _(pe):
            def body(i, first):
                for par in range(2):
                    t = i * 2 + par
                    pe.wait_ge(hot_hi_done, t + 1)
                    pe.wait_ge(carry_done, t + 1)
                    for gr in range(4):
                        last = pe.matmul(banks[gr][:, 0:256].rearrange("p (x e l) -> p x e l", x=2, e=8),
                                         hot_hi[:, par, 8 * gr:8 * gr + 8, :], carry[:, par, :, 8 * gr:8 * gr + 8, :],
                                         start=(first and par == 0), stop=False, skip_group_check=True)
                    last.then_inc(slots_done, 1)

            tiles(pe, body)
            pe.wait_ge(table_moved, 32)
            pe.transpose(banks[4][:, 0:2 * NE], slots_t[:, :],
                         cst[0:2 * NE, _C["ident"][0]:_C["ident"][0] + 2 * NE]).then_inc(turned, 1)

        @block.sync
        def _(sp):
            sp.wait_ge(table_done, 1)
            with nc.allow_non_contiguous_dma("slot table in 64-byte runs"):
                sp.dma_start(slots_v, table[:, :, :]).then_inc(table_moved, 16)
            sp.wait_ge(table_moved, 16)
            sp.dma_start(slots_t[:, :], slots_back).then_inc(table_moved, 16)


EU = 4


def routed_experts(nc, g, ins, dram):
    with ExitStack() as ctx:
        def sb(name, shape, dt=F32):
            return ctx.enter_context(nc.sbuf_tensor(name, shape, dt))

        def sem(name):
            return ctx.enter_context(nc.semaphore(name))

        cst, slot_rows = g["cst"], g["slot_rows"]
        wup = sb("wup", [P, EU, KC, D])
        wdn = sb("wdn", [P, EU, D])
        rows_now = sb("rows_now", [P, EU, 2], I32)
        xe = sb("xe", [P, EU, 2, XW])
        xeT = sb("xeT", [P, 2, KC, 2 * P])
        silu = sb("silu", [P, 2 * P])
        hT = sb("ehT", [P, 2, 2 * P])
        ye = sb("ye", [P, EU, 2, D])
        held = sb("held", [P, 2 * EU + 1])
        held_done = sem("held_done")
        b_x, b_u, b_y = g["banks"][0:2], g["banks"][2:4], g["banks"][4:6]

        w_loaded = [sem(f"expert_w{k}") for k in range(EU)]
        x_loaded = [sem(f"expert_x{k}") for k in range(EU)]
        index_done = sem("index_done")
        turned = sem("xe_turned")
        xeT_done = sem("xeT_done")
        up_done = sem("up_done")
        silu_done = sem("silu_done")
        h_done = sem("eh_done")
        down_done = sem("down_done")
        ye_done = sem("ye_done")
        added = sem("added")
        block = ctx.enter_context(nc.Block())
        ident = cst[:, _C["ident"][0]:_C["ident"][1]]
        wup_v = ins["wup"].rearrange("e (k p) n -> e p k n", p=P)

        def experts(eng, body):
            body(0, True, False)
            with eng.Fori(1, NE // EU - 1) as i:
                body(i, False, False)
            body(NE // EU - 1, False, True)

        @block.sync
        def _(sp):
            def body(i, first, last):
                for k in range(EU):
                    e = i * EU + k
                    wait(sp, down_done, e - EU + 1)
                    sp.dma_start(wup[:, k, :, :], wup_v[e]).then_inc(w_loaded[k], 16)
                    sp.dma_start(wdn[:, k, :], ins["wdn"][e]).then_inc(w_loaded[k], 16)

            experts(sp, body)

        @block.gpsimd
        def _(pool):
            def hold(j):
                pool.tensor_tensor(held[:, j + 1:j + 2], held[:, 0:1], held[:, 0:1], ALU.add)

            pool.memset(held[:, :], 0.0).then_inc(held_done, 1)
            pool.wait_ge(held_done, 1)

            def gather(e, k):
                wait(pool, ye_done, e - EU + 1)
                pool.tensor_copy(rows_now[:, k, :], slot_rows[:, bass.ds(e * 2, 2)]).then_inc(index_done, 1)
                pool.wait_ge(index_done, e + 1)
                hold(k)
                for hf in range(2):
                    pool.indirect_dma_start(out=xe[:, k, hf, :], out_offset=None, in_=dram["xrows"],
                                            in_offset=bass.IndirectOffsetOnAxis(ap=rows_now[:, k, hf:hf + 1], axis=0),
                                            bounds_check=ROWS - 1, oob_is_err=False).then_inc(x_loaded[k], 16)

            def add(e, k):
                pool.wait_ge(ye_done, e + 1)
                wait(pool, added, 32 * e)
                hold(EU + k)
                for hf in range(2):
                    pool.indirect_dma_start(out=dram["x1"], in_=ye[:, k, hf, :], in_offset=None,
                                            out_offset=bass.IndirectOffsetOnAxis(ap=rows_now[:, k, hf:hf + 1], axis=0),
                                            bounds_check=ROWS - 1, oob_is_err=True,
                                            compute_op=ALU.add).then_inc(added, 16)

            gather(0, 0)
            gather(1, 1)

            def body(i, first, last):
                for k in range(EU):
                    e = i * EU + k
                    if not (last and k >= EU - 2):
                        if not (first and k < 2):
                            wait(pool, added, 32 * (e - 1))
                        gather(e + 2, (k + 2) % EU)
                    add(e, k)

            experts(pool, body)
            pool.wait_ge(added, 32 * NE)

        @block.scalar
        def _(act):
            def body(i, first, last):
                for k in range(EU):
                    e = i * EU + k
                    par = k % 2
                    act.wait_ge(turned, e + 1)
                    wait(act, up_done, e - 1)
                    act.copy(xeT[:, par, :, :], b_x[par][:, :].rearrange("p (k t) -> p k t", k=KC))\
                       .then_inc(xeT_done, 1)
                    act.wait_ge(up_done, e + 1)
                    wait(act, h_done, e)
                    act.activation(silu[:, :], b_u[par][:, 0:256], ACT.Silu).then_inc(silu_done, 1)

            experts(act, body)

        @block.vector
        def _(dve):
            def body(i, first, last):
                for k in range(EU):
                    e = i * EU + k
                    par = k % 2
                    dve.wait_ge(silu_done, e + 1)
                    wait(dve, down_done, e - 1)
                    dve.tensor_tensor(hT[:, par, :], silu[:, :], b_u[par][:, 256:512], ALU.mult).then_inc(h_done, 1)
                    dve.wait_ge(down_done, e + 1)
                    wait(dve, added, 32 * (e - EU + 1))
                    for hf in range(2):
                        last_op = dve.tensor_scalar(ye[:, k, hf, :], b_y[par][:, hf * D:(hf + 1) * D],
                                                    xe[:, k, hf, bass.ds(e + D, 1)], None, ALU.mult)
                    last_op.then_inc(ye_done, 1)

            experts(dve, body)

        @block.tensor
        def _(pe):
            def body(i, first, last):
                def turn(j, k):
                    e = (i + j) * EU + k
                    par = k % 2
                    pe.wait_ge(x_loaded[k], (i + j) * 32 + 32)
                    wait(pe, xeT_done, e - 1)
                    for kc in range(KC):
                        for hf in range(2):
                            op = pe.transpose(b_x[par][:, (2 * kc + hf) * P:(2 * kc + hf + 1) * P],
                                              xe[:, k, hf, kc * P:(kc + 1) * P], ident)
                    op.then_inc(turned, 1)

                def up(e, k):
                    par = k % 2
                    pe.wait_ge(xeT_done, e + 1)
                    pe.wait_ge(w_loaded[k], i * 32 + 32)
                    wait(pe, h_done, e - 1)
                    for gu in range(2):
                        for kc in range(KC):
                            op = pe.matmul(b_u[par][:, gu * 256:gu * 256 + 256], wup[:, k, kc, gu * P:(gu + 1) * P],
                                           xeT[:, par, kc, :], start=(kc == 0), stop=(kc == KC - 1))
                    op.then_inc(up_done, 1)

                def down(e, k):
                    par = k % 2
                    pe.wait_ge(h_done, e + 1)
                    wait(pe, ye_done, e - 1)
                    for hf in range(2):
                        op = pe.matmul(b_y[par][:, hf * D:(hf + 1) * D], hT[:, par, hf * P:(hf + 1) * P], wdn[:, k, :],
                                       start=True, stop=True)
                    op.then_inc(down_done, 1)

                if first:
                    turn(0, 0)
                for k in range(EU):
                    e = i * EU + k
                    if k < EU - 1:
                        turn(0, k + 1)
                    elif not last:
                        turn(1, 0)
                    up(e, k)
                    down(e, k)

            experts(pe, body)


ST = 4
NS = NT // ST
HID = 768
MC = HID // P
INT_SCALE = 1.0 / 127.0
TOPK = 64
NPAIR = BATCH * H // 2


def layer1_project(nc, g, ins, dram):
    with ExitStack() as ctx:
        def sb(name, shape, dt=F32):
            return ctx.enter_context(nc.sbuf_tensor(name, shape, dt))

        def sem(name):
            return ctx.enter_context(nc.semaphore(name))

        cst, x_all, xnT, ln = g["cst"], g["x_all"], g["xnT_all"], g["ln"]
        wkv = sb("wkv", [P, KC, 2 * D])
        wsc = sb("wsc", [P, HD])
        wprod = sb("wprod", [P, KC, D])
        widx = sb("widx", [P, KC, H])
        xn = sb("xn1", [P, 2, D])
        xst = sb("xst", [P, 2, KC, 512])
        kv_row = sb("kv_row", [P, 2, 2 * D])
        score = sb("score", [H, 2, 512])
        b_t, b_kv, b_i = g["banks"][0:2], g["banks"][2:4], g["banks"][4:6]

        w_loaded = sem("w1_loaded")
        x_loaded = sem("x1_loaded")
        ln_done = sem("ln1_done")
        widx_done = sem("widx_done")
        xn_done = sem("xn1_done")
        turned = sem("xn1_turned")
        kept = sem("xnT_kept")
        xnT_done = sem("xnT1_done")
        kvp_done = sem("kvp1_done")
        kv_done = sem("kv1_done")
        kv_stored = [sem("kv_stored0"), sem("kv_stored1")]
        idx_done = sem("idx_done")
        score_done = sem("score_done")
        score_stored = [sem("score_stored0"), sem("score_stored1")]
        dstep = sem("d1step")
        block = ctx.enter_context(nc.Block())
        ident = cst[:, _C["ident"][0]:_C["ident"][1]]
        x1_v = dram["x1"][0:TOKENS, :].rearrange("(b c p) d -> b p c d", p=P, c=BT)
        kv_v = dram["kvrows"].rearrange("(t p h) e -> t p (h e)", p=P, h=H)
        score_v = dram["scores"].rearrange("(b h) (s t) -> b s h t", h=H, t=512)

        def batches(eng, body):
            body(0, True)
            with eng.Fori(1, BATCH) as b:
                body(b, False)

        @block.sync
        def _(sp):
            sp.dma_start(x_all[:, 0:BT, :], x1_v[0]).then_inc(x_loaded, 16)
            sp.dma_start(wkv[:, :, :], ins["wkv1"].rearrange("(k p) n -> p k n", p=P)).then_inc(w_loaded, 16)
            sp.dma_start(wsc[:, :], ins["wsc"]).then_inc(w_loaded, 16)
            for b in range(1, BATCH):
                sp.wait_ge(x_loaded, 16 * b)
                sp.dma_start(x_all[:, b * BT:(b + 1) * BT, :], x1_v[b]).then_inc(x_loaded, 16)

            def body(b, first):
                for c in range(BT):
                    n = b * BT + c
                    sp.wait_ge(kv_done, n + 1)
                    sp.dma_start(kv_v[n], kv_row[:, c % 2, :]).then_inc(kv_stored[c % 2], 16)
                    if c % ST == ST - 1:
                        sp.wait_ge(score_done, 2 * b + c // ST + 1)
                        sp.dma_start(score_v[b, c // ST], score[:, c // ST, :]).then_inc(score_stored[c // ST], 16)

            batches(sp, body)
            for par in range(2):
                sp.wait_ge(kv_stored[par], 16 * NT // 2)
                sp.wait_ge(score_stored[par], 16 * BATCH)

        @block.scalar
        def _(act):
            def body(b, first):
                act.wait_ge(ln_done, b + 1)
                for c in range(BT):
                    n = b * BT + c
                    wait(act, turned, n - 1)
                    act.activation(xn[:, c % 2, :], x_all[:, n, :], ACT.Identity, bias=ln["nmr"][:, bass.ds(n, 1)],
                                   scale=ln["rstd"][:, bass.ds(n, 1)]).then_inc(xn_done, 1)
                    if c > 0:
                        put(b, c - 1)
                    if c == ST:
                        put_score(b, 0)
                put(b, BT - 1)
                put_score(b, 1)

            def put(b, c):
                act.wait_ge(turned, b * BT + c + 1)
                if c % ST == 0:
                    wait(act, kept, b * 2 + c // ST - 1)
                act.copy(xst[:, c // ST, :, (c % ST) * P:(c % ST + 1) * P],
                         b_t[c % 2][:, 0:256].rearrange("p (k t) -> p k t", k=KC)).then_inc(xnT_done, 1)

            def put_score(b, s):
                act.wait_ge(idx_done, 2 * b + s + 1)
                wait(act, score_stored[s], 16 * b)
                act.copy(score[:, s, :], b_i[s][0:H, :]).then_inc(score_done, 1)

            batches(act, body)

        @block.gpsimd
        def _(pool):
            def body(b, first):
                for s in range(2):
                    pool.wait_ge(xnT_done, b * BT + (s + 1) * ST)
                    pool.tensor_copy(xnT[:, :, bass.ds((2 * b + s) * 512, 512)], xst[:, s, :, :]).then_inc(kept, 1)

            batches(pool, body)

        @block.vector
        def _(dve):
            step = Chain(dve, dstep)
            dve.wait_ge(x_loaded, 16)
            layernorm_stats(dve, step, x_all, ln, 0, BT).then_inc(ln_done, 1)
            dve.wait_ge(w_loaded, 32)
            step.mark(dve.tensor_tensor(wprod[:, :, :].rearrange("p k (h e) -> p k h e", e=HD),
                                        wkv[:, :, 0:D].rearrange("p k (h e) -> p k h e", e=HD),
                                        bcast(bcast(wsc[:, :], 1, H), 1, KC), ALU.mult))
            step.wait()
            dve.tensor_reduce(widx[:, :, :], wprod[:, :, :].rearrange("p k (h e) -> p k h e", e=HD), AX_X,
                              ALU.add).then_inc(widx_done, 1)
            fixed = step.k

            def body(b, first):
                for c in range(BT):
                    n = b * BT + c
                    dve.wait_ge(kvp_done, n + 1)
                    if not (first and c < 2):
                        dve.wait_ge(kv_stored[c % 2], b * (16 * BT // 2) + 16 * (c // 2))
                    dve.tensor_copy(kv_row[:, c % 2, :].rearrange("p (h x e) -> p x h e", h=H, x=2),
                                    b_kv[c % 2][:, :].rearrange("p (x h e) -> p x h e", h=H, x=2)).then_inc(kv_done, 1)
                    if c == BT // 2 and more[0]:
                        step = Chain(dve, dstep, fixed + b * LN_MARKS)
                        dve.wait_ge(x_loaded, b * 16 + 32)
                        layernorm_stats(dve, step, x_all, ln, (b + 1) * BT, BT).then_inc(ln_done, 1)

            more = [True]
            body(0, True)
            with dve.Fori(1, BATCH - 1) as b:
                body(b, False)
            more[0] = False
            body(BATCH - 1, False)

        @block.tensor
        def _(pe):
            pe.wait_ge(widx_done, 1)

            def turn(n, c):
                pe.wait_ge(xn_done, n + 1)
                wait(pe, xnT_done, n - 1)
                for k in range(KC):
                    op = pe.transpose(b_t[c % 2][:, k * P:(k + 1) * P], xn[:, c % 2, k * P:(k + 1) * P], ident)
                op.then_inc(turned, 1)

            def project(n, c):
                pe.wait_ge(xnT_done, n + 1)
                wait(pe, kv_done, n - 1)
                for k in range(KC):
                    op = pe.matmul(b_kv[c % 2][:, :], xst[:, c // ST, k, (c % ST) * P:(c % ST + 1) * P], wkv[:, k, :],
                                   start=(k == 0), stop=(k == KC - 1))
                op.then_inc(kvp_done, 1)

            def key_scores(b, s):
                wait(pe, score_done, 2 * b + s - 1)
                for k in range(KC):
                    op = pe.matmul(b_i[s][0:H, :], widx[:, k, :], xst[:, s, k, :], start=(k == 0), stop=(k == KC - 1))
                op.then_inc(idx_done, 1)

            def body(b, first):
                for c in range(BT):
                    turn(b * BT + c, c)
                    if c > 0:
                        project(b * BT + c - 1, c - 1)
                    if c == ST:
                        key_scores(b, 0)
                project(b * BT + BT - 1, BT - 1)
                key_scores(b, 1)

            batches(pe, body)


def layer1_ffn_and_keys(nc, g, ins, dram):
    with ExitStack() as ctx:
        def sb(name, shape, dt=F32):
            return ctx.enter_context(nc.sbuf_tensor(name, shape, dt))

        def sem(name):
            return ctx.enter_context(nc.semaphore(name))

        cst, x_all, xnT, keys = g["cst"], g["x_all"], g["xnT_all"], g["keys"]
        scores = sb("scores_sb", [P, 2, SEQ])
        best = sb("best", [P, 2, 8])
        picked = sb("picked", [P, TOPK], mybir.dt.uint32)
        pickedf = sb("pickedf", [P, TOPK])
        key_row = sb("key_row", [P, P])
        key_rows = sb("key_rows", [P, NPAIR], I32)
        wg = sb("wg", [P, KC, HID])
        wu = sb("wu", [P, KC, HID])
        wd = sb("wd", [P, MC, D])
        silu = sb("fsilu", [P, 2, 512])
        hT = sb("fhT", [P, 2, MC, 512])
        b_g, b_u, b_y = g["banks"][0:2], g["banks"][2:4], g["banks"][4:6]
        b_x = g["banks"][6]

        w_loaded = [sem(f"ffn_w{k}") for k in range(3)]
        weights_done = sem("ffn_weights")
        scores_loaded = sem("scores_loaded")
        key_row_done = sem("key_row_done")
        key_turned = sem("key_turned")
        key_rows_done = sem("key_rows_done")
        keys_loaded = sem("keys_loaded")
        gate_done = sem("gate_done")
        silu_done = sem("fsilu_done")
        h_done = sem("fh_done")
        y_done = sem("fy_done")
        x_done = sem("fx_done")
        estep = sem("estep")
        block = ctx.enter_context(nc.Block())
        ident = cst[:, _C["ident"][0]:_C["ident"][1]]

        def supertiles(eng, body):
            body(0, True)
            with eng.Fori(1, NS // 2) as i:
                body(i, False)

        @block.sync
        def _(sp):
            sp.dma_start(scores[:, 0, :], dram["scores"]).then_inc(scores_loaded, 16)
            for k, (dst, src) in enumerate(((wg, "wg1"), (wu, "wu1"), (wd, "wd1"))):
                sp.dma_start(dst[:, :, :].bitcast(I32), ins[src].rearrange("(k p) n -> p k n", p=P))\
                  .then_inc(w_loaded[k], 16)

        @block.gpsimd
        def _(pool):
            pool.wait_ge(key_rows_done, 2)
            for p in range(NPAIR):
                pool.indirect_dma_start(out=keys[:, p, :], out_offset=None, in_=dram["kvrows"],
                                        in_offset=bass.IndirectOffsetOnAxis(ap=key_rows[:, p:p + 1], axis=0),
                                        bounds_check=TOKENS * H - 1, oob_is_err=False).then_inc(keys_loaded, 16)
            pool.wait_ge(keys_loaded, 16 * NPAIR)

        @block.scalar
        def _(act):
            for k, w in enumerate((wg, wu, wd)):
                act.wait_ge(w_loaded[k], 16)
                act.activation(w[:, :, :], w[:, :, :].bitcast(I32), ACT.Copy, scale=INT_SCALE)\
                   .then_inc(weights_done, 1)

            def body(i, first):
                for s in range(2):
                    for m in range(MC):
                        j = (2 * i + s) * MC + m
                        act.wait_ge(gate_done, j + 1)
                        wait(act, h_done, j - 1)
                        act.activation(silu[:, m % 2, :], b_g[m % 2][:, :], ACT.Silu).then_inc(silu_done, 1)

            supertiles(act, body)

        @block.vector
        def _(dve):
            step = Chain(dve, estep)
            dve.wait_ge(scores_loaded, 16)
            for r in range(TOPK // 8):
                src, dst = scores[:, r % 2, :], scores[:, (r + 1) % 2, :]
                step.mark(dve.max(best[:, r % 2, :], src))
                step.wait()
                dve.max_index(picked[:, 8 * r:8 * r + 8], best[:, r % 2, :], src)
                step.mark(dve.match_replace(dst, best[:, r % 2, :], src, -BIG))
                step.wait()
            step.mark(dve.tensor_copy(pickedf[:, :], picked[:, :]))
            step.wait()
            for k in range(2):
                op = dve.tensor_scalar(key_row[:, k * TOPK:(k + 1) * TOPK], pickedf[:, :], float(H),
                                       cst[:, _C["keybase"][0]:_C["keybase"][1]], ALU.mult, ALU.add)
            op.then_inc(key_row_done, 1)
            dve.wait_ge(key_turned, 1)
            pairs = b_x[:, 0:P].rearrange("p (n two) -> p n two", two=2)
            dve.tensor_copy(key_rows[0:TOPK, :], pairs[0:TOPK, :, 0]).then_inc(key_rows_done, 1)
            dve.tensor_copy(key_rows[TOPK:P, :], pairs[TOPK:P, :, 1]).then_inc(key_rows_done, 1)

            def body(i, first):
                for s in range(2):
                    for m in range(MC):
                        j = (2 * i + s) * MC + m
                        dve.wait_ge(silu_done, j + 1)
                        wait(dve, y_done, ((2 * i + s) - 1) * 2)
                        dve.tensor_tensor(hT[:, s, m, :], silu[:, m % 2, :], b_u[m % 2][:, :], ALU.mult)\
                           .then_inc(h_done, 1)
                        if m in (2, 4) and not (first and s == 0):
                            add(i, s, m // 2 - 1)

            def add(i, s, hf):
                t = 2 * i + s - 1
                dve.wait_ge(y_done, 2 * t + hf + 1)
                rows = x_all[:, bass.ds(t * ST + 2 * hf, 2), :]
                dve.tensor_tensor(rows, rows, b_y[hf][:, :].rearrange("p (c n) -> p c n", c=2), ALU.add)\
                   .then_inc(x_done, 1)

            supertiles(dve, body)
            for hf in range(2):
                add(NS // 2, 0, hf)

        @block.tensor
        def _(pe):
            for k in range(3):
                pe.wait_ge(weights_done, k + 1)

            def up(i, s, m):
                t = 2 * i + s
                j = t * MC + m
                wait(pe, h_done, j - 1)
                for bank, w in ((b_g, wg), (b_u, wu)):
                    for k in range(KC):
                        op = pe.matmul(bank[m % 2][:, :], w[:, k, m * P:(m + 1) * P], xnT[:, k, bass.ds(t * 512, 512)],
                                       start=(k == 0), stop=(k == KC - 1))
                op.then_inc(gate_done, 1)

            def down(t, par, hf):
                pe.wait_ge(h_done, (t + 1) * MC)
                wait(pe, x_done, 2 * (t - 1) + hf + 1)
                for c in range(2):
                    q = 2 * hf + c
                    for m in range(MC):
                        op = pe.matmul(b_y[hf][:, c * D:(c + 1) * D], hT[:, par, m, q * P:(q + 1) * P], wd[:, m, :],
                                       start=(m == 0), stop=(m == MC - 1))
                op.then_inc(y_done, 1)

            def body(i, first):
                for s in range(2):
                    for m in range(MC):
                        up(i, s, m)
                        if first and s == 0 and m == 1:
                            pe.wait_ge(key_row_done, 1)
                            pe.transpose(b_x[:, 0:P], key_row[:, :], ident).then_inc(key_turned, 1)
                        if m in (1, 3) and not (first and s == 0):
                            down(2 * i + s - 1, (s + 1) % 2, m // 2)

            supertiles(pe, body)
            for hf in range(2):
                down(NS - 1, 1, hf)


def layer1_attention(nc, g, ins, out):
    with ExitStack() as ctx:
        def sb(name, shape, dt=F32):
            return ctx.enter_context(nc.sbuf_tensor(name, shape, dt))

        def sem(name):
            return ctx.enter_context(nc.semaphore(name))

        cst, x_all, xnT, keys = g["cst"], g["x_all"], g["xnT_all"], g["keys"]
        wq = sb("wq1_sb", [P, KC, D])
        wo = sb("wo1_sb", [P, KC, D])
        kz = sb("kz", [P, KC, 4, 32])
        kT = sb("kT1", [P, KC, P])
        kbd = sb("kbd", [P, 2, KC, 4, P])
        vb = sb("vb", [P, 2, 8, 34])
        qT = sb("qT1", [P, 2, KC, 512])
        smax = sb("smax", [P, 2, H])
        s_sb = sb("s_sb", [P, 2, H, TOPK])
        p_sb = sb("p_sb", [P, 2, H, TOPK])
        pT = sb("pT", [P, 2, 8, P])
        rden = sb("rden", [P, 2, H])
        att = sb("att", [P, 2, D])
        attT = sb("attT", [P, 2, KC, P])
        b_s, b_p, b_q, b_o, b_w = g["banks"][0:2], g["banks"][2:4], g["banks"][4], g["banks"][5], g["banks"][6]
        b_k = g["banks"][7]

        w_loaded = sem("w2_loaded")
        zero_done = sem("zero_done")
        kz_done = sem("kz_done")
        k_turned = sem("k_turned")
        kT_done = sem("kT_done")
        kbd_done = sem("kbd_done")
        vb_done = sem("vb_done")
        qp_done = sem("q1p_done")
        qT_done = sem("q1T_done")
        s_done = sem("s1_done")
        sub_done = sem("sub_done")
        exp_done = sem("exp_done")
        p_turned = sem("p_turned")
        pT_done = sem("pT_done")
        av_done = sem("av_done")
        att_done = sem("att_done")
        att_turned = sem("att_turned")
        attT_done = sem("attT_done")
        wo_done = sem("wo_done")
        out_done = sem("out_done")
        stored = sem("stored")
        rec_done = sem("rec_done")
        fstep = sem("fstep")
        block = ctx.enter_context(nc.Block())
        ident = cst[:, _C["ident"][0]:_C["ident"][1]]
        low = cst[:, _C["lowkeys"][0]:_C["lowkeys"][1]]
        high = cst[:, _C["highkeys"][0]:_C["highkeys"][1]]
        out_v = out.rearrange("b (c p) d -> (b c) p d", p=P)

        def pairs_of_batches(eng, body):
            body(0, True, False)
            with eng.Fori(1, BATCH // 2 - 1) as i:
                body(i, False, False)
            body(BATCH // 2 - 1, False, True)


        @block.sync
        def _(sp):
            for dst, src in ((wq, "wq1"), (wo, "wo1")):
                sp.dma_start(dst[:, :, :], ins[src].rearrange("(k p) n -> p k n", p=P)).then_inc(w_loaded, 16)

            def body(i, first, last):
                for c in range(2 * BT):
                    n = i * (2 * BT) + c
                    sp.wait_ge(out_done, n + 1)
                    sp.dma_start(out_v[n], x_all[:, n, :]).then_inc(stored, 16)

            pairs_of_batches(sp, body)
            sp.wait_ge(stored, 16 * NT)

        @block.gpsimd
        def _(pool):
            pool.memset(kbd[:, :, :, :, :], 0.0)
            pool.memset(vb[:, :, :, :], 0.0).then_inc(zero_done, 1)
            pool.wait_ge(zero_done, 1)
            for par in range(2):
                pool.tensor_scalar(vb[:, par, :, 16], vb[:, par, :, 16], low, None, ALU.add)
                pool.tensor_scalar(vb[:, par, :, 33], vb[:, par, :, 33], high, None, ALU.add)

            def body(i, first, last):
                for par in range(2):
                    b = 2 * i + par
                    kv = keys[:, bass.ds(b * 8, 8), :]
                    wait(pool, k_turned, b)
                    k_in = kv[:, :, 0:16].rearrange("p (k a) e -> p k a e", k=KC)
                    pool.tensor_tensor(kz[:, :, :, 0:16], k_in, low.unsqueeze(2).unsqueeze(3).broadcast_to(k_in.shape),
                                       ALU.mult)
                    pool.tensor_tensor(kz[:, :, :, 16:32], k_in,
                                       high.unsqueeze(2).unsqueeze(3).broadcast_to(k_in.shape),
                                       ALU.mult).then_inc(kz_done, 1)
                    wait(pool, av_done, (b - 1) * BT)
                    v_in = kv[:, :, 16:32]
                    pool.tensor_tensor(vb[:, par, :, 0:16], v_in, low.unsqueeze(2).broadcast_to(v_in.shape), ALU.mult)
                    pool.tensor_tensor(vb[:, par, :, 17:33], v_in, high.unsqueeze(2).broadcast_to(v_in.shape), ALU.mult)\
                        .then_inc(vb_done, 1)

            pairs_of_batches(pool, body)

        @block.scalar
        def _(act):
            def put_kT(b):
                act.wait_ge(k_turned, b + 1)
                wait(act, kbd_done, b)
                act.copy(kT[:, :, :], b_k[:, 0:256].rearrange("p (k t) -> p k t", k=KC)).then_inc(kT_done, 1)

            def put_q(q, par):
                for k in range(KC):
                    act.wait_ge(qp_done, 2 * q + k + 1)
                    act.activation(qT[:, par, k, :], b_q[:, :], ACT.Copy, scale=HD ** -0.5).then_inc(qT_done, 1)

            def exps(n, par):
                act.wait_ge(sub_done, 2 * n + 2)
                wait(act, p_turned, 2 * (n - 1))
                act.activation(p_sb[:, par, :, :], s_sb[:, par, :, :], ACT.Exp).then_inc(exp_done, 1)

            def put_pT(n, par):
                for hf in range(2):
                    act.wait_ge(p_turned, 2 * n + hf + 1)
                    wait(act, av_done, n - 1)
                    act.copy(pT[:, par, 4 * hf:4 * hf + 4, :], b_p[hf][:, :].rearrange("p (a t) -> p a t", a=4))\
                       .then_inc(pT_done, 1)

            def put_attT(n, par):
                act.wait_ge(att_turned, n + 1)
                act.copy(attT[:, par, :, :], b_w[:, 256:512].rearrange("p (k t) -> p k t", k=KC))\
                   .then_inc(attT_done, 1)

            put_kT(0)
            put_q(0, 0)

            def body(i, first, last):
                for c in range(2 * BT):
                    n = i * (2 * BT) + c
                    if c % ST == 0 and not (last and c == 2 * BT - ST):
                        if c % BT == ST:
                            put_kT(2 * i + c // BT + 1)
                        put_q(4 * i + c // ST + 1, (c // ST + 1) % 2)
                    exps(n, c % 2)
                    put_pT(n, c % 2)
                    if not (first and c == 0):
                        put_attT(n - 1, (c + 1) % 2)

            pairs_of_batches(act, body)
            put_attT(NT - 1, 1)

        @block.vector
        def _(dve):
            dve.wait_ge(zero_done, 1)

            def spread_keys(b, par):
                dve.wait_ge(kT_done, b + 1)
                wait(dve, s_done, 2 * BT * (b - 1))
                for pr in range(4):
                    r = slice(32 * pr, 32 * pr + 32)
                    op = dve.tensor_copy(kbd[r, par, :, pr, :], kT[r, :, :])
                op.then_inc(kbd_done, 1)

            def subtract_max(n, par, k):
                heads = slice(8 * k, 8 * k + 8)
                sc = b_s[k][:, :].rearrange("p (h j) -> p h j", j=TOPK)
                step = Chain(dve, fstep, 2 * n + k)
                dve.wait_ge(s_done, 2 * n + k + 1)
                step.mark(dve.tensor_reduce(smax[:, par, heads], sc, AX_X, ALU.max))
                step.wait()
                wait(dve, exp_done, n - 1)
                dve.tensor_tensor(s_sb[:, par, heads, :], sc, bcast(smax[:, par, heads], 2, TOPK),
                                  ALU.subtract).then_inc(sub_done, 1)

            def normalise(n, par):
                dve.wait_ge(av_done, n + 1)
                o = b_o[:, 0:272].rearrange("p (a x e) -> p a x e", a=8, x=2)
                dve.reciprocal(rden[:, par, :].rearrange("p (a x) -> p a x", x=2), o[:, :, :, 16]).then_inc(rec_done, 1)
                dve.wait_ge(rec_done, n + 1)
                dve.tensor_tensor(att[:, par, :].rearrange("p (a x e) -> p a x e", a=8, x=2), o[:, :, :, 0:16],
                                  bcast(rden[:, par, :].rearrange("p (a x) -> p a x", x=2), 3, 16),
                                  ALU.mult).then_inc(att_done, 1)

            def residual(n):
                dve.wait_ge(wo_done, n + 1)
                dve.tensor_tensor(x_all[:, n, :], x_all[:, n, :], b_w[:, 0:256], ALU.add).then_inc(out_done, 1)

            spread_keys(0, 0)
            for k in range(2):
                subtract_max(0, 0, k)

            def body(i, first, last):
                for c in range(2 * BT):
                    n = i * (2 * BT) + c
                    if c % BT == ST and not (last and c == BT + ST):
                        spread_keys(2 * i + c // BT + 1, (c // BT + 1) % 2)
                    if not (last and c == 2 * BT - 1):
                        for k in range(2):
                            subtract_max(n + 1, (c + 1) % 2, k)
                    if not (first and c == 0):
                        residual(n - 1)
                    normalise(n, c % 2)

            pairs_of_batches(dve, body)
            residual(NT - 1)

        @block.tensor
        def _(pe):
            def turn_keys(b):
                pe.wait_ge(kz_done, b + 1)
                wait(pe, kT_done, b)
                for k in range(KC):
                    op = pe.transpose(b_k[:, k * P:(k + 1) * P], kz[:, k, :, :], ident)
                op.then_inc(k_turned, 1)

            def project_q(q):
                for k in range(KC):
                    wait(pe, qT_done, 2 * q + k)
                    for kc in range(KC):
                        op = pe.matmul(b_q[:, :], wq[:, kc, k * P:(k + 1) * P], xnT[:, kc, bass.ds(q * 512, 512)],
                                       start=(kc == 0), stop=(kc == KC - 1))
                    op.then_inc(qp_done, 1)

            def scores(n, c, bpar, q):
                if c % ST == 0:
                    pe.wait_ge(qT_done, 2 * q + 2)
                for k in range(KC):
                    wait(pe, sub_done, 2 * (n - 1) + k + 1)
                    pe.matmul(b_s[k][:, :], qT[:, c // ST % 2, k, (c % ST) * P:(c % ST + 1) * P],
                              kbd[:, bpar, k, :, :], start=True, stop=True).then_inc(s_done, 1)

            def turn_p(n, par):
                pe.wait_ge(exp_done, n + 1)
                for hf in range(2):
                    wait(pe, pT_done, 2 * (n - 1) + hf + 1)
                    for a in range(4):
                        h = 8 * hf + 2 * a
                        op = pe.transpose(b_p[hf][:, a * P:(a + 1) * P], p_sb[:, par, h:h + 2, :], ident)
                    op.then_inc(p_turned, 1)

            def attend(n, par, bpar):
                for hf in range(2):
                    pe.wait_ge(pT_done, 2 * n + hf + 1)
                    for a in range(4 * hf, 4 * hf + 4):
                        op = pe.matmul(b_o[:, 34 * a:34 * a + 34], pT[:, par, a, :], vb[:, bpar, a, :], start=True,
                                       stop=True)
                op.then_inc(av_done, 1)

            def turn_att(n, par):
                pe.wait_ge(att_done, n + 1)
                for k in range(KC):
                    op = pe.transpose(b_w[:, 256 + k * P:256 + (k + 1) * P], att[:, par, k * P:(k + 1) * P], ident)
                op.then_inc(att_turned, 1)

            def output(n, par):
                pe.wait_ge(attT_done, n + 1)
                wait(pe, out_done, n)
                for k in range(KC):
                    op = pe.matmul(b_w[:, 0:256], attT[:, par, k, :], wo[:, k, :], start=(k == 0), stop=(k == KC - 1))
                op.then_inc(wo_done, 1)

            pe.wait_ge(w_loaded, 32)
            turn_keys(0)
            project_q(0)
            pe.wait_ge(kbd_done, 1)
            scores(0, 0, 0, 0)

            def body(i, first, last):
                for c in range(2 * BT):
                    n = i * (2 * BT) + c
                    if c % ST == 0 and not (last and c == 2 * BT - ST):
                        if c % BT == ST:
                            turn_keys(2 * i + c // BT + 1)
                        project_q(4 * i + c // ST + 1)
                    if not (last and c == 2 * BT - 1):
                        d = (c + 1) % (2 * BT)
                        if d % BT == 0:
                            pe.wait_ge(kbd_done, 2 * i + (c + 1) // BT + 1)
                        scores(n + 1, d, d // BT, 4 * i + (c + 1) // ST)
                    turn_p(n, c % 2)
                    if not (first and c == 0):
                        output(n - 1, (c + 1) % 2)
                    if c % BT == 0:
                        pe.wait_ge(vb_done, 2 * i + c // BT + 1)
                    attend(n, c % 2, c // BT)
                    turn_att(n, c % 2)

            pairs_of_batches(pe, body)
            output(NT - 1, 1)


def layers(nc, ins, out):
    with ExitStack() as ctx:
        def sb(name, shape, dt=F32):
            return ctx.enter_context(nc.sbuf_tensor(name, shape, dt))

        g = {"cst": sb("csts", [P, CW]), "x_all": sb("x_all", [P, NT, D]), "slot_rows": sb("slot_rows", [P, 2 * NE], I32),
             "ln": {"ve": sb("ln_ve", [P, BT]), "r": sb("ln_r", [P, BT]), "t": sb("ln_t", [P, BT]),
                    "st": sb("ln_st", [P, BT, 6]), "mv": sb("ln_mv", [P, BT, 2]), "rstd": sb("ln_rstd", [P, NT]),
                    "nmr": sb("ln_nmr", [P, NT])},
             "banks": [ctx.enter_context(nc.psum_tensor(f"bank{i}", [P, 512], F32)) for i in range(8)]}
        dram = {"xrows": nc.dram_tensor("xrows", (ROWS, XW), F32).ap(),
                "x1": nc.dram_tensor("x1_sum", (ROWS, D), F32).ap(),
                "slots": nc.dram_tensor("slot_table", (NE * CAP,), F32).ap(),
                "kvrows": nc.dram_tensor("kvrows", (TOKENS * H, 2 * HD), F32).ap(),
                "scores": nc.dram_tensor("key_scores", (BATCH * H, SEQ), F32).ap()}
        with ExitStack() as c0:
            g["place"] = c0.enter_context(nc.sbuf_tensor("place", [P, NT, NE], F32))
            layer0_dense(nc, g, ins, dram)
            expert_slots(nc, g, dram)
            routed_experts(nc, g, ins, dram)
        g["xnT_all"] = sb("xnT_all", [P, KC, TOKENS])
        layer1_project(nc, g, ins, dram)
        g["keys"] = sb("keys", [P, NPAIR, 2 * HD])
        layer1_ffn_and_keys(nc, g, ins, dram)
        layer1_attention(nc, g, ins, out)


def kernel(**inputs):
    import concourse.bacc as bacc
    from concourse.bass_utils import run_bass_kernel_spmd

    a = {k: np.asarray(v) for k, v in inputs.items()}
    qk_w, qk_b = a["L0_attn_Wqk_w"], a["L0_attn_Wqk_b"]
    columns = [qk_w[D:], a["L0_attn_Wv_w"], qk_w[:D], a["L0_attn_Wn_w"], a["L0_ffn_gate_w"]]
    biases = [qk_b[D:], a["L0_attn_Wv_b"], qk_b[:D], a["L0_attn_Wn_b"], np.zeros(NE, np.float32)]
    arrays = {
        "x": a["L0_attn_x"],
        "cst": shape_constants(),
        "wproj": np.concatenate(columns).T,
        "bproj": np.tile(np.concatenate(biases), (P, 1)),
        "wo": a["L0_attn_Wo_w"].T,
        "bo": np.tile(a["L0_attn_Wo_b"], (P, 1)),
        "wsu": a["L0_ffn_shared_w_gate_up"],
        "wsd": a["L0_ffn_shared_w_down"],
        "wup": a["L0_ffn_w_gate_up"],
        "wdn": a["L0_ffn_w_down"],
        "wkv1": np.concatenate([a["L1_attn_Wk"], a["L1_attn_Wv"]]).T,
        "wsc": np.tile(a["L1_attn_w_score"], (P, 1)),
        "wq1": a["L1_attn_Wq"].T,
        "wo1": a["L1_attn_Wo"].T,
        "wg1": a["L1_ffn_w_gate"].T,
        "wu1": a["L1_ffn_w_up"].T,
        "wd1": a["L1_ffn_w_down"].T,
    }
    nc = bacc.Bacc("TRN2", target_bir_lowering=False, num_devices=1)
    feed, ins = {}, {}
    for name, v in arrays.items():
        v = np.ascontiguousarray(v)
        feed["in_" + name] = v
        ins[name] = nc.dram_tensor("in_" + name, v.shape, mybir.dt.from_np(v.dtype), kind="ExternalInput").ap()
    out = nc.dram_tensor("out", (BATCH, SEQ, D), F32, kind="ExternalOutput").ap()
    layers(nc, ins, out)
    r = run_bass_kernel_spmd(nc, [feed], core_ids=[0])
    return r.results[0]["out"]
```

```python
from contextlib import ExitStack

import numpy as np

import concourse.bass as bass
from concourse import mybir

ALU = mybir.AluOpType
ACT = mybir.ActivationFunctionType
AX_X = mybir.AxisListType.X
F32 = mybir.dt.float32
BF16 = mybir.dt.bfloat16
F32R = mybir.dt.float32r
I32 = mybir.dt.int32

P = 128
BATCH, SEQ, D = 8, 1024, 256
TOKENS = BATCH * SEQ
NT = TOKENS // P
BT = SEQ // P
KC = D // P
H, HD = 16, 16
NE, TOPE, CAP = 32, 4, 256
EPS = 1e-5
BIG = 3.0e38

PK, PV, PQ, PN, PL, PW = 0, 256, 512, 768, 784, 816
XW = D + NE
DUMP = TOKENS
ROWS = TOKENS + P

_C = {}
_w = 0
for _name, _n in (("ident", P), ("causal", P), ("strict", P), ("block", P), ("even", 1), ("odd", 1),
                  ("part", 1), ("dump", 1), ("tile1", NT), ("iota16", 16), ("ediag", 8), ("eown", 8), ("lowkeys", 1),
                  ("highkeys", 1), ("keybase", 1)):
    _C[_name] = (_w, _w + _n)
    _w += _n
CW = _w


def shape_constants():
    c = np.zeros((P, CW), np.float32)
    i, j = np.arange(P)[:, None], np.arange(P)[None, :]

    def put(name, v):
        a, b = _C[name]
        c[:, a:b] = v

    put("ident", i == j)
    put("causal", i <= j)
    put("strict", i < j)
    put("block", i // HD == j // HD)
    put("even", i // HD % 2 == 0)
    put("odd", i // HD % 2 == 1)
    put("part", i)
    put("dump", DUMP + i + P)
    put("tile1", np.arange(NT)[None, :] + 1)
    put("iota16", np.arange(16)[None, :])
    put("ediag", i // 16 == np.arange(8)[None, :])
    put("eown", i % 8 == np.arange(8)[None, :])
    put("lowkeys", i < 64)
    put("highkeys", i >= 64)
    put("keybase", i // H * (SEQ * H) + i % H)
    return c


class Chain:

    def __init__(self, eng, sem, base=0):
        self.eng, self.sem, self.base, self.k = eng, sem, base, 0

    def mark(self, ins):
        self.k += 1
        ins.then_inc(self.sem, 1)
        return self.k

    def wait(self, k=None):
        self.eng.wait_ge(self.sem, self.base + (self.k if k is None else k))


LN_MARKS = 15


def tile_stats(dve, x_all, ln, tile0, k):
    return dve.bn_stats(ln["st"][:, k, :], x_all[:, tile0 + k, :])


def layernorm_stats(dve, step, x_all, ln, tile0, n, begun=0):
    ve, r, t = ln["ve"][:, 0:n], ln["r"][:, 0:n], ln["t"][:, 0:n]
    for k in range(begun, n):
        last = tile_stats(dve, x_all, ln, tile0, k)
    step.mark(last)
    step.wait()
    step.mark(dve.memset(ve, EPS))
    for k in range(n):
        last = dve.bn_aggr(ln["mv"][:, k, :], ln["st"][:, k, :])
    step.mark(last)
    step.wait()
    step.mark(dve.tensor_tensor(ve, ve, ln["mv"][:, 0:n, 1], ALU.add))
    step.wait()
    step.mark(dve.tensor_scalar(t.bitcast(I32), ve.bitcast(I32), 1, None, ALU.arith_shift_right))
    step.wait()
    step.mark(dve.tensor_scalar(r.bitcast(I32), t.bitcast(I32), -1, 0x5F3759DF, ALU.mult, ALU.add))
    step.wait()
    for k in range(3):
        dst = r if k < 2 else ln["rstd"][:, bass.ds(tile0, n)]
        step.mark(dve.tensor_tensor(t, r, r, ALU.mult))
        step.wait()
        step.mark(dve.scalar_tensor_tensor(out=t, in0=t, scalar=-0.5, in1=ve, op0=ALU.mult, op1=ALU.mult))
        step.wait()
        last = dve.scalar_tensor_tensor(out=dst, in0=t, scalar=1.5, in1=r, op0=ALU.add, op1=ALU.mult)
        if k < 2:
            step.mark(last)
            step.wait()
    step.mark(last)
    step.wait()
    return dve.scalar_tensor_tensor(out=ln["nmr"][:, bass.ds(tile0, n)], in0=ln["mv"][:, 0:n, 0], scalar=-1.0,
                                    in1=ln["rstd"][:, bass.ds(tile0, n)], op0=ALU.mult, op1=ALU.mult)


def wait(eng, sem, value):
    if not isinstance(value, int) or value > 0:
        eng.wait_ge(sem, value)


def bcast(ap, axis, n):
    return ap.unsqueeze(axis).broadcast_to([*ap.shape[:axis], n, *ap.shape[axis:]])


def layer0_dense(nc, g, ins, dram):
    with ExitStack() as ctx:
        def sb(name, shape, dt=F32):
            return ctx.enter_context(nc.sbuf_tensor(name, shape, dt))

        def sem(name):
            return ctx.enter_context(nc.semaphore(name))

        cst, x_all, ln, place = g["cst"], g["x_all"], g["ln"], g["place"]
        wproj = sb("wproj", [P, KC, PW])
        bproj = sb("bproj", [P, PW])
        wo = sb("wo", [P, KC, D])
        bo = sb("bo", [P, D])
        wsu = sb("wsu", [P, KC, D])
        wsd = sb("wsd", [P, D])
        xn = sb("xn", [P, 2, XW])
        xnT = sb("xnT", [P, 2, KC, P])
        k_sb = sb("k_sb", [P, 2, D])
        vz = sb("vz", [P, 2, H // 2, 64])
        q_in = sb("q_in", [P, 2, 308])
        qs = sb("qs", [P, 2, D])
        qkT = sb("qkT", [P, 2, 4, P])
        qbd = sb("qbd", [P, 2, KC, 8, P])
        at = sb("at", [P, 2, H, P])
        sbd = sb("sbd", [P, 2, KC, P])
        oT = sb("oT", [P, 2, KC, P])
        hT = sb("hT", [P, 2, P])
        th = sb("th", [P, P])
        hg = sb("hg", [P, P])
        nexp = sb("nexp", [P, H])
        elog = sb("elog", [P, NE])
        ewm = sb("ewm", [P, NE])
        top8 = sb("top8", [P, 8])
        negmax = sb("negmax", [P, 1])
        rep = sb("rep", [P, NE + 4])
        ssum = sb("ssum", [P, 1])
        rsum = sb("rsum", [P, 1])
        far = sb("far", [P, NE])
        maskb = sb("maskb", [P, 2, NE], BF16)
        msum = sb("msum", [P, 8, NE], BF16)
        strictb = sb("strictb", [P, P], BF16)
        onesb = sb("onesb", [P, P], BF16)
        zrow = sb("zrow", [P, XW])
        b_tg, b_kv, b_q, b_t2, b_a0, b_a1, b_o, b_s = g["banks"]
        b_a = (b_a0, b_a1)

        w_loaded = sem("w_loaded")
        x_loaded = sem("x_loaded")
        consts_ready = sem("consts_ready")
        zeros_stored = sem("zeros_stored")
        ln_done = sem("ln_done")
        xn_done = sem("xn_done")
        xn_stored = [sem("xn_stored0"), sem("xn_stored1")]
        x1_stored = sem("x1_stored")
        xb_done = sem("xb_done")
        t1_done = sem("t1_done")
        xnT_done = sem("xnT_done")
        kvp_done = sem("kvp_done")
        qp_done = sem("qp_done")
        kv_done = sem("kv_done")
        qin_done = sem("qin_done")
        negmax_done = sem("negmax_done")
        mask_done = sem("mask_done")
        nexp_done = sem("nexp_done")
        elog_done = sem("elog_done")
        qs_done = sem("qs_done")
        weights_done = sem("weights_done")
        t2_done = sem("t2_done")
        qkT_done = sem("qkT_done")
        spread_done = sem("spread_done")
        s_done = sem("s_done")
        sbd_done = sem("sbd_done")
        a_done = sem("a_done")
        am_done = sem("am_done")
        gu_done = sem("gu_done")
        tanh_done = sem("tanh_done")
        h_done = sem("h_done")
        o_done = sem("o_done")
        oT_done = sem("oT_done")
        pos_done = sem("pos_done")
        place_done = sem("place_done")
        y_done = sem("y_done")
        x1_done = sem("x1_done")
        dstep = sem("dstep")
        block = ctx.enter_context(nc.Block())

        xt = ins["x"].rearrange("b (c p) d -> b p c d", p=P)
        rows_v = dram["xrows"].rearrange("(t p) w -> t p w", p=P)
        x1_v = dram["x1"].rearrange("(t p) w -> t p w", p=P)
        ident = cst[:, _C["ident"][0]:_C["ident"][1]]
        causal = cst[:, _C["causal"][0]:_C["causal"][1]]
        blockm = cst[:, _C["block"][0]:_C["block"][1]]
        headm = cst[:, _C["ediag"][0]:_C["ediag"][1]]

        def batches(eng, body):
            with eng.Fori(0, BATCH - 1) as b:
                body(b, False)
            body(BATCH - 1, True)

        def batches_peeled(eng, body):
            body(0, True, False)
            with eng.Fori(1, BATCH - 1) as b:
                body(b, False, False)
            body(BATCH - 1, False, True)

        @block.sync
        def _(sp):
            sp.dma_start(cst[:, :], ins["cst"]).then_inc(w_loaded, 16)
            sp.dma_start(x_all[:, 0:BT, :], xt[0]).then_inc(x_loaded, 16)
            for dst, src in ((wproj, "wproj"), (wo, "wo"), (wsu, "wsu")):
                sp.dma_start(dst[:, :, :], ins[src].rearrange("(k p) n -> p k n", p=P)).then_inc(w_loaded, 16)
            for dst, src in ((bproj, "bproj"), (bo, "bo"), (wsd, "wsd")):
                sp.dma_start(dst[:, :], ins[src]).then_inc(w_loaded, 16)

            def load_x(b):
                sp.wait_ge(x_loaded, 16 * b)
                sp.dma_start(x_all[:, bass.ds(b * BT, BT), :], xt[b]).then_inc(x_loaded, 16)

            load_x(1)
            sp.wait_ge(consts_ready, 1)
            sp.dma_start(rows_v[NT], zrow[:, :]).then_inc(zeros_stored, 16)
            sp.dma_start(x1_v[NT], zrow[:, 0:D]).then_inc(zeros_stored, 16)

            def store_row(m, par, half):
                sp.wait_ge(weights_done, m + 1)
                sp.dma_start(rows_v[m], xn[:, par, :]).then_inc(xn_stored[par], 16)

            store_row(0, 0, 0)

            def body(b, last):
                for c in range(BT):
                    n = b * BT + c
                    if not (last and c == BT - 1):
                        store_row(n + 1, (c + 1) % 2, 0)
                    sp.wait_ge(x1_done, n + 1)
                    sp.dma_start(x1_v[n], x_all[:, n, :]).then_inc(x1_stored, 16)

            with sp.Fori(0, BATCH - 2) as b:
                load_x(b + 2)
                body(b, False)
            for b in (BATCH - 2, BATCH - 1):
                body(b, b == BATCH - 1)
            for par in range(2):
                sp.wait_ge(xn_stored[par], 16 * NT // 2)
            sp.wait_ge(x1_stored, 16 * NT)
            sp.wait_ge(zeros_stored, 32)

        @block.gpsimd
        def _(pool):
            def spread_heads(n, par):
                pool.wait_ge(qkT_done, n + 1)
                for hf in range(KC):
                    pool.tensor_tensor(qbd[:, par, hf, :, :], bcast(qkT[:, par, hf, :], 1, 8), bcast(headm, 2, P),
                                       ALU.mult).then_inc(spread_done, 1)

            def add_out_bias(n):
                pool.wait_ge(xn_done, n + 1)
                pool.tensor_tensor(x_all[:, n, :], x_all[:, n, :], bo[:, :], ALU.add).then_inc(xb_done, 1)

            pool.wait_ge(w_loaded, 16 * 7)
            pool.wait_ge(consts_ready, 1)

            def body(b, last):
                for c in range(BT):
                    n = b * BT + c
                    add_out_bias(n)
                    spread_heads(n, c % 2)

            batches(pool, body)

        @block.scalar
        def _(act):
            def norm(k, par, first):
                if not first:
                    act.wait_ge(t1_done, k - 1)
                    act.wait_ge(xn_stored[par], 16 * (k // 2) if isinstance(k, int) else 0)
                act.activation(xn[:, par, 0:D], x_all[:, k, :], ACT.Identity, bias=ln["nmr"][:, bass.ds(k, 1)],
                               scale=ln["rstd"][:, bass.ds(k, 1)]).then_inc(xn_done, 1)

            def put_xnT(m, par):
                act.wait_ge(t1_done, m + 1)
                act.copy(xnT[:, par, :, :], b_tg[:, 0:256].rearrange("p (k t) -> p k t", k=KC)).then_inc(xnT_done, 1)

            def put_qkT(n, par):
                act.wait_ge(t2_done, n + 1)
                act.copy(qkT[:, par, :, :], b_t2[:, :].rearrange("p (k t) -> p k t", k=4)).then_inc(qkT_done, 1)

            def exps(m, par):
                act.wait_ge(qin_done, m + 1)
                act.activation(nexp[:, :], q_in[:, par, 256:272], ACT.Exp, scale=-1.0).then_inc(nexp_done, 1)
                act.wait_ge(negmax_done, m + 1)
                act.activation(elog[:, :], q_in[:, par, 272:304], ACT.Exp, bias=negmax[:, :]).then_inc(elog_done, 1)

            def gate_tanh(m):
                act.wait_ge(gu_done, m + 1)
                act.activation(th[:, :], b_tg[:, 256:384], ACT.Tanh, scale=0.5).then_inc(tanh_done, 1)

            def put_oT(n, par):
                act.wait_ge(o_done, n + 1)
                act.copy(oT[:, par, :, :], b_o[:, 0:256].rearrange("p (k t) -> p k t", k=KC)).then_inc(oT_done, 1)

            act.wait_ge(ln_done, 1)
            norm(0, 0, True)
            norm(1, 1, True)
            put_xnT(0, 0)
            exps(0, 0)
            gate_tanh(0)

            def body(b, last):
                for c in range(BT):
                    n = b * BT + c
                    if not (last and c == BT - 1):
                        put_xnT(n + 1, (c + 1) % 2)
                    put_qkT(n, c % 2)
                    if not (last and c == BT - 1):
                        exps(n + 1, (c + 1) % 2)
                    if not (last and c >= BT - 2):
                        if c == BT - 2:
                            act.wait_ge(ln_done, b + 2)
                        act.wait_ge(xn_stored[c % 2], b * (16 * BT // 2) + 16 * (c // 2 + 1))
                        act.wait_ge(t1_done, n + 1)
                        act.activation(xn[:, c % 2, 0:D], x_all[:, n + 2, :], ACT.Identity,
                                       bias=ln["nmr"][:, bass.ds(n + 2, 1)],
                                       scale=ln["rstd"][:, bass.ds(n + 2, 1)]).then_inc(xn_done, 1)
                    if not (last and c == BT - 1):
                        gate_tanh(n + 1)
                    put_oT(n, c % 2)

            batches(act, body)

        @block.vector
        def _(dve):
            LN, KVQ, ROUTE = LN_MARKS, 0, 9
            setup = Chain(dve, dstep)
            dve.wait_ge(w_loaded, 16 * 7)
            dve.memset(vz[:, :, :, :], 0.0)
            dve.memset(q_in[:, :, 304:308], BIG)
            dve.memset(msum[:, 0, :], 0.0)
            dve.memset(onesb[:, :], 1.0)
            dve.memset(zrow[:, :], 0.0)
            dve.tensor_copy(strictb[:, :], cst[:, _C["strict"][0]:_C["strict"][1]]).then_inc(am_done, 2)
            setup.mark(dve.memset(ssum[:, :], 0.0))
            setup.wait()
            dve.memset(rsum[:, :], 0.0).then_inc(consts_ready, 1)
            dve.wait_ge(x_loaded, 16)
            layernorm_stats(dve, setup, x_all, ln, 0, BT).then_inc(ln_done, 1)
            fixed = setup.k
            PER_TILE = 8

            def project(m, par):
                dve.wait_ge(kvp_done, m + 1)
                dve.tensor_tensor(k_sb[:, par, :], b_kv[:, 0:D], bproj[:, PK:PK + D], ALU.add)
                dve.tensor_tensor(vz[:, par, :, :].rearrange("p a (x e) -> p a x e", e=HD)[:, :, 0::3, :],
                                  b_kv[:, D:2 * D].rearrange("p (a x e) -> p a x e", x=2, e=HD),
                                  bproj[:, PV:PV + D].rearrange("p (a x e) -> p a x e", x=2, e=HD),
                                  ALU.add).then_inc(kv_done, 1)
                dve.wait_ge(qp_done, m + 1)
                dve.tensor_tensor(q_in[:, par, 0:304], b_q[:, 0:304], bproj[:, PQ:PW], ALU.add).then_inc(qin_done, 1)

            def route(m, par, cm, step):
                logits = q_in[:, par, 272:308]
                step.mark(dve.max(top8[:, :], logits))
                step.wait()
                dve.tensor_scalar(negmax[:, :], top8[:, 4:5], -1.0, None, ALU.mult).then_inc(negmax_done, 1)
                step.mark(dve.match_replace(rep[:, :], top8[:, :], logits, -BIG))
                step.wait()
                step.mark(dve.tensor_scalar(maskb[:, par, :], rep[:, 0:NE], -1e38, None, ALU.is_lt))
                dve.tensor_scalar(far[:, :], rep[:, 0:NE], -1e38, 1024.0, ALU.is_ge, ALU.mult)
                step.wait()
                dve.tensor_tensor(msum[:, (cm + 1) % 8, :], msum[:, cm, :], maskb[:, par, :],
                                  ALU.add).then_inc(mask_done, 1)
                dve.wait_ge(nexp_done, m + 1)
                dve.tensor_tensor(qs[:, par, :].rearrange("p (h e) -> p h e", h=H),
                                  q_in[:, par, 0:D].rearrange("p (h e) -> p h e", h=H),
                                  bcast(nexp[:, :], 2, HD), ALU.mult).then_inc(qs_done, 1)

            def weigh(m, par, step):
                dve.wait_ge(elog_done, m + 1)
                step.mark(dve.tensor_tensor(ewm[:, :], elog[:, :], maskb[:, par, :], ALU.mult))
                step.wait()
                step.mark(dve.tensor_reduce(ssum[:, :], ewm[:, :], AX_X, ALU.add))
                step.wait()
                step.mark(dve.reciprocal(rsum[:, :], ssum[:, :]))
                step.wait()
                dve.tensor_scalar(xn[:, par, D:XW], ewm[:, :], rsum[:, :], None, ALU.mult).then_inc(weights_done, 1)

            def shared_act(m, par, step):
                dve.wait_ge(tanh_done, m + 1)
                step.mark(dve.scalar_tensor_tensor(out=hg[:, :], in0=th[:, :], scalar=1.0, in1=b_tg[:, 256:384],
                                                   op0=ALU.add, op1=ALU.mult))
                step.wait()
                dve.scalar_tensor_tensor(out=hT[:, par, :], in0=hg[:, :], scalar=0.5, in1=b_tg[:, 384:512],
                                         op0=ALU.mult, op1=ALU.mult).then_inc(h_done, 1)

            def places(m):
                dve.wait_ge(pos_done, m + 1)
                dve.tensor_tensor(place[:, m, :], b_q[:, 304:336], far[:, :], ALU.add).then_inc(place_done, 1)

            def state(s, nxt):
                dve.wait_ge(s_done, s)
                dve.tensor_tensor(sbd[:, nxt, :, :], b_s[:, 0:256].rearrange("p (k t) -> p k t", k=KC),
                                  bcast(blockm, 1, KC), ALU.mult).then_inc(sbd_done, 1)

            def mask_scores(n, par, j):
                dve.wait_ge(a_done, 4 * n + j + 1)
                dve.tensor_tensor(at[:, par, 4 * j:4 * j + 4, :], b_a[j % 2][:, :].rearrange("p (h t) -> p h t", h=4),
                                  bcast(causal, 1, 4), ALU.mult).then_inc(am_done, 1)

            def residual(n):
                dve.wait_ge(xb_done, n + 1)
                dve.wait_ge(y_done, n + 1)
                dve.tensor_tensor(x_all[:, n, :], x_all[:, n, :], b_o[:, 256:512], ALU.add).then_inc(x1_done, 1)

            first = Chain(dve, dstep, fixed)
            project(0, 0)
            dve.wait_ge(qin_done, 1)
            route(0, 0, 0, first)
            shared_act(0, 0, first)
            weigh(0, 0, first)
            places(0)
            fixed += first.k
            per_tile = first.k
            per_batch = per_tile * BT + LN_MARKS

            def body(b, first, last):
                step = Chain(dve, dstep, fixed + b * per_batch)
                for c in range(BT):
                    n = b * BT + c
                    more = not (last and c == BT - 1)
                    par = (c + 1) % 2
                    if c < BT - 1:
                        state(b * (BT - 1) + c + 1, (c + 1) % 2)
                    if not (first and c == 0):
                        residual(n - 1)
                    if more:
                        project(n + 1, par)
                        dve.wait_ge(qin_done, n + 2)
                    for j in range(4):
                        mask_scores(n, c % 2, j)
                    if more:
                        route(n + 1, par, (c + 1) % 8, step)
                        shared_act(n + 1, par, step)
                        weigh(n + 1, par, step)
                        places(n + 1)
                    if not last and c < 4:
                        if c == 0:
                            dve.wait_ge(x_loaded, b * 16 + 32)
                        for k in range(2 * c, min(2 * c + 2, BT - 1)):
                            tile_stats(dve, x_all, ln, (b + 1) * BT, k)
                    if not last and c == 4:
                        layernorm_stats(dve, step, x_all, ln, (b + 1) * BT, BT, BT - 1).then_inc(ln_done, 1)
                assert last or step.k == per_batch

            batches_peeled(dve, body)
            residual(NT - 1)

        @block.tensor
        def _(pe):
            def transpose_norm(m, par):
                pe.wait_ge(xn_done, m + 1)
                for k in range(KC):
                    last = pe.transpose(b_tg[:, k * P:(k + 1) * P], xn[:, par, k * P:(k + 1) * P], ident)
                last.then_inc(t1_done, 1)

            def project(m, par, first):
                pe.wait_ge(xnT_done, m + 1)
                if not first:
                    pe.wait_ge(kv_done, m)
                for k in range(KC):
                    last = pe.matmul(b_kv[:, :], xnT[:, par, k, :], wproj[:, k, 0:512], start=(k == 0),
                                     stop=(k == KC - 1))
                last.then_inc(kvp_done, 1)
                if not first:
                    pe.wait_ge(place_done, m)
                for k in range(KC):
                    last = pe.matmul(b_q[:, 0:304], xnT[:, par, k, :], wproj[:, k, 512:PW], start=(k == 0),
                                     stop=(k == KC - 1))
                last.then_inc(qp_done, 1)

            def shared_up(m, par):
                for gu in range(2):
                    for k in range(KC):
                        last = pe.matmul(b_tg[:, 256 + gu * P:256 + (gu + 1) * P], wsu[:, k, gu * P:(gu + 1) * P],
                                         xnT[:, par, k, :], start=(k == 0), stop=(k == KC - 1))
                last.then_inc(gu_done, 1)

            def positions(m, par, cm):
                pe.wait_ge(mask_done, m + 1)
                pe.matmul(b_q[:, 304:336], strictb[:, :], maskb[:, par, :], start=True, stop=False)
                pe.matmul(b_q[:, 304:336], onesb[:, :], msum[:, cm, :], start=False, stop=True).then_inc(pos_done, 1)

            def transpose_qk(n, par):
                pe.wait_ge(qs_done, n + 1)
                for k in range(KC):
                    pe.transpose(b_t2[:, k * P:(k + 1) * P], qs[:, par, k * P:(k + 1) * P], ident)
                for k in range(KC):
                    last = pe.transpose(b_t2[:, (2 + k) * P:(3 + k) * P], k_sb[:, par, k * P:(k + 1) * P], ident)
                last.then_inc(t2_done, 1)

            def v_pairs(par, hf):
                return vz[:, par, 4 * hf:4 * hf + 4, :].rearrange("p a (x e) -> p a x e", e=HD)[:, :, 0::3, :]

            def state(par, c):
                for k in range(KC):
                    last = pe.matmul(b_s[:, k * P:(k + 1) * P].rearrange("p (a x e) -> p a x e", x=2, e=HD),
                                     k_sb[:, par, k * P:(k + 1) * P], v_pairs(par, k),
                                     start=(c == 0 and k == 0), stop=(k == 1), skip_group_check=True)
                last.then_inc(s_done, 1)

            def head_scores(n, par):
                for j in range(4):
                    if j % 2 == 0:
                        pe.wait_ge(spread_done, 2 * n + j // 2 + 1)
                    pe.wait_ge(am_done, 4 * n + j + 1)
                    pe.matmul(b_a[j % 2][:, :], qkT[:, par, 2 + j // 2, :],
                              qbd[:, par, j // 2, 4 * (j % 2):4 * (j % 2) + 4, :], start=True,
                              stop=True).then_inc(a_done, 1)

            def attend(n, par, c):
                pe.wait_ge(am_done, 4 * n + 6)
                for hf in range(KC):
                    cols = slice(hf * P, (hf + 1) * P)
                    if c > 0:
                        pe.matmul(b_o[:, cols], sbd[:, par, hf, :], qkT[:, par, hf, :], start=True, stop=False,
                                  skip_group_check=True)
                    for eo in range(2):
                        for pr in range(4):
                            last = pe.matmul(b_o[32 * pr:32 * pr + 32, cols],
                                             vz[:, par, 4 * hf + pr, 32 * eo:32 * eo + 32],
                                             at[:, par, 8 * hf + 2 * pr + eo, :], start=(c == 0 and eo == 0),
                                             stop=(eo == 1), skip_group_check=True)
                last.then_inc(o_done, 1)

            def output(n, par):
                pe.wait_ge(oT_done, n + 1)
                for k in range(KC):
                    pe.matmul(b_o[:, 256:512], oT[:, par, k, :], wo[:, k, :], start=(k == 0), stop=False)
                pe.matmul(b_o[:, 256:512], hT[:, par, :], wsd[:, :], start=False, stop=True).then_inc(y_done, 1)

            pe.wait_ge(w_loaded, 16 * 7)
            pe.wait_ge(consts_ready, 1)
            transpose_norm(0, 0)
            project(0, 0, True)
            shared_up(0, 0)
            positions(0, 0, 0)

            def body(b, first, last):
                for c in range(BT):
                    n = b * BT + c
                    more = not (last and c == BT - 1)
                    par = (c + 1) % 2
                    pe.wait_ge(h_done, n + 1)
                    if more:
                        transpose_norm(n + 1, par)
                    transpose_qk(n, c % 2)
                    if c > 0:
                        pe.wait_ge(sbd_done, b * (BT - 1) + c)
                    if c < BT - 1:
                        state(c % 2, c)
                    if not (first and c == 0):
                        output(n - 1, par)
                    if more:
                        project(n + 1, par, False)
                    head_scores(n, c % 2)
                    if more:
                        shared_up(n + 1, par)
                    wait(pe, x1_done, n)
                    attend(n, c % 2, c)
                    if more:
                        positions(n + 1, par, (c + 1) % 8)

            batches_peeled(pe, body)
            output(NT - 1, 1)


def expert_slots(nc, g, dram):
    with ExitStack() as ctx:
        def sb(name, shape, dt=F32):
            return ctx.enter_context(nc.sbuf_tensor(name, shape, dt))

        def sem(name):
            return ctx.enter_context(nc.semaphore(name))

        cst, place, slot_rows = g["cst"], g["place"], g["slot_rows"]
        banks = g["banks"]
        place_i = sb("place_i", [P, NT, NE], I32)
        part_i = sb("part_i", [P, NT, NE], I32)
        lo = sb("lo", [P, NT, NE], BF16)
        hi = sb("hi", [P, NT, NE], BF16)
        iota_b = sb("iota_b", [P, 16, NE], BF16)
        hot_hi = sb("hot_hi", [P, 4, 4, 16, 8], BF16)
        hot_lo = sb("hot_lo", [P, 4, 16, NE], BF16)
        carry = sb("carry", [P, 4, 2, 16, NE], BF16)
        own = sb("own", [P, 4, 2, 8, 16])
        parts = sb("parts", [P, 4, 2, 16])
        table = sb("table", [P, 4, 16])
        slots_t = sb("slots_t", [2 * NE, P])
        empty = sb("empty", [P, 2 * NE])

        digits_done = sem("digits_done")
        hot_hi_done = sem("hot_hi_done")
        hot_lo_done = sem("hot_lo_done")
        part_done = sem("part_done")
        tile_done = sem("tile_done")
        slots_done = sem("slots_done")
        own_done = sem("own_done")
        table_done = sem("table_done")
        table_moved = sem("table_moved")
        turned = sem("turned")
        rows_done = sem("rows_done")
        bstep = sem("bstep")
        block = ctx.enter_context(nc.Block())

        partc = cst[:, _C["part"][0]:_C["part"][1]]
        tile1 = _C["tile1"][0]
        ediag = cst[:, _C["eown"][0]:_C["eown"][1]]
        slots_v = dram["slots"].rearrange("(p w) -> p w", p=P)
        slots_back = dram["slots"].rearrange("(f h e g l) -> f g e h l", f=2, h=8, e=8, g=4)

        def tiles(eng, body):
            body(0, True)
            with eng.Fori(1, NT // 4) as i:
                body(i, False)

        @block.vector
        def _(dve):
            step = Chain(dve, bstep)
            step.mark(dve.tensor_scalar(place_i[:, :, :], place[:, :, :], float(CAP), None, ALU.min))
            dve.tensor_copy(iota_b[:, :, :], bcast(cst[:, _C["iota16"][0]:_C["iota16"][1]], 2, NE))
            step.wait()
            step.mark(dve.tensor_scalar(part_i[:, :, :], place_i[:, :, :], 4, None, ALU.arith_shift_right))
            step.wait()
            step.mark(dve.tensor_copy(hi[:, :, :], part_i[:, :, :]))
            step.mark(dve.tensor_scalar(place_i[:, :, :], place_i[:, :, :], 15, None, ALU.bitwise_and))
            step.wait()
            dve.tensor_copy(lo[:, :, :], place_i[:, :, :]).then_inc(digits_done, 1)
            dve.wait_ge(digits_done, 1)
            fixed = step.k

            def body(i, first):
                for par in range(4):
                    t = i * 4 + par
                    wait(dve, slots_done, t - 3)
                    dve.tensor_tensor(hot_lo[:, par, :, :], bcast(lo[:, t, :], 1, 16), iota_b[:, :, :],
                                      ALU.is_equal).then_inc(hot_lo_done, 1)
                    dve.tensor_tensor(hot_hi[:, par, :, :, :], bcast(hi[:, t, :].rearrange("p (g e) -> p g e", g=4), 2, 16),
                                      bcast(iota_b[:, :, 0:8], 1, 4), ALU.is_equal).then_inc(hot_hi_done, 1)
                    dve.wait_ge(hot_lo_done, t + 1)
                    dve.tensor_scalar(carry[:, par, 0, :, :], hot_lo[:, par, :, :], partc, None,
                                      ALU.mult).then_inc(part_done, 1)

            tiles(dve, body)
            step = Chain(dve, bstep, fixed)
            dve.wait_ge(slots_done, NT)
            for gr in range(4):
                last = dve.tensor_tensor(own[:, gr, :, :, :],
                                         banks[gr][:, 0:256].rearrange("p (x e l) -> p x e l", x=2, e=8),
                                         bcast(bcast(ediag, 2, 16), 1, 2), ALU.mult)
            step.mark(last)
            step.wait()
            for gr in range(4):
                last = dve.tensor_reduce(parts[:, gr, :, :], own[:, gr, :, :, :].rearrange("p x e l -> p x l e"), AX_X,
                                         ALU.add)
            step.mark(last)
            step.wait()
            step.mark(dve.scalar_tensor_tensor(out=table[:, :, :], in0=parts[:, :, 1, :], scalar=float(P),
                                               in1=parts[:, :, 0, :], op0=ALU.mult, op1=ALU.add))
            step.wait()
            dve.tensor_scalar(table[:, :, :], table[:, :, :], float(-P), None, ALU.add).then_inc(table_done, 1)
            dve.wait_ge(turned, 1)
            step.mark(dve.tensor_scalar(empty[:, :], banks[4][:, 0:2 * NE], 0.0,
                                        cst[:, _C["dump"][0]:_C["dump"][1]], ALU.is_lt, ALU.mult))
            step.wait()
            dve.tensor_tensor(slot_rows[:, :].rearrange("p (e f) -> p f e", f=2),
                              banks[4][:, 0:2 * NE].rearrange("p (f e) -> p f e", f=2),
                              empty[:, :].rearrange("p (f e) -> p f e", f=2), ALU.add).then_inc(rows_done, 1)
            dve.wait_ge(rows_done, 1)

        @block.scalar
        def _(act):
            def body(i, first):
                for par in range(4):
                    t = i * 4 + par
                    act.wait_ge(hot_lo_done, t + 1)
                    act.activation(carry[:, par, 1, :, :], hot_lo[:, par, :, :], ACT.Copy,
                                   scale=cst[:, bass.ds(t + tile1, 1)]).then_inc(tile_done, 1)

            tiles(act, body)

        @block.tensor
        def _(pe):
            def body(i, first):
                for par in range(4):
                    t = i * 4 + par
                    pe.wait_ge(part_done, t + 1)
                    pe.wait_ge(tile_done, t + 1)
                    for gr in range(4):
                        last = pe.matmul(banks[gr][:, 0:256].rearrange("p (x e l) -> p x e l", x=2, e=8),
                                         hot_hi[:, par, gr, :, :].rearrange("p l e -> p (l e)"),
                                         carry[:, par, :, :, 8 * gr:8 * gr + 8].rearrange("p x l e -> p x e l"),
                                         start=(first and par == 0), stop=False, skip_group_check=True)
                    last.then_inc(slots_done, 1)

            tiles(pe, body)
            pe.wait_ge(table_moved, 16 * 9)
            pe.transpose(banks[4][:, 0:2 * NE], slots_t[:, :],
                         cst[0:2 * NE, _C["ident"][0]:_C["ident"][0] + 2 * NE]).then_inc(turned, 1)

        @block.sync
        def _(sp):
            sp.wait_ge(table_done, 1)
            sp.dma_start(slots_v, table[:, :, :].rearrange("p g l -> p (g l)")).then_inc(table_moved, 16)
            sp.wait_ge(table_moved, 16)
            with nc.allow_non_contiguous_dma("slot table in 64-byte runs"):
                for half in range(2):
                    for gr in range(4):
                        r = half * NE + gr * 8
                        sp.dma_start(slots_t[r:r + 8, :].rearrange("e (h l) -> e h l", h=8), slots_back[half, gr])\
                          .then_inc(table_moved, 16)


EU = 8
AHEAD = 4


def routed_experts(nc, g, ins, dram):
    with ExitStack() as ctx:
        def sb(name, shape, dt=F32):
            return ctx.enter_context(nc.sbuf_tensor(name, shape, dt))

        def sem(name):
            return ctx.enter_context(nc.semaphore(name))

        cst, slot_rows = g["cst"], g["slot_rows"]
        wup = sb("wup", [P, EU, KC, D])
        wdn = sb("wdn", [P, EU, D])
        rows_now = sb("rows_now", [P, EU, 2], I32)
        xe = sb("xe", [P, EU, 2, XW])
        xeT = sb("xeT", [P, 2, KC, 2 * P])
        silu = sb("silu", [P, 2 * P])
        hT = sb("ehT", [P, 2, 2 * P])
        ye = sb("ye", [P, EU, 2, D])
        held = sb("held", [P, 2 * EU + 1])
        held_done = sem("held_done")
        b_x, b_u, b_y = g["banks"][0:2], g["banks"][2:4], g["banks"][4:6]

        w_loaded = [sem(f"expert_w{k}") for k in range(EU)]
        x_loaded = [sem(f"expert_x{k}") for k in range(EU)]
        index_done = sem("index_done")
        turned = sem("xe_turned")
        xeT_done = sem("xeT_done")
        up_done = sem("up_done")
        silu_done = sem("silu_done")
        h_done = sem("eh_done")
        down_done = sem("down_done")
        ye_done = sem("ye_done")
        added = sem("added")
        block = ctx.enter_context(nc.Block())
        ident = cst[:, _C["ident"][0]:_C["ident"][1]]
        wup_v = ins["wup"].rearrange("e (k p) n -> e p k n", p=P)

        def experts(eng, body):
            body(0, True, False)
            with eng.Fori(1, NE // EU - 1) as i:
                body(i, False, False)
            body(NE // EU - 1, False, True)

        @block.sync
        def _(sp):
            def body(i, first, last):
                for k in range(EU):
                    e = i * EU + k
                    wait(sp, down_done, e - EU + 1)
                    sp.dma_start(wup[:, k, :, :], wup_v[e]).then_inc(w_loaded[k], 16)
                    sp.dma_start(wdn[:, k, :], ins["wdn"][e]).then_inc(w_loaded[k], 16)

            experts(sp, body)

        @block.gpsimd
        def _(pool):
            def hold(j):
                pool.tensor_tensor(held[:, j + 1:j + 2], held[:, 0:1], held[:, 0:1], ALU.add)

            pool.memset(held[:, :], 0.0).then_inc(held_done, 1)
            pool.wait_ge(held_done, 1)

            def gather(e, k):
                wait(pool, ye_done, e - EU + 1)
                pool.tensor_copy(rows_now[:, k, :], slot_rows[:, bass.ds(e * 2, 2)]).then_inc(index_done, 1)
                pool.wait_ge(index_done, e + 1)
                hold(k)
                for hf in range(2):
                    pool.indirect_dma_start(out=xe[:, k, hf, :], out_offset=None, in_=dram["xrows"],
                                            in_offset=bass.IndirectOffsetOnAxis(ap=rows_now[:, k, hf:hf + 1], axis=0),
                                            bounds_check=ROWS - 1, oob_is_err=False).then_inc(x_loaded[k], 16)

            def add(e, k):
                pool.wait_ge(ye_done, e + 1)
                wait(pool, added, 32 * e)
                hold(EU + k)
                for hf in range(2):
                    pool.indirect_dma_start(out=dram["x1"], in_=ye[:, k, hf, :], in_offset=None,
                                            out_offset=bass.IndirectOffsetOnAxis(ap=rows_now[:, k, hf:hf + 1], axis=0),
                                            bounds_check=ROWS - 1, oob_is_err=True,
                                            compute_op=ALU.add).then_inc(added, 16)

            for e in range(AHEAD):
                gather(e, e)

            def body(i, first, last):
                for k in range(EU):
                    e = i * EU + k
                    if not (last and k >= EU - AHEAD):
                        wait(pool, added, 32 * (e + AHEAD - EU + 1))
                        gather(e + AHEAD, (k + AHEAD) % EU)
                    add(e, k)

            experts(pool, body)
            pool.wait_ge(added, 32 * NE)

        @block.scalar
        def _(act):
            def body(i, first, last):
                for k in range(EU):
                    e = i * EU + k
                    par = k % 2
                    act.wait_ge(turned, e + 1)
                    wait(act, up_done, e - 1)
                    act.copy(xeT[:, par, :, :], b_x[par][:, :].rearrange("p (k t) -> p k t", k=KC))\
                       .then_inc(xeT_done, 1)
                    act.wait_ge(up_done, e + 1)
                    wait(act, h_done, e)
                    act.activation(silu[:, :], b_u[par][:, 0:256], ACT.Silu).then_inc(silu_done, 1)

            experts(act, body)

        @block.vector
        def _(dve):
            def body(i, first, last):
                for k in range(EU):
                    e = i * EU + k
                    par = k % 2
                    dve.wait_ge(silu_done, e + 1)
                    wait(dve, down_done, e - 1)
                    dve.tensor_tensor(hT[:, par, :], silu[:, :], b_u[par][:, 256:512], ALU.mult).then_inc(h_done, 1)
                    dve.wait_ge(down_done, e + 1)
                    wait(dve, added, 32 * (e - EU + 1))
                    for hf in range(2):
                        last_op = dve.tensor_scalar(ye[:, k, hf, :], b_y[par][:, hf * D:(hf + 1) * D],
                                                    xe[:, k, hf, bass.ds(e + D, 1)], None, ALU.mult)
                    last_op.then_inc(ye_done, 1)

            experts(dve, body)

        @block.tensor
        def _(pe):
            def body(i, first, last):
                def turn(j, k):
                    e = (i + j) * EU + k
                    par = k % 2
                    pe.wait_ge(x_loaded[k], (i + j) * 32 + 32)
                    wait(pe, xeT_done, e - 1)
                    for kc in range(KC):
                        for hf in range(2):
                            op = pe.transpose(b_x[par][:, (2 * kc + hf) * P:(2 * kc + hf + 1) * P],
                                              xe[:, k, hf, kc * P:(kc + 1) * P], ident)
                    op.then_inc(turned, 1)

                def up(e, k):
                    par = k % 2
                    pe.wait_ge(xeT_done, e + 1)
                    pe.wait_ge(w_loaded[k], i * 32 + 32)
                    wait(pe, h_done, e - 1)
                    for gu in range(2):
                        for kc in range(KC):
                            op = pe.matmul(b_u[par][:, gu * 256:gu * 256 + 256], wup[:, k, kc, gu * P:(gu + 1) * P],
                                           xeT[:, par, kc, :], start=(kc == 0), stop=(kc == KC - 1))
                    op.then_inc(up_done, 1)

                def down(e, k):
                    par = k % 2
                    pe.wait_ge(h_done, e + 1)
                    wait(pe, ye_done, e - 1)
                    for hf in range(2):
                        op = pe.matmul(b_y[par][:, hf * D:(hf + 1) * D], hT[:, par, hf * P:(hf + 1) * P], wdn[:, k, :],
                                       start=True, stop=True)
                    op.then_inc(down_done, 1)

                if first:
                    turn(0, 0)
                for k in range(EU):
                    e = i * EU + k
                    if k < EU - 1:
                        turn(0, k + 1)
                    elif not last:
                        turn(1, 0)
                    up(e, k)
                    down(e, k)

            experts(pe, body)


ST = 4
NS = NT // ST
HID = 768
MC = HID // P
INT_SCALE = 1.0 / 127.0
TOPK = 64
NPAIR = BATCH * H // 2


def layer1_project(nc, g, ins, dram):
    with ExitStack() as ctx:
        def sb(name, shape, dt=F32):
            return ctx.enter_context(nc.sbuf_tensor(name, shape, dt))

        def sem(name):
            return ctx.enter_context(nc.semaphore(name))

        cst, x_all, xnT, ln = g["cst"], g["x_all"], g["xnT_all"], g["ln"]
        wkv = sb("wkv", [P, KC, 2 * D])
        wsc = sb("wsc", [P, HD])
        wprod = sb("wprod", [P, KC, D])
        widx = sb("widx", [P, KC, H])
        xn = sb("xn1", [P, 2, D])
        xst = sb("xst", [P, 2, KC, 512])
        kv_row = sb("kv_row", [P, 2, 2 * D])
        score = sb("score", [H, 2, 512])
        b_t, b_i, b_kv = g["banks"][0:2], g["banks"][2:4], g["banks"][4:8]

        w_loaded = sem("w1_loaded")
        x_loaded = sem("x1_loaded")
        ln_done = sem("ln1_done")
        widx_done = sem("widx_done")
        xn_done = sem("xn1_done")
        turned = sem("xn1_turned")
        xst_done = sem("xst_done")
        kept = sem("xnT_kept")
        kvp_done = sem("kvp1_done")
        kv_done = sem("kv1_done")
        kv_stored = [sem("kv_stored0"), sem("kv_stored1")]
        idx_done = sem("idx_done")
        score_done = sem("score_done")
        score_stored = [sem("score_stored0"), sem("score_stored1")]
        dstep = sem("d1step")
        block = ctx.enter_context(nc.Block())
        ident = cst[:, _C["ident"][0]:_C["ident"][1]]
        x1_v = dram["x1"][0:TOKENS, :].rearrange("(b c p) d -> b p c d", p=P, c=BT)
        kv_v = dram["kvrows"].rearrange("(t p h) e -> t p (h e)", p=P, h=H)
        score_v = dram["scores"].rearrange("(b h) (s t) -> b s h t", h=H, t=512)

        def batches(eng, body):
            body(0, True, False)
            with eng.Fori(1, BATCH - 1) as b:
                body(b, False, False)
            body(BATCH - 1, False, True)

        @block.sync
        def _(sp):
            sp.dma_start(x_all[:, 0:BT, :], x1_v[0]).then_inc(x_loaded, 16)
            sp.dma_start(wkv[:, :, :], ins["wkv1"].rearrange("(k p) n -> p k n", p=P)).then_inc(w_loaded, 16)
            sp.dma_start(wsc[:, :], ins["wsc"]).then_inc(w_loaded, 16)

            def load_x(b):
                sp.wait_ge(x_loaded, 16 * b)
                sp.dma_start(x_all[:, bass.ds(b * BT, BT), :], x1_v[b]).then_inc(x_loaded, 16)

            load_x(1)

            def store_score(b, s):
                sp.wait_ge(score_done, 2 * b + s + 1)
                sp.dma_start(score_v[b, s], score[:, s, :]).then_inc(score_stored[s], 16)

            def body(b, first, last, load):
                if load:
                    load_x(b + 2)
                for c in range(BT):
                    n = b * BT + c
                    sp.wait_ge(kv_done, n + 1)
                    sp.dma_start(kv_v[n], kv_row[:, c % 2, :]).then_inc(kv_stored[c % 2], 16)
                    if c == 1 and not first:
                        store_score(b - 1, 1)
                    if c == ST + 1:
                        store_score(b, 0)

            body(0, True, False, True)
            with sp.Fori(1, BATCH - 2) as b:
                body(b, False, False, True)
            for b in (BATCH - 2, BATCH - 1):
                body(b, False, b == BATCH - 1, False)
            store_score(BATCH - 1, 1)
            for par in range(2):
                sp.wait_ge(kv_stored[par], 16 * NT // 2)
                sp.wait_ge(score_stored[par], 16 * BATCH)

        @block.scalar
        def _(act):
            def norm(n, par):
                wait(act, turned, n - 1)
                act.activation(xn[:, par, :], x_all[:, n, :], ACT.Identity, bias=ln["nmr"][:, bass.ds(n, 1)],
                               scale=ln["rstd"][:, bass.ds(n, 1)]).then_inc(xn_done, 1)

            def put(n, c):
                act.wait_ge(turned, n + 1)
                turned_x = b_t[c % 2][:, 0:256].rearrange("p (k t) -> p k t", k=KC)
                act.copy(xst[:, c // ST, :, (c % ST) * P:(c % ST + 1) * P], turned_x).then_inc(xst_done, 1)
                act.copy(xnT[:, :, bass.ds(n * P, P)], turned_x).then_inc(kept, 1)

            def put_score(b, s):
                act.wait_ge(idx_done, 2 * b + s + 1)
                wait(act, score_stored[s], 16 * b)
                act.copy(score[:, s, :], b_i[s][0:H, :]).then_inc(score_done, 1)

            act.wait_ge(ln_done, 1)
            norm(0, 0)
            norm(1, 1)
            put(0, 0)

            def body(b, first, last):
                for c in range(BT):
                    n = b * BT + c
                    if c == 0 and not first:
                        put_score(b - 1, 1)
                    if c == ST:
                        put_score(b, 0)
                    if c == BT - 2 and not last:
                        act.wait_ge(ln_done, b + 2)
                    if not (last and c >= BT - 2):
                        norm(n + 2, c % 2)
                    if not (last and c == BT - 1):
                        put(n + 1, (c + 1) % BT)

            batches(act, body)
            put_score(BATCH - 1, 1)

        @block.vector
        def _(dve):
            step = Chain(dve, dstep)
            dve.wait_ge(x_loaded, 16)
            layernorm_stats(dve, step, x_all, ln, 0, BT).then_inc(ln_done, 1)
            dve.wait_ge(w_loaded, 32)
            step.mark(dve.tensor_tensor(wprod[:, :, :].rearrange("p k (h e) -> p k h e", e=HD),
                                        wkv[:, :, 0:D].rearrange("p k (h e) -> p k h e", e=HD),
                                        bcast(bcast(wsc[:, :], 1, H), 1, KC), ALU.mult))
            step.wait()
            dve.tensor_reduce(widx[:, :, :], wprod[:, :, :].rearrange("p k (h e) -> p k h e", e=HD), AX_X,
                              ALU.add).then_inc(widx_done, 1)
            fixed = step.k

            def body(b, first, last):
                for c in range(BT):
                    n = b * BT + c
                    dve.wait_ge(kvp_done, n + 1)
                    if not (first and c < 2):
                        dve.wait_ge(kv_stored[c % 2], b * (16 * BT // 2) + 16 * (c // 2))
                    dve.tensor_copy(kv_row[:, c % 2, :].rearrange("p (h x e) -> p x h e", h=H, x=2),
                                    b_kv[c % 4][:, :].rearrange("p (x h e) -> p x h e", h=H, x=2)).then_inc(kv_done, 1)
                    if not last and c < 4:
                        if c == 0:
                            dve.wait_ge(x_loaded, b * 16 + 32)
                        for k in range(2 * c, min(2 * c + 2, BT - 1)):
                            tile_stats(dve, x_all, ln, (b + 1) * BT, k)
                    if not last and c == 4:
                        step = Chain(dve, dstep, fixed + b * LN_MARKS)
                        layernorm_stats(dve, step, x_all, ln, (b + 1) * BT, BT, BT - 1).then_inc(ln_done, 1)

            batches(dve, body)

        @block.tensor
        def _(pe):
            def turn(n, c):
                pe.wait_ge(xn_done, n + 1)
                wait(pe, kept, n - 1)
                for k in range(KC):
                    op = pe.transpose(b_t[c % 2][:, k * P:(k + 1) * P], xn[:, c % 2, k * P:(k + 1) * P], ident)
                op.then_inc(turned, 1)

            def project(n, c):
                pe.wait_ge(xst_done, n + 1)
                wait(pe, kv_done, n - 3)
                for k in range(KC):
                    op = pe.matmul(b_kv[c % 4][:, :], xst[:, c // ST, k, (c % ST) * P:(c % ST + 1) * P], wkv[:, k, :],
                                   start=(k == 0), stop=(k == KC - 1))
                op.then_inc(kvp_done, 1)

            def key_scores(b, s):
                pe.wait_ge(xst_done, b * BT + (s + 1) * ST)
                wait(pe, score_done, 2 * b + s - 1)
                for k in range(KC):
                    op = pe.matmul(b_i[s][0:H, :], widx[:, k, :], xst[:, s, k, :], start=(k == 0), stop=(k == KC - 1))
                op.then_inc(idx_done, 1)

            pe.wait_ge(w_loaded, 32)
            turn(0, 0)

            def body(b, first, last):
                for c in range(BT):
                    n = b * BT + c
                    if c == 0 and not first:
                        key_scores(b - 1, 1)
                    if c == ST:
                        if first:
                            pe.wait_ge(widx_done, 1)
                        key_scores(b, 0)
                    if not (last and c == BT - 1):
                        turn(n + 1, c + 1)
                    project(n, c)

            batches(pe, body)
            key_scores(BATCH - 1, 1)


def layer1_ffn_and_keys(nc, g, ins, dram):
    with ExitStack() as ctx:
        def sb(name, shape, dt=F32):
            return ctx.enter_context(nc.sbuf_tensor(name, shape, dt))

        def sem(name):
            return ctx.enter_context(nc.semaphore(name))

        cst, x_all, xnT, keys = g["cst"], g["x_all"], g["xnT_all"], g["keys"]
        scores = sb("scores_sb", [P, 2, SEQ])
        best = sb("best", [P, 2, 8])
        picked = sb("picked", [P, TOPK], mybir.dt.uint32)
        pickedf = sb("pickedf", [P, TOPK])
        key_row = sb("key_row", [P, P])
        key_rows = sb("key_rows", [P, NPAIR], I32)
        wg = sb("wg", [P, KC, HID], F32R)
        wu = sb("wu", [P, KC, HID], F32R)
        wd = sb("wd", [P, MC, D], F32R)
        x_hi = sb("x_hi", [P, 2, KC, 512], F32R)
        x_lo = sb("x_lo", [P, 2, KC, 512], F32R)
        silu = sb("fsilu", [P, 2, 512])
        h = sb("fh", [P, 2, 512])
        h_hi = sb("h_hi", [P, 3, 512], F32R)
        h_lo = sb("h_lo", [P, 3, 512], F32R)
        b_g, b_u = g["banks"][0:2], g["banks"][2:4]
        b_y = (g["banks"][4:6], g["banks"][6:8])

        wg_loaded = sem("wg_loaded")
        wu_loaded = sem("wu_loaded")
        wd_loaded = sem("wd_loaded")
        weights_done = sem("ffn_weights")
        scores_loaded = sem("scores_loaded")
        key_row_done = sem("key_row_done")
        key_turned = sem("key_turned")
        key_rows_done = sem("key_rows_done")
        keys_loaded = sem("keys_loaded")
        x_hi_done = sem("x_hi_done")
        x_lo_done = sem("x_lo_done")
        up_done = sem("fup_done")
        silu_done = sem("fsilu_done")
        h_done = sem("fh_done")
        h_hi_done = sem("h_hi_done")
        h_lo_done = sem("h_lo_done")
        down_done = sem("fdown_done")
        x_done = sem("fx_done")
        estep = sem("estep")
        block = ctx.enter_context(nc.Block())
        ident = cst[:, _C["ident"][0]:_C["ident"][1]]
        scores_int = scores[:, :, :].rearrange("p n e -> p (n e)").bitcast(I32)[:, 0:KC * HID]
        keys_int = keys[:, :, :].rearrange("p n e -> p (n e)").bitcast(I32)[:, 0:KC * HID]

        def supertiles(eng, body):
            body(0, True, False)
            with eng.Fori(1, NS // 2 - 1) as i:
                body(i, False, False)
            body(NS // 2 - 1, False, True)


        @block.sync
        def _(sp):
            whole = {k: ins[k].rearrange("(k p) n -> p k n", p=P) for k in ("wg1", "wu1", "wd1")}
            sp.dma_start(scores_int.rearrange("p (k n) -> p k n", k=KC), whole["wg1"]).then_inc(wg_loaded, 16)
            sp.dma_start(keys_int.rearrange("p (k n) -> p k n", k=KC), whole["wu1"]).then_inc(wu_loaded, 16)
            sp.wait_ge(weights_done, 1)
            sp.dma_start(scores[:, 0, :], dram["scores"]).then_inc(scores_loaded, 16)
            sp.wait_ge(weights_done, 2)
            sp.dma_start(keys_int.rearrange("p (k n) -> p k n", k=MC), whole["wd1"]).then_inc(wd_loaded, 16)

        @block.gpsimd
        def _(pool):
            pool.wait_ge(key_rows_done, 2)
            for p in range(NPAIR):
                pool.indirect_dma_start(out=keys[:, p, :], out_offset=None, in_=dram["kvrows"],
                                        in_offset=bass.IndirectOffsetOnAxis(ap=key_rows[:, p:p + 1], axis=0),
                                        bounds_check=TOKENS * H - 1, oob_is_err=False).then_inc(keys_loaded, 16)
            pool.wait_ge(keys_loaded, 16 * NPAIR)

        @block.scalar
        def _(act):
            def round_x(t, par):
                act.copy(x_hi[:, par, :, :], xnT[:, :, bass.ds(t * 512, 512)]).then_inc(x_hi_done, 1)

            def whole_to_float(w, src, k, loaded):
                act.wait_ge(loaded, 16)
                act.copy(w[:, :, :], src.rearrange("p (k n) -> p k n", k=k)).then_inc(weights_done, 1)

            round_x(0, 0)
            whole_to_float(wg, scores_int, KC, wg_loaded)
            whole_to_float(wu, keys_int, KC, wu_loaded)

            def body(i, first, last):
                for s in range(2):
                    for m in range(MC):
                        j = (2 * i + s) * MC + m
                        par = m % 2
                        act.wait_ge(up_done, j + 1)
                        wait(act, h_done, j - 1)
                        act.activation(silu[:, par, :], b_g[par][:, :], ACT.Silu, scale=INT_SCALE)\
                           .then_inc(silu_done, 1)
                        if first and s == 0 and m == 0:
                            whole_to_float(wd, keys_int, MC, wd_loaded)
                        act.wait_ge(h_done, j + 1)
                        wait(act, down_done, 2 * (j - 2))
                        act.copy(h_hi[:, (s * MC + m) % 3, :], h[:, par, :]).then_inc(h_hi_done, 1)
                        if m == 1 and not (last and s == 1):
                            round_x(2 * i + s + 1, (s + 1) % 2)

            supertiles(act, body)

        @block.vector
        def _(dve):
            step = Chain(dve, estep)

            def rest_of_x(t, par):
                dve.wait_ge(x_hi_done, t + 1)
                dve.tensor_tensor(x_lo[:, par, :, :], xnT[:, :, bass.ds(t * 512, 512)],
                                  x_hi[:, par, :, :].bitcast(F32), ALU.subtract).then_inc(x_lo_done, 1)

            def choose_keys(r):
                src, dst = scores[:, r % 2, :], scores[:, (r + 1) % 2, :]
                if r == 0:
                    dve.wait_ge(scores_loaded, 16)
                else:
                    step.wait()
                step.mark(dve.max(best[:, r % 2, :], src))
                step.wait()
                dve.max_index(picked[:, 8 * r:8 * r + 8], best[:, r % 2, :], src)
                step.mark(dve.match_replace(dst, best[:, r % 2, :], src, -BIG))

            def key_row_numbers():
                step.wait()
                step.mark(dve.tensor_copy(pickedf[:, :], picked[:, :]))
                step.wait()
                for k in range(2):
                    op = dve.tensor_scalar(key_row[:, k * TOPK:(k + 1) * TOPK], pickedf[:, :], float(H),
                                           cst[:, _C["keybase"][0]:_C["keybase"][1]], ALU.mult, ALU.add)
                op.then_inc(key_row_done, 1)

            def put_key_rows():
                dve.wait_ge(key_turned, 1)
                pairs = b_y[0][0][:, 0:P].rearrange("p (n two) -> p n two", two=2)
                dve.tensor_copy(key_rows[0:TOPK, :], pairs[0:TOPK, :, 0]).then_inc(key_rows_done, 1)
                dve.tensor_copy(key_rows[TOPK:P, :], pairs[TOPK:P, :, 1]).then_inc(key_rows_done, 1)

            def add(t, par, hf):
                dve.wait_ge(down_done, 2 * ((t + 1) * MC - 1) + hf + 1)
                rows = x_all[:, bass.ds(t * ST + 2 * hf, 2), :]
                dve.scalar_tensor_tensor(out=rows, in0=b_y[par][hf][:, :].rearrange("p (c n) -> p c n", c=2),
                                         scalar=INT_SCALE * INT_SCALE, in1=rows, op0=ALU.mult,
                                         op1=ALU.add).then_inc(x_done, 1)

            rest_of_x(0, 0)

            def body(i, first, last):
                for s in range(2):
                    for m in range(MC):
                        j = (2 * i + s) * MC + m
                        par, third = m % 2, (s * MC + m) % 3
                        dve.wait_ge(silu_done, j + 1)
                        wait(dve, h_hi_done, j - 1)
                        dve.tensor_tensor(h[:, par, :], silu[:, par, :], b_u[par][:, :], ALU.mult).then_inc(h_done, 1)
                        if m == 3 and not (last and s == 1):
                            rest_of_x(2 * i + s + 1, (s + 1) % 2)
                        if m in (2, 4) and not (first and s == 0):
                            add(2 * i + s - 1, (s + 1) % 2, m // 2 - 1)
                        dve.wait_ge(h_hi_done, j + 1)
                        dve.tensor_tensor(h_lo[:, third, :], h[:, par, :], h_hi[:, third, :].bitcast(F32),
                                          ALU.subtract).then_inc(h_lo_done, 1)
                        if first and j < TOPK // 8:
                            choose_keys(j)
                        if first and j == TOPK // 8:
                            key_row_numbers()
                if first:
                    put_key_rows()

            supertiles(dve, body)
            for hf in range(2):
                add(NS - 1, 1, hf)

        @block.tensor
        def _(pe):
            def up(i, s, m, first):
                t = 2 * i + s
                j = t * MC + m
                if m == 0:
                    pe.wait_ge(x_lo_done, t + 1)
                wait(pe, h_done, j - 1)
                for bank, w, n in ((b_g, wg, 1), (b_u, wu, 2)):
                    if first and j == 0:
                        pe.wait_ge(weights_done, n)
                    for x_part in (x_hi, x_lo):
                        for k in range(KC):
                            op = pe.matmul(bank[m % 2][:, :], w[:, k, m * P:(m + 1) * P], x_part[:, s, k, :],
                                           start=(x_part is x_hi and k == 0), stop=(x_part is x_lo and k == KC - 1))
                op.then_inc(up_done, 1)

            def down(t, s, m):
                j = t * MC + m
                if m == 0:
                    wait(pe, x_done, 2 * (t - 1))
                pe.wait_ge(h_lo_done, j + 1)
                for hf in range(2):
                    for q in (2 * hf, 2 * hf + 1):
                        for part in (h_hi, h_lo):
                            op = pe.matmul(b_y[s][hf][:, (q % 2) * D:(q % 2 + 1) * D],
                                           part[:, (s * MC + m) % 3, q * P:(q + 1) * P], wd[:, m, :],
                                           start=(m == 0 and q % 2 == 0 and part is h_hi),
                                           stop=(m == MC - 1 and q % 2 == 1 and part is h_lo), skip_group_check=True)
                    op.then_inc(down_done, 1)

            def body(i, first, last):
                for s in range(2):
                    for m in range(MC):
                        up(i, s, m, first)
                        if first and s == 0 and m == 2:
                            pe.wait_ge(weights_done, 3)
                        if first and s == 1 and m == MC - 1:
                            pe.wait_ge(x_done, 2)
                            pe.wait_ge(key_row_done, 1)
                            pe.transpose(b_y[0][0][:, 0:P], key_row[:, :], ident).then_inc(key_turned, 1)
                        if not first and s == 0 and m == 2:
                            pe.wait_ge(key_rows_done, 2)
                        if m >= 2:
                            down(2 * i + s, s, m - 2)
                        elif not (first and s == 0):
                            down(2 * i + s - 1, (s + 1) % 2, m + MC - 2)

            supertiles(pe, body)
            for m in (MC - 2, MC - 1):
                down(NS - 1, 1, m)


def layer1_attention(nc, g, ins, out):
    with ExitStack() as ctx:
        def sb(name, shape, dt=F32):
            return ctx.enter_context(nc.sbuf_tensor(name, shape, dt))

        def sem(name):
            return ctx.enter_context(nc.semaphore(name))

        cst, x_all, xnT, keys = g["cst"], g["x_all"], g["xnT_all"], g["keys"]
        wq = sb("wq1_sb", [P, KC, D])
        wo = sb("wo1_sb", [P, KC, D])
        kz = sb("kz", [P, KC, 4, 32])
        kT = sb("kT1", [P, KC, P])
        kbd = sb("kbd", [P, 2, KC, 4, P])
        vb = sb("vb", [P, 2, 8, 34])
        qT = sb("qT1", [P, 2, KC, 512])
        smax = sb("smax", [P, 2, H])
        s_sb = sb("s_sb", [P, 2, H, TOPK])
        p_sb = sb("p_sb", [P, 2, H, TOPK])
        pT = sb("pT", [P, 2, 8, P])
        rden = sb("rden", [P, 2, H])
        att = sb("att", [P, 2, D])
        attT = sb("attT", [P, 2, KC, P])
        b_s, b_p, b_q, b_o, b_w = g["banks"][0:2], g["banks"][2:4], g["banks"][4], g["banks"][5], g["banks"][6]
        b_k = g["banks"][7]

        w_loaded = sem("w2_loaded")
        zero_done = sem("zero_done")
        kz_done = sem("kz_done")
        k_turned = sem("k_turned")
        kT_done = sem("kT_done")
        kbd_done = sem("kbd_done")
        vb_done = sem("vb_done")
        qp_done = sem("q1p_done")
        qT_done = sem("q1T_done")
        s_done = sem("s1_done")
        sub_done = sem("sub_done")
        exp_done = sem("exp_done")
        p_turned = sem("p_turned")
        pT_done = sem("pT_done")
        av_done = sem("av_done")
        att_done = sem("att_done")
        att_turned = sem("att_turned")
        attT_done = sem("attT_done")
        wo_done = sem("wo_done")
        out_done = sem("out_done")
        stored = sem("stored")
        rec_done = sem("rec_done")
        fstep = sem("fstep")
        block = ctx.enter_context(nc.Block())
        ident = cst[:, _C["ident"][0]:_C["ident"][1]]
        low = cst[:, _C["lowkeys"][0]:_C["lowkeys"][1]]
        high = cst[:, _C["highkeys"][0]:_C["highkeys"][1]]
        out_v = out.rearrange("b (c p) d -> (b c) p d", p=P)

        def pairs_of_batches(eng, body):
            body(0, True, False)
            with eng.Fori(1, BATCH // 2 - 1) as i:
                body(i, False, False)
            body(BATCH // 2 - 1, False, True)


        @block.sync
        def _(sp):
            for dst, src in ((wq, "wq1"), (wo, "wo1")):
                sp.dma_start(dst[:, :, :], ins[src].rearrange("(k p) n -> p k n", p=P)).then_inc(w_loaded, 16)

            def body(i, first, last):
                for c in range(2 * BT):
                    n = i * (2 * BT) + c
                    sp.wait_ge(out_done, n + 1)
                    sp.dma_start(out_v[n], x_all[:, n, :]).then_inc(stored, 16)

            pairs_of_batches(sp, body)
            sp.wait_ge(stored, 16 * NT)

        @block.gpsimd
        def _(pool):
            pool.memset(kbd[:, :, :, :, :], 0.0)
            pool.memset(vb[:, :, :, :], 0.0).then_inc(zero_done, 1)
            pool.wait_ge(zero_done, 1)
            for par in range(2):
                pool.tensor_scalar(vb[:, par, :, 16], vb[:, par, :, 16], low, None, ALU.add)
                pool.tensor_scalar(vb[:, par, :, 33], vb[:, par, :, 33], high, None, ALU.add)

            def body(i, first, last):
                for par in range(2):
                    b = 2 * i + par
                    kv = keys[:, bass.ds(b * 8, 8), :]
                    wait(pool, k_turned, b)
                    k_in = kv[:, :, 0:16].rearrange("p (k a) e -> p k a e", k=KC)
                    pool.tensor_tensor(kz[:, :, :, 0:16], k_in, low.unsqueeze(2).unsqueeze(3).broadcast_to(k_in.shape),
                                       ALU.mult)
                    pool.tensor_tensor(kz[:, :, :, 16:32], k_in,
                                       high.unsqueeze(2).unsqueeze(3).broadcast_to(k_in.shape),
                                       ALU.mult).then_inc(kz_done, 1)
                    wait(pool, av_done, (b - 1) * BT)
                    v_in = kv[:, :, 16:32]
                    pool.tensor_tensor(vb[:, par, :, 0:16], v_in, low.unsqueeze(2).broadcast_to(v_in.shape), ALU.mult)
                    pool.tensor_tensor(vb[:, par, :, 17:33], v_in, high.unsqueeze(2).broadcast_to(v_in.shape), ALU.mult)\
                        .then_inc(vb_done, 1)

            pairs_of_batches(pool, body)

        @block.scalar
        def _(act):
            def put_kT(b):
                act.wait_ge(k_turned, b + 1)
                wait(act, kbd_done, b)
                act.copy(kT[:, :, :], b_k[:, 0:256].rearrange("p (k t) -> p k t", k=KC)).then_inc(kT_done, 1)

            def put_q(q, par, k):
                act.wait_ge(qp_done, 2 * q + k + 1)
                act.activation(qT[:, par, k, :], b_q[:, :], ACT.Copy, scale=HD ** -0.5).then_inc(qT_done, 1)

            def exps(n, par):
                act.wait_ge(sub_done, 2 * n + 2)
                wait(act, p_turned, 2 * (n - 1))
                act.activation(p_sb[:, par, :, :], s_sb[:, par, :, :], ACT.Exp).then_inc(exp_done, 1)

            def put_pT(n, par):
                for hf in range(2):
                    act.wait_ge(p_turned, 2 * n + hf + 1)
                    wait(act, av_done, n - 1)
                    act.copy(pT[:, par, 4 * hf:4 * hf + 4, :], b_p[hf][:, :].rearrange("p (a t) -> p a t", a=4))\
                       .then_inc(pT_done, 1)

            def put_attT(n, par):
                act.wait_ge(att_turned, n + 1)
                wait(act, wo_done, n - 1)
                act.copy(attT[:, par, :, :], b_k[:, 256:512].rearrange("p (k t) -> p k t", k=KC))\
                   .then_inc(attT_done, 1)

            put_kT(0)
            for k in range(KC):
                put_q(0, 0, k)
            exps(0, 0)

            def body(i, first, last):
                for c in range(2 * BT):
                    n = i * (2 * BT) + c
                    if c % BT == ST and not (last and c == BT + ST):
                        put_kT(2 * i + c // BT + 1)
                    if c % ST < KC and not (last and c >= 2 * BT - ST):
                        put_q(4 * i + c // ST + 1, (c // ST + 1) % 2, c % ST)
                    put_pT(n, c % 2)
                    if not (last and c == 2 * BT - 1):
                        exps(n + 1, (c + 1) % 2)
                    if not (first and c < 2):
                        put_attT(n - 2, c % 2)

            pairs_of_batches(act, body)
            put_attT(NT - 2, 0)
            put_attT(NT - 1, 1)

        @block.vector
        def _(dve):
            dve.wait_ge(zero_done, 1)

            def spread_keys(b, par):
                dve.wait_ge(kT_done, b + 1)
                wait(dve, s_done, 2 * BT * (b - 1))
                for pr in range(4):
                    r = slice(32 * pr, 32 * pr + 32)
                    op = dve.tensor_copy(kbd[r, par, :, pr, :], kT[r, :, :])
                op.then_inc(kbd_done, 1)

            def subtract_max(n, par, k):
                heads = slice(8 * k, 8 * k + 8)
                sc = b_s[k][:, :].rearrange("p (h j) -> p h j", j=TOPK)
                step = Chain(dve, fstep, 2 * n + k)
                dve.wait_ge(s_done, 2 * n + k + 1)
                step.mark(dve.tensor_reduce(smax[:, par, heads], sc, AX_X, ALU.max))
                step.wait()
                wait(dve, exp_done, n - 1)
                dve.tensor_tensor(s_sb[:, par, heads, :], sc, bcast(smax[:, par, heads], 2, TOPK),
                                  ALU.subtract).then_inc(sub_done, 1)

            def normalise(n, par):
                dve.wait_ge(av_done, n + 1)
                wait(dve, att_turned, n - 1)
                o = b_o[:, 0:272].rearrange("p (a x e) -> p a x e", a=8, x=2)
                dve.reciprocal(rden[:, par, :].rearrange("p (a x) -> p a x", x=2), o[:, :, :, 16]).then_inc(rec_done, 1)
                dve.wait_ge(rec_done, n + 1)
                dve.tensor_tensor(att[:, par, :].rearrange("p (a x e) -> p a x e", a=8, x=2), o[:, :, :, 0:16],
                                  bcast(rden[:, par, :].rearrange("p (a x) -> p a x", x=2), 3, 16),
                                  ALU.mult).then_inc(att_done, 1)

            def residual(n):
                dve.wait_ge(wo_done, n + 1)
                dve.tensor_tensor(x_all[:, n, :], x_all[:, n, :], b_w[:, 0:256], ALU.add).then_inc(out_done, 1)

            spread_keys(0, 0)
            for k in range(2):
                subtract_max(0, 0, k)

            def body(i, first, last):
                for c in range(2 * BT):
                    n = i * (2 * BT) + c
                    if c % BT == ST and not (last and c == BT + ST):
                        spread_keys(2 * i + c // BT + 1, (c // BT + 1) % 2)
                    if not (last and c == 2 * BT - 1):
                        for k in range(2):
                            subtract_max(n + 1, (c + 1) % 2, k)
                    if not (first and c == 0):
                        normalise(n - 1, (c + 1) % 2)
                    if not (first and c < 3):
                        residual(n - 3)

            pairs_of_batches(dve, body)
            normalise(NT - 1, 1)
            for n in range(NT - 3, NT):
                residual(n)

        @block.tensor
        def _(pe):
            def turn_keys(b):
                pe.wait_ge(kz_done, b + 1)
                wait(pe, kT_done, b)
                for k in range(KC):
                    op = pe.transpose(b_k[:, k * P:(k + 1) * P], kz[:, k, :, :], ident)
                op.then_inc(k_turned, 1)

            def project_q(q, k):
                wait(pe, qT_done, 2 * q + k)
                for kc in range(KC):
                    op = pe.matmul(b_q[:, :], wq[:, kc, k * P:(k + 1) * P], xnT[:, kc, bass.ds(q * 512, 512)],
                                   start=(kc == 0), stop=(kc == KC - 1))
                op.then_inc(qp_done, 1)

            def scores(n, c, bpar, q):
                if c % ST == 0:
                    pe.wait_ge(qT_done, 2 * q + 2)
                for k in range(KC):
                    wait(pe, sub_done, 2 * (n - 1) + k + 1)
                    pe.matmul(b_s[k][:, :], qT[:, c // ST % 2, k, (c % ST) * P:(c % ST + 1) * P],
                              kbd[:, bpar, k, :, :], start=True, stop=True).then_inc(s_done, 1)

            def turn_p(n, par):
                pe.wait_ge(exp_done, n + 1)
                for hf in range(2):
                    wait(pe, pT_done, 2 * (n - 1) + hf + 1)
                    for a in range(4):
                        h = 8 * hf + 2 * a
                        op = pe.transpose(b_p[hf][:, a * P:(a + 1) * P], p_sb[:, par, h:h + 2, :], ident)
                    op.then_inc(p_turned, 1)

            def attend(n, par, bpar):
                wait(pe, att_done, n)
                for hf in range(2):
                    pe.wait_ge(pT_done, 2 * n + hf + 1)
                    for a in range(4 * hf, 4 * hf + 4):
                        op = pe.matmul(b_o[:, 34 * a:34 * a + 34], pT[:, par, a, :], vb[:, bpar, a, :], start=True,
                                       stop=True)
                op.then_inc(av_done, 1)

            def turn_att(n, par):
                pe.wait_ge(att_done, n + 1)
                wait(pe, attT_done, n)
                for k in range(KC):
                    op = pe.transpose(b_k[:, 256 + k * P:256 + (k + 1) * P], att[:, par, k * P:(k + 1) * P], ident)
                op.then_inc(att_turned, 1)

            def output(n, par):
                pe.wait_ge(attT_done, n + 1)
                wait(pe, out_done, n)
                for k in range(KC):
                    op = pe.matmul(b_w[:, 0:256], attT[:, par, k, :], wo[:, k, :], start=(k == 0), stop=(k == KC - 1))
                op.then_inc(wo_done, 1)

            pe.wait_ge(w_loaded, 32)
            turn_keys(0)
            for k in range(KC):
                project_q(0, k)
            pe.wait_ge(kbd_done, 1)
            scores(0, 0, 0, 0)

            def body(i, first, last):
                for c in range(2 * BT):
                    n = i * (2 * BT) + c
                    if c % BT == ST and not (last and c == BT + ST):
                        pe.wait_ge(attT_done, n - 2)
                        turn_keys(2 * i + c // BT + 1)
                    if c % ST < KC and not (last and c >= 2 * BT - ST):
                        project_q(4 * i + c // ST + 1, c % ST)
                    if not (last and c == 2 * BT - 1):
                        d = (c + 1) % (2 * BT)
                        if d % BT == 0:
                            pe.wait_ge(kbd_done, 2 * i + (c + 1) // BT + 1)
                        scores(n + 1, d, d // BT, 4 * i + (c + 1) // ST)
                    turn_p(n, c % 2)
                    if not (first and c == 0):
                        attend(n - 1, (c + 1) % 2, (c + 2 * BT - 1) % (2 * BT) // BT)
                    if c % BT == 0:
                        pe.wait_ge(vb_done, 2 * i + c // BT + 1)
                    if not (first and c < 3):
                        output(n - 3, (c + 1) % 2)
                    if c % BT == ST and not (last and c == BT + ST):
                        pe.wait_ge(kT_done, 2 * i + c // BT + 2)
                    if not (first and c < 2):
                        turn_att(n - 2, c % 2)

            pairs_of_batches(pe, body)
            attend(NT - 1, 1, 1)
            output(NT - 3, 1)
            turn_att(NT - 2, 0)
            output(NT - 2, 0)
            turn_att(NT - 1, 1)
            output(NT - 1, 1)


def layers(nc, ins, out):
    with ExitStack() as ctx:
        def sb(name, shape, dt=F32):
            return ctx.enter_context(nc.sbuf_tensor(name, shape, dt))

        g = {"cst": sb("csts", [P, CW]), "x_all": sb("x_all", [P, NT, D]), "slot_rows": sb("slot_rows", [P, 2 * NE], I32),
             "ln": {"ve": sb("ln_ve", [P, BT]), "r": sb("ln_r", [P, BT]), "t": sb("ln_t", [P, BT]),
                    "st": sb("ln_st", [P, BT, 6]), "mv": sb("ln_mv", [P, BT, 2]), "rstd": sb("ln_rstd", [P, NT]),
                    "nmr": sb("ln_nmr", [P, NT])},
             "banks": [ctx.enter_context(nc.psum_tensor(f"bank{i}", [P, 512], F32)) for i in range(8)]}
        dram = {"xrows": nc.dram_tensor("xrows", (ROWS, XW), F32).ap(),
                "x1": nc.dram_tensor("x1_sum", (ROWS, D), F32).ap(),
                "slots": nc.dram_tensor("slot_table", (NE * CAP,), F32).ap(),
                "kvrows": nc.dram_tensor("kvrows", (TOKENS * H, 2 * HD), F32).ap(),
                "scores": nc.dram_tensor("key_scores", (BATCH * H, SEQ), F32).ap()}
        with ExitStack() as c0:
            g["place"] = c0.enter_context(nc.sbuf_tensor("place", [P, NT, NE], F32))
            layer0_dense(nc, g, ins, dram)
            expert_slots(nc, g, dram)
            routed_experts(nc, g, ins, dram)
        g["xnT_all"] = sb("xnT_all", [P, KC, TOKENS])
        layer1_project(nc, g, ins, dram)
        g["keys"] = sb("keys", [P, NPAIR, 2 * HD])
        layer1_ffn_and_keys(nc, g, ins, dram)
        layer1_attention(nc, g, ins, out)


def kernel(**inputs):
    import concourse.bacc as bacc
    from concourse.bass_utils import run_bass_kernel_spmd

    a = {k: np.asarray(v) for k, v in inputs.items()}
    qk_w, qk_b = a["L0_attn_Wqk_w"], a["L0_attn_Wqk_b"]
    columns = [qk_w[D:], a["L0_attn_Wv_w"], qk_w[:D], a["L0_attn_Wn_w"], a["L0_ffn_gate_w"]]
    biases = [qk_b[D:], a["L0_attn_Wv_b"], qk_b[:D], a["L0_attn_Wn_b"], np.zeros(NE, np.float32)]
    arrays = {
        "x": a["L0_attn_x"],
        "cst": shape_constants(),
        "wproj": np.concatenate(columns).T,
        "bproj": np.tile(np.concatenate(biases), (P, 1)),
        "wo": a["L0_attn_Wo_w"].T,
        "bo": np.tile(a["L0_attn_Wo_b"], (P, 1)),
        "wsu": a["L0_ffn_shared_w_gate_up"],
        "wsd": a["L0_ffn_shared_w_down"],
        "wup": a["L0_ffn_w_gate_up"],
        "wdn": a["L0_ffn_w_down"],
        "wkv1": np.concatenate([a["L1_attn_Wk"], a["L1_attn_Wv"]]).T,
        "wsc": np.tile(a["L1_attn_w_score"], (P, 1)),
        "wq1": a["L1_attn_Wq"].T,
        "wo1": a["L1_attn_Wo"].T,
        "wg1": a["L1_ffn_w_gate"].T,
        "wu1": a["L1_ffn_w_up"].T,
        "wd1": a["L1_ffn_w_down"].T,
    }
    nc = bacc.Bacc("TRN2", target_bir_lowering=False, num_devices=1)
    feed, ins = {}, {}
    for name, v in arrays.items():
        v = np.ascontiguousarray(v)
        feed["in_" + name] = v
        ins[name] = nc.dram_tensor("in_" + name, v.shape, mybir.dt.from_np(v.dtype), kind="ExternalInput").ap()
    out = nc.dram_tensor("out", (BATCH, SEQ, D), F32, kind="ExternalOutput").ap()
    layers(nc, ins, out)
    r = run_bass_kernel_spmd(nc, [feed], core_ids=[0])
    return r.results[0]["out"]
```

```python
from contextlib import ExitStack

import numpy as np

import concourse.bass as bass
from concourse import mybir

ALU = mybir.AluOpType
ACT = mybir.ActivationFunctionType
AX_X = mybir.AxisListType.X
F32 = mybir.dt.float32
BF16 = mybir.dt.bfloat16
F32R = mybir.dt.float32r
I32 = mybir.dt.int32

P = 128
BATCH, SEQ, D = 8, 1024, 256
TOKENS = BATCH * SEQ
NT = TOKENS // P
BT = SEQ // P
KC = D // P
H, HD = 16, 16
NE, TOPE, CAP = 32, 4, 256
EPS = 1e-5
BIG = 3.0e38

PK, PV, PQ, PN, PL, PW = 0, 256, 512, 768, 784, 816
XW = D + NE
DUMP = TOKENS
ROWS = TOKENS + P

_C = {}
_w = 0
for _name, _n in (("ident", P), ("causal", P), ("strict", P), ("block", P), 
                  ("part", 1), ("dump", 1), ("tile1", NT), ("iota16", 16), ("ediag", 8), ("eown", 8), ("lowkeys", 1),
                  ("highkeys", 1), ("keybase", 1)):
    _C[_name] = (_w, _w + _n)
    _w += _n
CW = _w


def shape_constants():
    c = np.zeros((P, CW), np.float32)
    i, j = np.arange(P)[:, None], np.arange(P)[None, :]

    def put(name, v):
        a, b = _C[name]
        c[:, a:b] = v

    put("ident", i == j)
    put("causal", i <= j)
    put("strict", i < j)
    put("block", i // HD == j // HD)
    put("part", i)
    put("dump", DUMP + i + P)
    put("tile1", np.arange(NT)[None, :] + 1)
    put("iota16", np.arange(16)[None, :])
    put("ediag", i // 16 == np.arange(8)[None, :])
    put("eown", i % 8 == np.arange(8)[None, :])
    put("lowkeys", i < 64)
    put("highkeys", i >= 64)
    put("keybase", i // H * (SEQ * H) + i % H)
    return c


class Chain:

    def __init__(self, eng, sem, base=0):
        self.eng, self.sem, self.base, self.k = eng, sem, base, 0

    def mark(self, ins):
        self.k += 1
        ins.then_inc(self.sem, 1)
        return self.k

    def wait(self, k=None):
        self.eng.wait_ge(self.sem, self.base + (self.k if k is None else k))


LN_MARKS = 15


def tile_stats(dve, x_all, ln, tile0, k):
    return dve.bn_stats(ln["st"][:, k, :], x_all[:, tile0 + k, :])


def layernorm_seed(dve, step, x_all, ln, tile0, n, begun=0):
    ve, r, t = ln["ve"][:, 0:n], ln["r"][:, 0:n], ln["t"][:, 0:n]
    for k in range(begun, n):
        last = tile_stats(dve, x_all, ln, tile0, k)
    step.mark(last)
    step.wait()
    step.mark(dve.memset(ve, EPS))
    for k in range(n):
        last = dve.bn_aggr(ln["mv"][:, k, :], ln["st"][:, k, :])
    step.mark(last)
    step.wait()
    step.mark(dve.tensor_tensor(ve, ve, ln["mv"][:, 0:n, 1], ALU.add))
    step.wait()
    step.mark(dve.tensor_scalar(t.bitcast(I32), ve.bitcast(I32), 1, None, ALU.arith_shift_right))
    step.wait()
    step.mark(dve.tensor_scalar(r.bitcast(I32), t.bitcast(I32), -1, 0x5F3759DF, ALU.mult, ALU.add))


def layernorm_refine(dve, step, ln, n, dst):
    ve, r, t = ln["ve"][:, 0:n], ln["r"][:, 0:n], ln["t"][:, 0:n]
    step.wait()
    step.mark(dve.tensor_tensor(t, r, r, ALU.mult))
    step.wait()
    step.mark(dve.scalar_tensor_tensor(out=t, in0=t, scalar=-0.5, in1=ve, op0=ALU.mult, op1=ALU.mult))
    step.wait()
    step.mark(dve.scalar_tensor_tensor(out=dst, in0=t, scalar=1.5, in1=r, op0=ALU.add, op1=ALU.mult))


def layernorm_finish(dve, step, ln, tile0, n):
    layernorm_refine(dve, step, ln, n, ln["rstd"][:, bass.ds(tile0, n)])
    step.wait()
    return dve.scalar_tensor_tensor(out=ln["nmr"][:, bass.ds(tile0, n)], in0=ln["mv"][:, 0:n, 0], scalar=-1.0,
                                    in1=ln["rstd"][:, bass.ds(tile0, n)], op0=ALU.mult, op1=ALU.mult)


def layernorm_stats(dve, step, x_all, ln, tile0, n):
    layernorm_seed(dve, step, x_all, ln, tile0, n)
    for _ in range(2):
        layernorm_refine(dve, step, ln, n, ln["r"][:, 0:n])
    return layernorm_finish(dve, step, ln, tile0, n)


def next_layernorm(dve, step, x_all, ln, tile0, c, done):
    if c < BT // 2:
        for k in range(2 * c, min(2 * c + 2, BT - 1)):
            tile_stats(dve, x_all, ln, tile0, k)
    if c == 3:
        layernorm_seed(dve, step, x_all, ln, tile0, BT, BT - 1)
    if c == 4:
        for _ in range(2):
            layernorm_refine(dve, step, ln, BT, ln["r"][:, 0:BT])
    if c == 5:
        layernorm_finish(dve, step, ln, tile0, BT).then_inc(done, 1)


def wait(eng, sem, value):
    if not isinstance(value, int) or value > 0:
        eng.wait_ge(sem, value)


def bcast(ap, axis, n):
    return ap.unsqueeze(axis).broadcast_to([*ap.shape[:axis], n, *ap.shape[axis:]])


def product_by_parts(pe, out, x_parts, w_parts, rest_done=None, count=0):
    passes = ((0, 0), (0, 1), (1, 0))
    for i, (a, b) in enumerate(passes):
        if a == 1 and rest_done is not None:
            pe.wait_ge(rest_done, count)
        for k in range(KC):
            op = pe.matmul(out, x_parts[a](k), w_parts[b](k), start=(i == 0 and k == 0),
                           stop=(i == len(passes) - 1 and k == KC - 1))
    return op


def layer0_dense(nc, g, ins, dram):
    with ExitStack() as ctx:
        def sb(name, shape, dt=F32):
            return ctx.enter_context(nc.sbuf_tensor(name, shape, dt))

        def sem(name):
            return ctx.enter_context(nc.semaphore(name))

        cst, x_all, ln, place = g["cst"], g["x_all"], g["ln"], g["place"]
        wproj = sb("wproj", [P, KC, PW])
        wproj_hi = sb("wproj_hi", [P, KC, PW], F32R)
        wproj_lo = sb("wproj_lo", [P, KC, PW], F32R)
        bproj = sb("bproj", [P, PW])
        wo = sb("wo", [P, KC, D])
        bo = sb("bo", [P, D])
        wsu = sb("wsu", [P, KC, D])
        wsd = sb("wsd", [P, D])
        xn = sb("xn", [P, 2, XW])
        xnT = sb("xnT", [P, 2, KC, P])
        xnT_hi = sb("xnT_hi", [P, 2, KC, P], F32R)
        xnT_lo = sb("xnT_lo", [P, 2, KC, P], F32R)
        k_sb = sb("k_sb", [P, 2, D])
        vz = sb("vz", [P, 2, H // 2, 64])
        q_in = sb("q_in", [P, 2, 308])
        qs = sb("qs", [P, 2, D])
        qkT = sb("qkT", [P, 2, 4, P])
        qbd = sb("qbd", [P, 2, KC, 8, P])
        at = sb("at", [P, 2, H, P])
        sbd = sb("sbd", [P, 2, KC, P])
        oT = sb("oT", [P, 2, KC, P])
        hT = sb("hT", [P, 2, P])
        th = sb("th", [P, P])
        hg = sb("hg", [P, P])
        nexp = sb("nexp", [P, H])
        elog = sb("elog", [P, NE])
        ewm = sb("ewm", [P, NE])
        top8 = sb("top8", [P, 8])
        negmax = sb("negmax", [P, 1])
        rep = sb("rep", [P, NE + 4])
        ssum = sb("ssum", [P, 1])
        rsum = sb("rsum", [P, 1])
        far = sb("far", [P, NE])
        maskb = sb("maskb", [P, 2, NE], BF16)
        msum = sb("msum", [P, 8, NE], BF16)
        strictb = sb("strictb", [P, P], BF16)
        onesb = sb("onesb", [P, P], BF16)
        zrow = sb("zrow", [P, XW])
        b_tg, b_kv, b_q, b_t2, b_a0, b_a1, b_o, b_s = g["banks"]
        b_a = (b_a0, b_a1)

        w_loaded = sem("w_loaded")
        x_loaded = sem("x_loaded")
        consts_ready = sem("consts_ready")
        zeros_stored = sem("zeros_stored")
        ln_done = sem("ln_done")
        xn_done = sem("xn_done")
        xn_stored = [sem("xn_stored0"), sem("xn_stored1")]
        x1_stored = sem("x1_stored")
        xb_done = sem("xb_done")
        t1_done = sem("t1_done")
        xnT_done = sem("xnT_done")
        xnT_lo_done = sem("xnT_lo_done")
        w_hi_done = sem("w_hi_done")
        w_lo_done = sem("w_lo_done")
        kvp_done = sem("kvp_done")
        qp_done = sem("qp_done")
        kv_done = sem("kv_done")
        qin_done = sem("qin_done")
        negmax_done = sem("negmax_done")
        mask_done = sem("mask_done")
        nexp_done = sem("nexp_done")
        elog_done = sem("elog_done")
        qs_done = sem("qs_done")
        weights_done = sem("weights_done")
        t2_done = sem("t2_done")
        qkT_done = sem("qkT_done")
        spread_done = sem("spread_done")
        s_done = sem("s_done")
        sbd_done = sem("sbd_done")
        a_done = sem("a_done")
        am_done = sem("am_done")
        gu_done = sem("gu_done")
        tanh_done = sem("tanh_done")
        h_done = sem("h_done")
        o_done = sem("o_done")
        oT_done = sem("oT_done")
        pos_done = sem("pos_done")
        place_done = sem("place_done")
        y_done = sem("y_done")
        x1_done = sem("x1_done")
        dstep = sem("dstep")
        block = ctx.enter_context(nc.Block())

        xt = ins["x"].rearrange("b (c p) d -> b p c d", p=P)
        rows_v = dram["xrows"].rearrange("(t p) w -> t p w", p=P)
        x1_v = dram["x1"].rearrange("(t p) w -> t p w", p=P)
        ident = cst[:, _C["ident"][0]:_C["ident"][1]]
        causal = cst[:, _C["causal"][0]:_C["causal"][1]]
        blockm = cst[:, _C["block"][0]:_C["block"][1]]
        headm = cst[:, _C["ediag"][0]:_C["ediag"][1]]

        def batches(eng, body):
            with eng.Fori(0, BATCH - 1) as b:
                body(b, False)
            body(BATCH - 1, True)

        def batches_peeled(eng, body):
            body(0, True, False)
            with eng.Fori(1, BATCH - 1) as b:
                body(b, False, False)
            body(BATCH - 1, False, True)

        @block.sync
        def _(sp):
            sp.dma_start(x_all[:, 0:BT, :], xt[0]).then_inc(x_loaded, 16)
            sp.dma_start(cst[:, :], ins["cst"]).then_inc(w_loaded, 16)
            for dst, src in ((wproj, "wproj"), (wo, "wo"), (wsu, "wsu")):
                sp.dma_start(dst[:, :, :], ins[src].rearrange("(k p) n -> p k n", p=P)).then_inc(w_loaded, 16)
            for dst, src in ((bproj, "bproj"), (bo, "bo"), (wsd, "wsd")):
                sp.dma_start(dst[:, :], ins[src]).then_inc(w_loaded, 16)

            def load_x(b):
                sp.wait_ge(x_loaded, 16 * b)
                sp.dma_start(x_all[:, bass.ds(b * BT, BT), :], xt[b]).then_inc(x_loaded, 16)

            load_x(1)
            sp.wait_ge(consts_ready, 1)
            sp.dma_start(rows_v[NT], zrow[:, :]).then_inc(zeros_stored, 16)
            sp.dma_start(x1_v[NT], zrow[:, 0:D]).then_inc(zeros_stored, 16)

            def store_row(m, par):
                sp.wait_ge(weights_done, m + 1)
                sp.dma_start(rows_v[m], xn[:, par, :]).then_inc(xn_stored[par], 16)

            store_row(0, 0)

            def body(b, last):
                for c in range(BT):
                    n = b * BT + c
                    if not (last and c == BT - 1):
                        store_row(n + 1, (c + 1) % 2)
                    sp.wait_ge(x1_done, n + 1)
                    sp.dma_start(x1_v[n], x_all[:, n, :]).then_inc(x1_stored, 16)

            with sp.Fori(0, BATCH - 2) as b:
                load_x(b + 2)
                body(b, False)
            for b in (BATCH - 2, BATCH - 1):
                body(b, b == BATCH - 1)
            for par in range(2):
                sp.wait_ge(xn_stored[par], 16 * NT // 2)
            sp.wait_ge(x1_stored, 16 * NT)
            sp.wait_ge(zeros_stored, 32)

        @block.gpsimd
        def _(pool):
            def spread_heads(n, par):
                pool.wait_ge(qkT_done, n + 1)
                for hf in range(KC):
                    pool.tensor_tensor(qbd[:, par, hf, :, :], bcast(qkT[:, par, hf, :], 1, 8), bcast(headm, 2, P),
                                       ALU.mult).then_inc(spread_done, 1)

            def add_out_bias(n):
                pool.wait_ge(xn_done, n + 1)
                pool.tensor_tensor(x_all[:, n, :], x_all[:, n, :], bo[:, :], ALU.add).then_inc(xb_done, 1)

            pool.wait_ge(w_loaded, 16 * 7)
            pool.wait_ge(consts_ready, 1)

            def body(b, last):
                for c in range(BT):
                    n = b * BT + c
                    add_out_bias(n)
                    spread_heads(n, c % 2)

            batches(pool, body)

        @block.scalar
        def _(act):
            def norm(k, par):
                act.activation(xn[:, par, 0:D], x_all[:, k, :], ACT.Identity, bias=ln["nmr"][:, bass.ds(k, 1)],
                               scale=ln["rstd"][:, bass.ds(k, 1)]).then_inc(xn_done, 1)

            def put_xnT(m, par):
                act.wait_ge(t1_done, m + 1)
                turned = b_tg[:, 0:256].rearrange("p (k t) -> p k t", k=KC)
                act.copy(xnT_hi[:, par, :, :], turned)
                act.copy(xnT[:, par, :, :], turned).then_inc(xnT_done, 1)

            def put_qkT(n, par):
                act.wait_ge(t2_done, n + 1)
                act.copy(qkT[:, par, :, :], b_t2[:, :].rearrange("p (k t) -> p k t", k=4)).then_inc(qkT_done, 1)

            def exps(m, par):
                act.wait_ge(qin_done, m + 1)
                act.activation(nexp[:, :], q_in[:, par, 256:272], ACT.Exp, scale=-1.0).then_inc(nexp_done, 1)
                act.wait_ge(negmax_done, m + 1)
                act.activation(elog[:, :], q_in[:, par, 272:304], ACT.Exp, bias=negmax[:, :]).then_inc(elog_done, 1)

            def gate_tanh(m):
                act.wait_ge(gu_done, m + 1)
                act.activation(th[:, :], b_tg[:, 256:384], ACT.Tanh, scale=0.5).then_inc(tanh_done, 1)

            def put_oT(n, par):
                act.wait_ge(o_done, n + 1)
                act.copy(oT[:, par, :, :], b_o[:, 0:256].rearrange("p (k t) -> p k t", k=KC)).then_inc(oT_done, 1)

            act.wait_ge(ln_done, 1)
            norm(0, 0)
            norm(1, 1)
            act.wait_ge(w_loaded, 16 * 7)
            act.copy(wproj_hi[:, :, :], wproj[:, :, :]).then_inc(w_hi_done, 1)
            put_xnT(0, 0)
            exps(0, 0)
            gate_tanh(0)

            def body(b, last):
                for c in range(BT):
                    n = b * BT + c
                    if not (last and c == BT - 1):
                        put_xnT(n + 1, (c + 1) % 2)
                    put_qkT(n, c % 2)
                    if not (last and c == BT - 1):
                        exps(n + 1, (c + 1) % 2)
                        gate_tanh(n + 1)
                    if not (last and c >= BT - 2):
                        if c == BT - 2:
                            act.wait_ge(ln_done, b + 2)
                        act.wait_ge(xn_stored[c % 2], b * (16 * BT // 2) + 16 * (c // 2 + 1))
                        act.wait_ge(t1_done, n + 1)
                        norm(n + 2, c % 2)
                    put_oT(n, c % 2)

            batches(act, body)

        @block.vector
        def _(dve):
            setup = Chain(dve, dstep)
            dve.memset(vz[:, :, :, :], 0.0)
            dve.memset(q_in[:, :, 304:308], BIG)
            dve.memset(msum[:, 0, :], 0.0)
            dve.memset(onesb[:, :], 1.0)
            dve.memset(zrow[:, :], 0.0)
            dve.wait_ge(x_loaded, 16)
            layernorm_stats(dve, setup, x_all, ln, 0, BT).then_inc(ln_done, 1)
            dve.wait_ge(w_loaded, 16 * 7)
            dve.tensor_copy(strictb[:, :], cst[:, _C["strict"][0]:_C["strict"][1]]).then_inc(am_done, 2)
            setup.mark(dve.memset(ssum[:, :], 0.0))
            setup.wait()
            dve.memset(rsum[:, :], 0.0).then_inc(consts_ready, 1)
            fixed = setup.k

            def rest_of_xnT(m, par):
                dve.wait_ge(xnT_done, m + 1)
                dve.tensor_tensor(xnT_lo[:, par, :, :], xnT[:, par, :, :], xnT_hi[:, par, :, :].bitcast(F32),
                                  ALU.subtract).then_inc(xnT_lo_done, 1)

            def project(m, par):
                dve.wait_ge(kvp_done, m + 1)
                dve.tensor_tensor(k_sb[:, par, :], b_kv[:, 0:D], bproj[:, PK:PK + D], ALU.add)
                dve.tensor_tensor(vz[:, par, :, :].rearrange("p a (x e) -> p a x e", e=HD)[:, :, 0::3, :],
                                  b_kv[:, D:2 * D].rearrange("p (a x e) -> p a x e", x=2, e=HD),
                                  bproj[:, PV:PV + D].rearrange("p (a x e) -> p a x e", x=2, e=HD),
                                  ALU.add).then_inc(kv_done, 1)
                dve.wait_ge(qp_done, m + 1)
                dve.tensor_tensor(q_in[:, par, 0:304], b_q[:, 0:304], bproj[:, PQ:PW], ALU.add).then_inc(qin_done, 1)

            def route(m, par, cm, step):
                logits = q_in[:, par, 272:308]
                step.mark(dve.max(top8[:, :], logits))
                step.wait()
                dve.tensor_scalar(negmax[:, :], top8[:, 4:5], -1.0, None, ALU.mult).then_inc(negmax_done, 1)
                step.mark(dve.match_replace(rep[:, :], top8[:, :], logits, -BIG))
                step.wait()
                step.mark(dve.tensor_scalar(maskb[:, par, :], rep[:, 0:NE], -1e38, None, ALU.is_lt))
                dve.tensor_scalar(far[:, :], rep[:, 0:NE], -1e38, 1024.0, ALU.is_ge, ALU.mult)
                step.wait()
                dve.tensor_tensor(msum[:, (cm + 1) % 8, :], msum[:, cm, :], maskb[:, par, :],
                                  ALU.add).then_inc(mask_done, 1)
                dve.wait_ge(nexp_done, m + 1)
                dve.tensor_tensor(qs[:, par, :].rearrange("p (h e) -> p h e", h=H),
                                  q_in[:, par, 0:D].rearrange("p (h e) -> p h e", h=H),
                                  bcast(nexp[:, :], 2, HD), ALU.mult).then_inc(qs_done, 1)

            def weigh(m, par, step):
                dve.wait_ge(elog_done, m + 1)
                step.mark(dve.tensor_tensor(ewm[:, :], elog[:, :], maskb[:, par, :], ALU.mult))
                step.wait()
                step.mark(dve.tensor_reduce(ssum[:, :], ewm[:, :], AX_X, ALU.add))
                step.wait()
                step.mark(dve.reciprocal(rsum[:, :], ssum[:, :]))
                step.wait()
                dve.tensor_scalar(xn[:, par, D:XW], ewm[:, :], rsum[:, :], None, ALU.mult).then_inc(weights_done, 1)

            def shared_act(m, par, step):
                dve.wait_ge(tanh_done, m + 1)
                step.mark(dve.scalar_tensor_tensor(out=hg[:, :], in0=th[:, :], scalar=1.0, in1=b_tg[:, 256:384],
                                                   op0=ALU.add, op1=ALU.mult))
                step.wait()
                dve.scalar_tensor_tensor(out=hT[:, par, :], in0=hg[:, :], scalar=0.5, in1=b_tg[:, 384:512],
                                         op0=ALU.mult, op1=ALU.mult).then_inc(h_done, 1)

            def places(m):
                dve.wait_ge(pos_done, m + 1)
                dve.tensor_tensor(place[:, m, :], b_q[:, 304:336], far[:, :], ALU.add).then_inc(place_done, 1)

            def state(s, nxt):
                dve.wait_ge(s_done, s)
                dve.tensor_tensor(sbd[:, nxt, :, :], b_s[:, 0:256].rearrange("p (k t) -> p k t", k=KC),
                                  bcast(blockm, 1, KC), ALU.mult).then_inc(sbd_done, 1)

            def mask_scores(n, par, j):
                dve.wait_ge(a_done, 4 * n + j + 1)
                dve.tensor_tensor(at[:, par, 4 * j:4 * j + 4, :], b_a[j % 2][:, :].rearrange("p (h t) -> p h t", h=4),
                                  bcast(causal, 1, 4), ALU.mult).then_inc(am_done, 1)

            def residual(n):
                dve.wait_ge(xb_done, n + 1)
                dve.wait_ge(y_done, n + 1)
                dve.tensor_tensor(x_all[:, n, :], x_all[:, n, :], b_o[:, 256:512], ALU.add).then_inc(x1_done, 1)

            first = Chain(dve, dstep, fixed)
            dve.wait_ge(w_hi_done, 1)
            dve.tensor_tensor(wproj_lo[:, :, :], wproj[:, :, :], wproj_hi[:, :, :].bitcast(F32),
                              ALU.subtract).then_inc(w_lo_done, 1)
            rest_of_xnT(0, 0)
            project(0, 0)
            dve.wait_ge(qin_done, 1)
            route(0, 0, 0, first)
            shared_act(0, 0, first)
            weigh(0, 0, first)
            places(0)
            fixed += first.k
            per_tile = first.k
            per_batch = per_tile * BT + LN_MARKS

            def body(b, first, last):
                step = Chain(dve, dstep, fixed + b * per_batch)
                for c in range(BT):
                    n = b * BT + c
                    more = not (last and c == BT - 1)
                    par = (c + 1) % 2
                    if more:
                        rest_of_xnT(n + 1, par)
                    if c < BT - 1:
                        state(b * (BT - 1) + c + 1, (c + 1) % 2)
                    if not (first and c == 0):
                        residual(n - 1)
                    if more:
                        project(n + 1, par)
                        dve.wait_ge(qin_done, n + 2)
                    for j in range(4):
                        mask_scores(n, c % 2, j)
                    if more:
                        route(n + 1, par, (c + 1) % 8, step)
                        shared_act(n + 1, par, step)
                        weigh(n + 1, par, step)
                        places(n + 1)
                    if not last:
                        if c == 0:
                            dve.wait_ge(x_loaded, b * 16 + 32)
                        next_layernorm(dve, step, x_all, ln, (b + 1) * BT, c, ln_done)
                assert last or step.k == per_batch

            batches_peeled(dve, body)
            residual(NT - 1)

        @block.tensor
        def _(pe):
            def transpose_norm(m, par):
                pe.wait_ge(xn_done, m + 1)
                for k in range(KC):
                    last = pe.transpose(b_tg[:, k * P:(k + 1) * P], xn[:, par, k * P:(k + 1) * P], ident)
                last.then_inc(t1_done, 1)

            def project(m, par, first):
                pe.wait_ge(xnT_done, m + 1)
                if not first:
                    pe.wait_ge(kv_done, m)
                x_parts = [lambda k, p=p: p[:, par, k, :] for p in (xnT_hi, xnT_lo)]
                for out, c0, c1, done in ((b_kv[:, :], 0, PQ, kvp_done), (b_q[:, 0:PW - PQ], PQ, PW, qp_done)):
                    if c0 > 0 and not first:
                        pe.wait_ge(place_done, m)
                    product_by_parts(pe, out, x_parts, [lambda k, p=p: p[:, k, c0:c1] for p in (wproj_hi, wproj_lo)],
                                     xnT_lo_done, m + 1).then_inc(done, 1)

            def shared_up(m, par, gu):
                for k in range(KC):
                    last = pe.matmul(b_tg[:, 256 + gu * P:256 + (gu + 1) * P], wsu[:, k, gu * P:(gu + 1) * P],
                                     xnT[:, par, k, :], start=(k == 0), stop=(k == KC - 1))
                if gu == 1:
                    last.then_inc(gu_done, 1)

            def positions(m, par, cm):
                pe.wait_ge(mask_done, m + 1)
                pe.matmul(b_q[:, 304:336], strictb[:, :], maskb[:, par, :], start=True, stop=False)
                pe.matmul(b_q[:, 304:336], onesb[:, :], msum[:, cm, :], start=False, stop=True).then_inc(pos_done, 1)

            def transpose_qk(n, par):
                pe.wait_ge(qs_done, n + 1)
                for k in range(KC):
                    pe.transpose(b_t2[:, k * P:(k + 1) * P], qs[:, par, k * P:(k + 1) * P], ident)
                for k in range(KC):
                    last = pe.transpose(b_t2[:, (2 + k) * P:(3 + k) * P], k_sb[:, par, k * P:(k + 1) * P], ident)
                last.then_inc(t2_done, 1)

            def v_pairs(par, hf):
                return vz[:, par, 4 * hf:4 * hf + 4, :].rearrange("p a (x e) -> p a x e", e=HD)[:, :, 0::3, :]

            def state(par, c):
                for k in range(KC):
                    last = pe.matmul(b_s[:, k * P:(k + 1) * P].rearrange("p (a x e) -> p a x e", x=2, e=HD),
                                     k_sb[:, par, k * P:(k + 1) * P], v_pairs(par, k),
                                     start=(c == 0 and k == 0), stop=(k == 1), skip_group_check=True)
                last.then_inc(s_done, 1)

            def head_scores(n, par):
                for j in range(4):
                    if j % 2 == 0:
                        pe.wait_ge(spread_done, 2 * n + j // 2 + 1)
                    pe.wait_ge(am_done, 4 * n + j + 1)
                    pe.matmul(b_a[j % 2][:, :], qkT[:, par, 2 + j // 2, :],
                              qbd[:, par, j // 2, 4 * (j % 2):4 * (j % 2) + 4, :], start=True,
                              stop=True).then_inc(a_done, 1)

            def attend(n, par, c):
                for hf in range(KC):
                    pe.wait_ge(am_done, 4 * n + 2 * hf + 4)
                    cols = slice(hf * P, (hf + 1) * P)
                    if c > 0:
                        pe.matmul(b_o[:, cols], sbd[:, par, hf, :], qkT[:, par, hf, :], start=True, stop=False,
                                  skip_group_check=True)
                    for eo in range(2):
                        for pr in range(4):
                            last = pe.matmul(b_o[32 * pr:32 * pr + 32, cols],
                                             vz[:, par, 4 * hf + pr, 32 * eo:32 * eo + 32],
                                             at[:, par, 8 * hf + 2 * pr + eo, :], start=(c == 0 and eo == 0),
                                             stop=(eo == 1), skip_group_check=True)
                last.then_inc(o_done, 1)

            def output(n, par):
                pe.wait_ge(oT_done, n + 1)
                for k in range(KC):
                    pe.matmul(b_o[:, 256:512], oT[:, par, k, :], wo[:, k, :], start=(k == 0), stop=False)
                pe.matmul(b_o[:, 256:512], hT[:, par, :], wsd[:, :], start=False, stop=True).then_inc(y_done, 1)

            pe.wait_ge(w_loaded, 16 * 7)
            pe.wait_ge(consts_ready, 1)
            transpose_norm(0, 0)
            pe.wait_ge(w_lo_done, 1)
            project(0, 0, True)
            for gu in range(2):
                shared_up(0, 0, gu)
            positions(0, 0, 0)

            def body(b, first, last):
                for c in range(BT):
                    n = b * BT + c
                    more = not (last and c == BT - 1)
                    par = (c + 1) % 2
                    pe.wait_ge(h_done, n + 1)
                    if more:
                        transpose_norm(n + 1, par)
                    transpose_qk(n, c % 2)
                    if c > 0:
                        pe.wait_ge(sbd_done, b * (BT - 1) + c)
                    if c < BT - 1:
                        state(c % 2, c)
                    if not (first and c == 0):
                        output(n - 1, par)
                    if more:
                        project(n + 1, par, False)
                    head_scores(n, c % 2)
                    if more:
                        for gu in range(2):
                            shared_up(n + 1, par, gu)
                    wait(pe, x1_done, n)
                    attend(n, c % 2, c)
                    if more:
                        positions(n + 1, par, (c + 1) % 8)

            batches_peeled(pe, body)
            output(NT - 1, 1)


def expert_slots(nc, g, dram):
    with ExitStack() as ctx:
        def sb(name, shape, dt=F32):
            return ctx.enter_context(nc.sbuf_tensor(name, shape, dt))

        def sem(name):
            return ctx.enter_context(nc.semaphore(name))

        cst, place, slot_rows = g["cst"], g["place"], g["slot_rows"]
        banks = g["banks"]
        place_i = sb("place_i", [P, NT, NE], I32)
        part_i = sb("part_i", [P, NT, NE], I32)
        lo = sb("lo", [P, NT, NE], BF16)
        hi = sb("hi", [P, NT, NE], BF16)
        iota_b = sb("iota_b", [P, 16, NE], BF16)
        hot_hi = sb("hot_hi", [P, 4, 4, 16, 8], BF16)
        hot_lo = sb("hot_lo", [P, 4, 16, NE], BF16)
        carry = sb("carry", [P, 4, 2, 16, NE], BF16)
        own = sb("own", [P, 4, 2, 8, 16])
        parts = sb("parts", [P, 4, 2, 16])
        table = sb("table", [P, 4, 16])
        slots_t = sb("slots_t", [2 * NE, P])
        empty = sb("empty", [P, 2 * NE])

        digits_done = sem("digits_done")
        hot_hi_done = sem("hot_hi_done")
        hot_lo_done = sem("hot_lo_done")
        part_done = sem("part_done")
        tile_done = sem("tile_done")
        slots_done = sem("slots_done")
        own_done = sem("own_done")
        table_done = sem("table_done")
        table_moved = sem("table_moved")
        turned = sem("turned")
        rows_done = sem("rows_done")
        bstep = sem("bstep")
        block = ctx.enter_context(nc.Block())

        partc = cst[:, _C["part"][0]:_C["part"][1]]
        tile1 = _C["tile1"][0]
        ediag = cst[:, _C["eown"][0]:_C["eown"][1]]
        slots_v = dram["slots"].rearrange("(p w) -> p w", p=P)
        slots_back = dram["slots"].rearrange("(f h e g l) -> f g e h l", f=2, h=8, e=8, g=4)

        def tiles(eng, body):
            body(0, True)
            with eng.Fori(1, NT // 4) as i:
                body(i, False)

        @block.vector
        def _(dve):
            step = Chain(dve, bstep)
            step.mark(dve.tensor_scalar(place_i[:, :, :], place[:, :, :], float(CAP), None, ALU.min))
            dve.tensor_copy(iota_b[:, :, :], bcast(cst[:, _C["iota16"][0]:_C["iota16"][1]], 2, NE))
            step.wait()
            step.mark(dve.tensor_scalar(part_i[:, :, :], place_i[:, :, :], 4, None, ALU.arith_shift_right))
            step.wait()
            step.mark(dve.tensor_copy(hi[:, :, :], part_i[:, :, :]))
            step.mark(dve.tensor_scalar(place_i[:, :, :], place_i[:, :, :], 15, None, ALU.bitwise_and))
            step.wait()
            dve.tensor_copy(lo[:, :, :], place_i[:, :, :]).then_inc(digits_done, 1)
            dve.wait_ge(digits_done, 1)
            fixed = step.k

            def body(i, first):
                for par in range(4):
                    t = i * 4 + par
                    wait(dve, slots_done, t - 3)
                    dve.tensor_tensor(hot_lo[:, par, :, :], bcast(lo[:, t, :], 1, 16), iota_b[:, :, :],
                                      ALU.is_equal).then_inc(hot_lo_done, 1)
                    dve.tensor_tensor(hot_hi[:, par, :, :, :], bcast(hi[:, t, :].rearrange("p (g e) -> p g e", g=4), 2, 16),
                                      bcast(iota_b[:, :, 0:8], 1, 4), ALU.is_equal).then_inc(hot_hi_done, 1)
                    dve.wait_ge(hot_lo_done, t + 1)
                    dve.tensor_scalar(carry[:, par, 0, :, :], hot_lo[:, par, :, :], partc, None,
                                      ALU.mult).then_inc(part_done, 1)

            tiles(dve, body)
            step = Chain(dve, bstep, fixed)
            dve.wait_ge(slots_done, NT)
            for gr in range(4):
                last = dve.tensor_tensor(own[:, gr, :, :, :],
                                         banks[gr][:, 0:256].rearrange("p (x e l) -> p x e l", x=2, e=8),
                                         bcast(bcast(ediag, 2, 16), 1, 2), ALU.mult)
            step.mark(last)
            step.wait()
            for gr in range(4):
                last = dve.tensor_reduce(parts[:, gr, :, :], own[:, gr, :, :, :].rearrange("p x e l -> p x l e"), AX_X,
                                         ALU.add)
            step.mark(last)
            step.wait()
            step.mark(dve.scalar_tensor_tensor(out=table[:, :, :], in0=parts[:, :, 1, :], scalar=float(P),
                                               in1=parts[:, :, 0, :], op0=ALU.mult, op1=ALU.add))
            step.wait()
            dve.tensor_scalar(table[:, :, :], table[:, :, :], float(-P), None, ALU.add).then_inc(table_done, 1)
            dve.wait_ge(turned, 1)
            step.mark(dve.tensor_scalar(empty[:, :], banks[4][:, 0:2 * NE], 0.0,
                                        cst[:, _C["dump"][0]:_C["dump"][1]], ALU.is_lt, ALU.mult))
            step.wait()
            dve.tensor_tensor(slot_rows[:, :].rearrange("p (e f) -> p f e", f=2),
                              banks[4][:, 0:2 * NE].rearrange("p (f e) -> p f e", f=2),
                              empty[:, :].rearrange("p (f e) -> p f e", f=2), ALU.add).then_inc(rows_done, 1)
            dve.wait_ge(rows_done, 1)

        @block.scalar
        def _(act):
            def body(i, first):
                for par in range(4):
                    t = i * 4 + par
                    act.wait_ge(hot_lo_done, t + 1)
                    act.activation(carry[:, par, 1, :, :], hot_lo[:, par, :, :], ACT.Copy,
                                   scale=cst[:, bass.ds(t + tile1, 1)]).then_inc(tile_done, 1)

            tiles(act, body)

        @block.tensor
        def _(pe):
            def body(i, first):
                for par in range(4):
                    t = i * 4 + par
                    pe.wait_ge(part_done, t + 1)
                    pe.wait_ge(tile_done, t + 1)
                    for gr in range(4):
                        last = pe.matmul(banks[gr][:, 0:256].rearrange("p (x e l) -> p x e l", x=2, e=8),
                                         hot_hi[:, par, gr, :, :].rearrange("p l e -> p (l e)"),
                                         carry[:, par, :, :, 8 * gr:8 * gr + 8].rearrange("p x l e -> p x e l"),
                                         start=(first and par == 0), stop=False, skip_group_check=True)
                    last.then_inc(slots_done, 1)

            tiles(pe, body)
            pe.wait_ge(table_moved, 16 * 9)
            pe.transpose(banks[4][:, 0:2 * NE], slots_t[:, :],
                         cst[0:2 * NE, _C["ident"][0]:_C["ident"][0] + 2 * NE]).then_inc(turned, 1)

        @block.sync
        def _(sp):
            sp.wait_ge(table_done, 1)
            sp.dma_start(slots_v, table[:, :, :].rearrange("p g l -> p (g l)")).then_inc(table_moved, 16)
            sp.wait_ge(table_moved, 16)
            with nc.allow_non_contiguous_dma("slot table in 64-byte runs"):
                for half in range(2):
                    for gr in range(4):
                        r = half * NE + gr * 8
                        sp.dma_start(slots_t[r:r + 8, :].rearrange("e (h l) -> e h l", h=8), slots_back[half, gr])\
                          .then_inc(table_moved, 16)


EU = 8
AHEAD = 4


def routed_experts(nc, g, ins, dram):
    with ExitStack() as ctx:
        def sb(name, shape, dt=F32):
            return ctx.enter_context(nc.sbuf_tensor(name, shape, dt))

        def sem(name):
            return ctx.enter_context(nc.semaphore(name))

        cst, slot_rows = g["cst"], g["slot_rows"]
        wup = sb("wup", [P, EU, KC, D])
        wdn = sb("wdn", [P, EU, D])
        rows_now = sb("rows_now", [P, EU, 2], I32)
        xe = sb("xe", [P, EU, 2, XW])
        xeT = sb("xeT", [P, 2, KC, 2 * P])
        silu = sb("silu", [P, 2 * P])
        hT = sb("ehT", [P, 2, 2 * P])
        ye = sb("ye", [P, EU, 2, D])
        held = sb("held", [P, 2 * EU + 1])
        held_done = sem("held_done")
        b_x, b_u, b_y = g["banks"][0:2], g["banks"][2:4], g["banks"][4:6]

        w_loaded = [sem(f"expert_w{k}") for k in range(EU)]
        x_loaded = [sem(f"expert_x{k}") for k in range(EU)]
        index_done = sem("index_done")
        turned = sem("xe_turned")
        xeT_done = sem("xeT_done")
        up_done = sem("up_done")
        silu_done = sem("silu_done")
        h_done = sem("eh_done")
        down_done = sem("down_done")
        ye_done = sem("ye_done")
        added = sem("added")
        block = ctx.enter_context(nc.Block())
        ident = cst[:, _C["ident"][0]:_C["ident"][1]]
        wup_v = ins["wup"].rearrange("e (k p) n -> e p k n", p=P)

        def experts(eng, body):
            body(0, True, False)
            with eng.Fori(1, NE // EU - 1) as i:
                body(i, False, False)
            body(NE // EU - 1, False, True)

        @block.sync
        def _(sp):
            def body(i, first, last):
                for k in range(EU):
                    e = i * EU + k
                    wait(sp, down_done, e - EU + 1)
                    sp.dma_start(wup[:, k, :, :], wup_v[e]).then_inc(w_loaded[k], 16)
                    sp.dma_start(wdn[:, k, :], ins["wdn"][e]).then_inc(w_loaded[k], 16)

            experts(sp, body)

        @block.gpsimd
        def _(pool):
            def hold(j):
                pool.tensor_tensor(held[:, j + 1:j + 2], held[:, 0:1], held[:, 0:1], ALU.add)

            pool.memset(held[:, :], 0.0).then_inc(held_done, 1)
            pool.wait_ge(held_done, 1)

            def gather(e, k):
                wait(pool, ye_done, e - EU + 1)
                pool.tensor_copy(rows_now[:, k, :], slot_rows[:, bass.ds(e * 2, 2)]).then_inc(index_done, 1)
                pool.wait_ge(index_done, e + 1)
                hold(k)
                for hf in range(2):
                    pool.indirect_dma_start(out=xe[:, k, hf, :], out_offset=None, in_=dram["xrows"],
                                            in_offset=bass.IndirectOffsetOnAxis(ap=rows_now[:, k, hf:hf + 1], axis=0),
                                            bounds_check=ROWS - 1, oob_is_err=False).then_inc(x_loaded[k], 16)

            def add(e, k):
                pool.wait_ge(ye_done, e + 1)
                wait(pool, added, 32 * e)
                hold(EU + k)
                for hf in range(2):
                    pool.indirect_dma_start(out=dram["x1"], in_=ye[:, k, hf, :], in_offset=None,
                                            out_offset=bass.IndirectOffsetOnAxis(ap=rows_now[:, k, hf:hf + 1], axis=0),
                                            bounds_check=ROWS - 1, oob_is_err=True,
                                            compute_op=ALU.add).then_inc(added, 16)

            for e in range(AHEAD):
                gather(e, e)

            def body(i, first, last):
                for k in range(EU):
                    e = i * EU + k
                    if not (last and k >= EU - AHEAD):
                        wait(pool, added, 32 * (e + AHEAD - EU + 1))
                        gather(e + AHEAD, (k + AHEAD) % EU)
                    add(e, k)

            experts(pool, body)
            pool.wait_ge(added, 32 * NE)

        @block.scalar
        def _(act):
            def body(i, first, last):
                for k in range(EU):
                    e = i * EU + k
                    par = k % 2
                    act.wait_ge(turned, e + 1)
                    wait(act, up_done, e - 1)
                    act.copy(xeT[:, par, :, :], b_x[par][:, :].rearrange("p (k t) -> p k t", k=KC))\
                       .then_inc(xeT_done, 1)
                    act.wait_ge(up_done, e + 1)
                    wait(act, h_done, e)
                    act.activation(silu[:, :], b_u[par][:, 0:256], ACT.Silu).then_inc(silu_done, 1)

            experts(act, body)

        @block.vector
        def _(dve):
            def body(i, first, last):
                for k in range(EU):
                    e = i * EU + k
                    par = k % 2
                    dve.wait_ge(silu_done, e + 1)
                    wait(dve, down_done, e - 1)
                    dve.tensor_tensor(hT[:, par, :], silu[:, :], b_u[par][:, 256:512], ALU.mult).then_inc(h_done, 1)
                    dve.wait_ge(down_done, e + 1)
                    wait(dve, added, 32 * (e - EU + 1))
                    for hf in range(2):
                        last_op = dve.tensor_scalar(ye[:, k, hf, :], b_y[par][:, hf * D:(hf + 1) * D],
                                                    xe[:, k, hf, bass.ds(e + D, 1)], None, ALU.mult)
                    last_op.then_inc(ye_done, 1)

            experts(dve, body)

        @block.tensor
        def _(pe):
            def body(i, first, last):
                def turn(j, k):
                    e = (i + j) * EU + k
                    par = k % 2
                    pe.wait_ge(x_loaded[k], (i + j) * 32 + 32)
                    wait(pe, xeT_done, e - 1)
                    for kc in range(KC):
                        for hf in range(2):
                            op = pe.transpose(b_x[par][:, (2 * kc + hf) * P:(2 * kc + hf + 1) * P],
                                              xe[:, k, hf, kc * P:(kc + 1) * P], ident)
                    op.then_inc(turned, 1)

                def up(e, k):
                    par = k % 2
                    pe.wait_ge(xeT_done, e + 1)
                    pe.wait_ge(w_loaded[k], i * 32 + 32)
                    wait(pe, h_done, e - 1)
                    for gu in range(2):
                        for kc in range(KC):
                            op = pe.matmul(b_u[par][:, gu * 256:gu * 256 + 256], wup[:, k, kc, gu * P:(gu + 1) * P],
                                           xeT[:, par, kc, :], start=(kc == 0), stop=(kc == KC - 1))
                    op.then_inc(up_done, 1)

                def down(e, k):
                    par = k % 2
                    pe.wait_ge(h_done, e + 1)
                    wait(pe, ye_done, e - 1)
                    for hf in range(2):
                        op = pe.matmul(b_y[par][:, hf * D:(hf + 1) * D], hT[:, par, hf * P:(hf + 1) * P], wdn[:, k, :],
                                       start=True, stop=True)
                    op.then_inc(down_done, 1)

                if first:
                    turn(0, 0)
                for k in range(EU):
                    e = i * EU + k
                    if k < EU - 1:
                        turn(0, k + 1)
                    elif not last:
                        turn(1, 0)
                    up(e, k)
                    down(e, k)

            experts(pe, body)


ST = 4
NS = NT // ST
HID = 768
MC = HID // P
INT_SCALE = 1.0 / 127.0
TOPK = 64
NPAIR = BATCH * H // 2


def layer1_project(nc, g, ins, dram):
    with ExitStack() as ctx:
        def sb(name, shape, dt=F32):
            return ctx.enter_context(nc.sbuf_tensor(name, shape, dt))

        def sem(name):
            return ctx.enter_context(nc.semaphore(name))

        cst, x_all, xnT, ln = g["cst"], g["x_all"], g["xnT_all"], g["ln"]
        wkv = sb("wkv", [P, KC, 2 * D])
        wsc = sb("wsc", [P, HD])
        wprod = sb("wprod", [P, KC, D])
        widx = sb("widx", [P, KC, H])
        xn = sb("xn1", [P, 2, D])
        wkv_hi = sb("wkv_hi", [P, KC, 2 * D], F32R)
        wkv_lo = sb("wkv_lo", [P, KC, 2 * D], F32R)
        widx_hi = sb("widx_hi", [P, KC, H], F32R)
        widx_lo = sb("widx_lo", [P, KC, H], F32R)
        xst_hi = sb("xst_hi", [P, 2, KC, 512], F32R)
        xst_lo = sb("xst_lo", [P, 2, KC, 512], F32R)
        kv_row = sb("kv_row", [P, 2, 2 * D])
        score = sb("score", [H, 2, 512])
        wg_int = sb("wg_int", [P, KC * HID], I32)
        keys_int = g["keys"][:, :, :].rearrange("p n e -> p (n e)").bitcast(I32)[:, 0:KC * HID]
        b_t, b_i, b_kv = g["banks"][0:2], g["banks"][2:4], g["banks"][4:8]

        w_loaded = sem("w1_loaded")
        x_loaded = sem("x1_loaded")
        ln_done = sem("ln1_done")
        widx_done = sem("widx_done")
        xn_done = sem("xn1_done")
        turned = sem("xn1_turned")
        xst_done = sem("xst_done")
        xst_lo_done = sem("xst_lo_done")
        ffn_int_loaded = sem("ffn_int_loaded")
        ffn_weights_done = sem("ffn_weights_done")
        w_hi_done = sem("w1_hi_done")
        w_lo_done = sem("w1_lo_done")
        kept = sem("xnT_kept")
        kvp_done = sem("kvp1_done")
        kv_done = sem("kv1_done")
        kv_stored = [sem("kv_stored0"), sem("kv_stored1")]
        idx_done = sem("idx_done")
        score_done = sem("score_done")
        score_stored = [sem("score_stored0"), sem("score_stored1")]
        dstep = sem("d1step")
        block = ctx.enter_context(nc.Block())
        ident = cst[:, _C["ident"][0]:_C["ident"][1]]
        x1_v = dram["x1"][0:TOKENS, :].rearrange("(b c p) d -> b p c d", p=P, c=BT)
        kv_v = dram["kvrows"].rearrange("(t p h) e -> t p (h e)", p=P, h=H)
        score_v = dram["scores"].rearrange("(b h) (s t) -> b s h t", h=H, t=512)

        def batches(eng, body):
            body(0, True, False)
            with eng.Fori(1, BATCH - 1) as b:
                body(b, False, False)
            body(BATCH - 1, False, True)

        @block.sync
        def _(sp):
            sp.dma_start(x_all[:, 0:BT, :], x1_v[0]).then_inc(x_loaded, 16)
            sp.dma_start(wkv[:, :, :], ins["wkv1"].rearrange("(k p) n -> p k n", p=P)).then_inc(w_loaded, 16)
            sp.dma_start(wsc[:, :], ins["wsc"]).then_inc(w_loaded, 16)

            def load_x(b):
                sp.wait_ge(x_loaded, 16 * b)
                sp.dma_start(x_all[:, bass.ds(b * BT, BT), :], x1_v[b]).then_inc(x_loaded, 16)

            load_x(1)

            def load_ffn(dst, name, k):
                sp.dma_start(dst.rearrange("p (k n) -> p k n", k=k), ins[name].rearrange("(k p) n -> p k n", p=P))\
                  .then_inc(ffn_int_loaded, 16)

            load_ffn(wg_int[:, :], "wg1", KC)
            load_ffn(keys_int, "wu1", KC)

            def store_score(b, s):
                sp.wait_ge(score_done, 2 * b + s + 1)
                sp.dma_start(score_v[b, s], score[:, s, :]).then_inc(score_stored[s], 16)

            def body(b, first, last, load):
                if load:
                    load_x(b + 2)
                for c in range(BT):
                    n = b * BT + c
                    sp.wait_ge(kv_done, n + 1)
                    sp.dma_start(kv_v[n], kv_row[:, c % 2, :]).then_inc(kv_stored[c % 2], 16)
                    if c == 1 and not first:
                        store_score(b - 1, 1)
                    if c == ST + 1:
                        store_score(b, 0)

            body(0, True, False, True)
            with sp.Fori(1, BATCH - 2) as b:
                body(b, False, False, True)
            sp.wait_ge(ffn_weights_done, 2)
            load_ffn(keys_int, "wd1", MC)
            for b in (BATCH - 2, BATCH - 1):
                body(b, False, b == BATCH - 1, False)
            store_score(BATCH - 1, 1)
            for par in range(2):
                sp.wait_ge(kv_stored[par], 16 * NT // 2)
                sp.wait_ge(score_stored[par], 16 * BATCH)

        @block.gpsimd
        def _(pool):
            for name, src, k, loaded in (("wg", wg_int[:, :], KC, 2), ("wu", keys_int, KC, 2), ("wd", keys_int, MC, 3)):
                pool.wait_ge(ffn_int_loaded, 16 * loaded)
                pool.tensor_copy(g[name][:, :, :], src.rearrange("p (k n) -> p k n", k=k)).then_inc(ffn_weights_done, 1)
            pool.wait_ge(ffn_weights_done, 3)

        @block.scalar
        def _(act):
            def norm(n, par):
                wait(act, turned, n - 1)
                act.activation(xn[:, par, :], x_all[:, n, :], ACT.Identity, bias=ln["nmr"][:, bass.ds(n, 1)],
                               scale=ln["rstd"][:, bass.ds(n, 1)]).then_inc(xn_done, 1)

            def put(n, c):
                act.wait_ge(turned, n + 1)
                turned_x = b_t[c % 2][:, 0:256].rearrange("p (k t) -> p k t", k=KC)
                act.copy(xst_hi[:, c // ST, :, (c % ST) * P:(c % ST + 1) * P], turned_x).then_inc(xst_done, 1)
                act.copy(xnT[:, :, bass.ds(n * P, P)], turned_x).then_inc(kept, 1)

            def put_score(b, s):
                act.wait_ge(idx_done, 2 * b + s + 1)
                wait(act, score_stored[s], 16 * b)
                act.copy(score[:, s, :], b_i[s][0:H, :]).then_inc(score_done, 1)

            act.wait_ge(w_loaded, 32)
            act.copy(wkv_hi[:, :, :], wkv[:, :, :]).then_inc(w_hi_done, 1)
            act.wait_ge(ln_done, 1)
            norm(0, 0)
            norm(1, 1)
            put(0, 0)

            def body(b, first, last):
                for c in range(BT):
                    n = b * BT + c
                    if c == 0 and not first:
                        put_score(b - 1, 1)
                    if c == ST:
                        put_score(b, 0)
                    if c == BT - 2 and not last:
                        act.wait_ge(ln_done, b + 2)
                    if not (last and c >= BT - 2):
                        norm(n + 2, c % 2)
                    if not (last and c == BT - 1):
                        put(n + 1, (c + 1) % BT)

            batches(act, body)
            put_score(BATCH - 1, 1)

        @block.vector
        def _(dve):
            step = Chain(dve, dstep)
            dve.wait_ge(x_loaded, 16)
            layernorm_stats(dve, step, x_all, ln, 0, BT).then_inc(ln_done, 1)
            dve.wait_ge(w_loaded, 32)
            dve.wait_ge(w_hi_done, 1)
            dve.tensor_tensor(wkv_lo[:, :, :], wkv[:, :, :], wkv_hi[:, :, :].bitcast(F32),
                              ALU.subtract).then_inc(w_lo_done, 1)
            step.mark(dve.tensor_tensor(wprod[:, :, :].rearrange("p k (h e) -> p k h e", e=HD),
                                        wkv[:, :, 0:D].rearrange("p k (h e) -> p k h e", e=HD),
                                        bcast(bcast(wsc[:, :], 1, H), 1, KC), ALU.mult))
            step.wait()
            step.mark(dve.tensor_reduce(widx[:, :, :], wprod[:, :, :].rearrange("p k (h e) -> p k h e", e=HD), AX_X,
                                        ALU.add))
            step.wait()
            step.mark(dve.tensor_copy(widx_hi[:, :, :], widx[:, :, :]))
            step.wait()
            dve.tensor_tensor(widx_lo[:, :, :], widx[:, :, :], widx_hi[:, :, :].bitcast(F32),
                              ALU.subtract).then_inc(widx_done, 1)
            fixed = step.k

            def rest_of_x(n, c):
                dve.wait_ge(kept, n + 1)
                cols = slice((c % ST) * P, (c % ST + 1) * P)
                dve.tensor_tensor(xst_lo[:, c // ST, :, cols], xnT[:, :, bass.ds(n * P, P)],
                                  xst_hi[:, c // ST, :, cols].bitcast(F32), ALU.subtract).then_inc(xst_lo_done, 1)

            rest_of_x(0, 0)

            def body(b, first, last):
                step = Chain(dve, dstep, fixed + b * LN_MARKS)
                for c in range(BT):
                    n = b * BT + c
                    if not (last and c == BT - 1):
                        rest_of_x(n + 1, (c + 1) % BT)
                    dve.wait_ge(kvp_done, n + 1)
                    if not (first and c < 2):
                        dve.wait_ge(kv_stored[c % 2], b * (16 * BT // 2) + 16 * (c // 2))
                    dve.tensor_copy(kv_row[:, c % 2, :].rearrange("p (h x e) -> p x h e", h=H, x=2),
                                    b_kv[c % 4][:, :].rearrange("p (x h e) -> p x h e", h=H, x=2)).then_inc(kv_done, 1)
                    if not last:
                        if c == 0:
                            dve.wait_ge(x_loaded, b * 16 + 32)
                        next_layernorm(dve, step, x_all, ln, (b + 1) * BT, c, ln_done)

            batches(dve, body)

        @block.tensor
        def _(pe):
            def turn(n, c):
                pe.wait_ge(xn_done, n + 1)
                wait(pe, kept, n - 1)
                for k in range(KC):
                    op = pe.transpose(b_t[c % 2][:, k * P:(k + 1) * P], xn[:, c % 2, k * P:(k + 1) * P], ident)
                op.then_inc(turned, 1)

            def project(n, c):
                pe.wait_ge(xst_done, n + 1)
                wait(pe, kv_done, n - 3)
                cols = slice((c % ST) * P, (c % ST + 1) * P)
                product_by_parts(pe, b_kv[c % 4][:, :],
                                 [lambda k, p=p: p[:, c // ST, k, cols] for p in (xst_hi, xst_lo)],
                                 [lambda k, p=p: p[:, k, :] for p in (wkv_hi, wkv_lo)],
                                 xst_lo_done, n + 1).then_inc(kvp_done, 1)

            def key_scores(b, s):
                pe.wait_ge(xst_lo_done, b * BT + (s + 1) * ST)
                wait(pe, score_done, 2 * b + s - 1)
                product_by_parts(pe, b_i[s][0:H, :], [lambda k, p=p: p[:, k, :] for p in (widx_hi, widx_lo)],
                                 [lambda k, p=p: p[:, s, k, :] for p in (xst_hi, xst_lo)]).then_inc(idx_done, 1)

            turn(0, 0)
            pe.wait_ge(w_lo_done, 1)

            def body(b, first, last):
                for c in range(BT):
                    n = b * BT + c
                    if c == 0 and not first:
                        key_scores(b - 1, 1)
                    if c == ST:
                        if first:
                            pe.wait_ge(widx_done, 1)
                        key_scores(b, 0)
                    if not (last and c == BT - 1):
                        turn(n + 1, c + 1)
                    project(n, c)

            batches(pe, body)
            key_scores(BATCH - 1, 1)


def layer1_ffn_and_keys(nc, g, ins, dram):
    with ExitStack() as ctx:
        def sb(name, shape, dt=F32):
            return ctx.enter_context(nc.sbuf_tensor(name, shape, dt))

        def sem(name):
            return ctx.enter_context(nc.semaphore(name))

        cst, x_all, xnT, keys = g["cst"], g["x_all"], g["xnT_all"], g["keys"]
        scores = sb("scores_sb", [P, 2, SEQ])
        best = sb("best", [P, 2, 8])
        picked = sb("picked", [P, TOPK], mybir.dt.uint32)
        pickedf = sb("pickedf", [P, TOPK])
        key_row = sb("key_row", [P, P])
        key_rows = sb("key_rows", [P, NPAIR], I32)
        wg, wu, wd = g["wg"], g["wu"], g["wd"]
        x_hi = sb("x_hi", [P, 2, KC, 512], F32R)
        x_lo = sb("x_lo", [P, 2, KC, 512], F32R)
        silu = sb("fsilu", [P, 2, 512])
        h = sb("fh", [P, 2, 512])
        h_hi = sb("h_hi", [P, 3, 512], F32R)
        h_lo = sb("h_lo", [P, 3, 512], F32R)
        b_g, b_u = g["banks"][0:2], g["banks"][2:4]
        b_y = (g["banks"][4:6], g["banks"][6:8])

        scores_loaded = sem("scores_loaded")
        wqo_loaded = sem("wqo_loaded")
        key_row_done = sem("key_row_done")
        key_turned = sem("key_turned")
        key_rows_done = sem("key_rows_done")
        keys_loaded = sem("keys_loaded")
        x_hi_done = sem("x_hi_done")
        x_lo_done = sem("x_lo_done")
        up_done = sem("fup_done")
        silu_done = sem("fsilu_done")
        h_done = sem("fh_done")
        h_hi_done = sem("h_hi_done")
        h_lo_done = sem("h_lo_done")
        down_done = sem("fdown_done")
        x_done = sem("fx_done")
        estep = sem("estep")
        block = ctx.enter_context(nc.Block())
        ident = cst[:, _C["ident"][0]:_C["ident"][1]]
        def supertiles(eng, body):
            body(0, True, False)
            body(1, False, False)
            with eng.Fori(2, NS // 2 - 1) as i:
                body(i, False, False)
            body(NS // 2 - 1, False, True)

        CHOSEN = 4 * MC - 4



        @block.sync
        def _(sp):
            sp.dma_start(scores[:, 0, :], dram["scores"]).then_inc(scores_loaded, 16)
            for name in ("wq", "wo"):
                sp.dma_start(g[name][:, :, :], ins[name + "1"].rearrange("(k p) n -> p k n", p=P)).then_inc(wqo_loaded, 16)
            sp.wait_ge(wqo_loaded, 32)

        @block.gpsimd
        def _(pool):
            pool.wait_ge(key_rows_done, 2)
            for p in range(NPAIR):
                pool.indirect_dma_start(out=keys[:, p, :], out_offset=None, in_=dram["kvrows"],
                                        in_offset=bass.IndirectOffsetOnAxis(ap=key_rows[:, p:p + 1], axis=0),
                                        bounds_check=TOKENS * H - 1, oob_is_err=False).then_inc(keys_loaded, 16)
            pool.wait_ge(keys_loaded, 16 * NPAIR)

        @block.scalar
        def _(act):
            def round_x(t, par):
                act.copy(x_hi[:, par, :, :], xnT[:, :, bass.ds(t * 512, 512)]).then_inc(x_hi_done, 1)

            round_x(0, 0)

            def body(i, first, last):
                for s in range(2):
                    for m in range(MC):
                        j = (2 * i + s) * MC + m
                        par = m % 2
                        act.wait_ge(up_done, j + 1)
                        wait(act, h_done, j - 1)
                        act.activation(silu[:, par, :], b_g[par][:, :], ACT.Silu, scale=INT_SCALE)\
                           .then_inc(silu_done, 1)
                        act.wait_ge(h_done, j + 1)
                        wait(act, down_done, 2 * (j - 2))
                        act.copy(h_hi[:, (s * MC + m) % 3, :], h[:, par, :]).then_inc(h_hi_done, 1)
                        if m == 1 and not (last and s == 1):
                            round_x(2 * i + s + 1, (s + 1) % 2)

            supertiles(act, body)

        @block.vector
        def _(dve):
            step = Chain(dve, estep)

            def rest_of_x(t, par):
                dve.wait_ge(x_hi_done, t + 1)
                dve.tensor_tensor(x_lo[:, par, :, :], xnT[:, :, bass.ds(t * 512, 512)],
                                  x_hi[:, par, :, :].bitcast(F32), ALU.subtract).then_inc(x_lo_done, 1)

            def choose_keys(piece):
                r, part = piece // 3, piece % 3
                src, dst = scores[:, r % 2, :], scores[:, (r + 1) % 2, :]
                if piece == 0:
                    dve.wait_ge(scores_loaded, 16)
                else:
                    step.wait()
                if part == 0:
                    step.mark(dve.max(best[:, r % 2, :], src))
                elif part == 1:
                    step.mark(dve.max_index(picked[:, 8 * r:8 * r + 8], best[:, r % 2, :], src))
                else:
                    step.mark(dve.match_replace(dst, best[:, r % 2, :], src, -BIG))

            def key_row_numbers():
                step.wait()
                step.mark(dve.tensor_copy(pickedf[:, :], picked[:, :]))
                step.wait()
                for k in range(2):
                    op = dve.tensor_scalar(key_row[:, k * TOPK:(k + 1) * TOPK], pickedf[:, :], float(H),
                                           cst[:, _C["keybase"][0]:_C["keybase"][1]], ALU.mult, ALU.add)
                op.then_inc(key_row_done, 1)

            def put_key_rows():
                dve.wait_ge(key_turned, 1)
                pairs = b_y[0][0][:, 0:P].rearrange("p (n two) -> p n two", two=2)
                dve.tensor_copy(key_rows[0:TOPK, :], pairs[0:TOPK, :, 0]).then_inc(key_rows_done, 1)
                dve.tensor_copy(key_rows[TOPK:P, :], pairs[TOPK:P, :, 1]).then_inc(key_rows_done, 1)

            def add(t, par, hf):
                dve.wait_ge(down_done, 2 * ((t + 1) * MC - 1) + hf + 1)
                rows = x_all[:, bass.ds(t * ST + 2 * hf, 2), :]
                dve.scalar_tensor_tensor(out=rows, in0=b_y[par][hf][:, :].rearrange("p (c n) -> p c n", c=2),
                                         scalar=INT_SCALE * INT_SCALE, in1=rows, op0=ALU.mult,
                                         op1=ALU.add).then_inc(x_done, 1)

            rest_of_x(0, 0)

            def body(i, first, last):
                for s in range(2):
                    for m in range(MC):
                        j = (2 * i + s) * MC + m
                        par, third = m % 2, (s * MC + m) % 3
                        dve.wait_ge(silu_done, j + 1)
                        wait(dve, h_hi_done, j - 1)
                        dve.tensor_tensor(h[:, par, :], silu[:, par, :], b_u[par][:, :], ALU.mult).then_inc(h_done, 1)
                        if m == 3 and not (last and s == 1):
                            rest_of_x(2 * i + s + 1, (s + 1) % 2)
                        if m in (2, 4) and not (first and s == 0):
                            add(2 * i + s - 1, (s + 1) % 2, m // 2 - 1)
                        if isinstance(j, int) and j < CHOSEN:
                            for piece in ((2 * j, 2 * j + 1) if j < 4 else (j + 4,)):
                                choose_keys(piece)
                        if isinstance(j, int) and j == CHOSEN:
                            key_row_numbers()
                        dve.wait_ge(h_hi_done, j + 1)
                        dve.tensor_tensor(h_lo[:, third, :], h[:, par, :], h_hi[:, third, :].bitcast(F32),
                                          ALU.subtract).then_inc(h_lo_done, 1)
                if isinstance(i, int) and i == 1:
                    put_key_rows()

            supertiles(dve, body)
            for hf in range(2):
                add(NS - 1, 1, hf)

        @block.tensor
        def _(pe):
            def up(i, s, m):
                t = 2 * i + s
                j = t * MC + m
                if m == 0:
                    pe.wait_ge(x_lo_done, t + 1)
                wait(pe, h_done, j - 1)
                for bank, w in ((b_g, wg), (b_u, wu)):
                    for x_part in (x_hi, x_lo):
                        for k in range(KC):
                            op = pe.matmul(bank[m % 2][:, :], w[:, k, m * P:(m + 1) * P], x_part[:, s, k, :],
                                           start=(x_part is x_hi and k == 0), stop=(x_part is x_lo and k == KC - 1))
                op.then_inc(up_done, 1)

            def down(t, s, m):
                j = t * MC + m
                if m == 0:
                    wait(pe, x_done, 2 * (t - 1))
                pe.wait_ge(h_lo_done, j + 1)
                for hf in range(2):
                    for q in (2 * hf, 2 * hf + 1):
                        for part in (h_hi, h_lo):
                            op = pe.matmul(b_y[s][hf][:, (q % 2) * D:(q % 2 + 1) * D],
                                           part[:, (s * MC + m) % 3, q * P:(q + 1) * P], wd[:, m, :],
                                           start=(m == 0 and q % 2 == 0 and part is h_hi),
                                           stop=(m == MC - 1 and q % 2 == 1 and part is h_lo), skip_group_check=True)
                    op.then_inc(down_done, 1)

            def body(i, first, last):
                for s in range(2):
                    for m in range(MC):
                        up(i, s, m)
                        if isinstance(i, int) and i == 1 and s == 1 and m == MC - 1:
                            pe.wait_ge(x_done, 6)
                            pe.wait_ge(key_row_done, 1)
                            pe.transpose(b_y[0][0][:, 0:P], key_row[:, :], ident).then_inc(key_turned, 1)
                        if s == 0 and m == 2 and not (isinstance(i, int) and i < 2):
                            pe.wait_ge(key_rows_done, 2)
                        if m >= 2:
                            down(2 * i + s, s, m - 2)
                        elif not (first and s == 0):
                            down(2 * i + s - 1, (s + 1) % 2, m + MC - 2)

            supertiles(pe, body)
            for m in (MC - 2, MC - 1):
                down(NS - 1, 1, m)


KEY_PLACES = [[(64 * j + 32 * pp, 64 * (1 - j) + 32 * pp, slice(j, 4, 2), slice(pp * P, (pp + 1) * P))
               for pp in range(2)] for j in range(2)]


def layer1_attention(nc, g, ins, out):
    with ExitStack() as ctx:
        def sb(name, shape, dt=F32):
            return ctx.enter_context(nc.sbuf_tensor(name, shape, dt))

        def sem(name):
            return ctx.enter_context(nc.semaphore(name))

        cst, x_all, xnT, keys = g["cst"], g["x_all"], g["xnT_all"], g["keys"]
        wq, wo = g["wq"], g["wo"]
        kz = sb("kz", [P, KC, 4, 32])
        kT = sb("kT1", [P, KC, P])
        kbd = sb("kbd", [P, 2, 4, 2, 2 * P], F32R)
        zero = sb("zero", [P, 1])
        vb = sb("vb", [P, 2, 8, 34])
        q_parts = sb("q_parts", [P, 2, 4, 512], F32R)
        smax = sb("smax", [P, 2, H])
        s_sb = sb("s_sb", [P, 2, H, TOPK])
        p_sb = sb("p_sb", [P, 2, H, TOPK])
        pT = sb("pT", [P, 2, 8, P])
        rden = sb("rden", [P, 2, H])
        att = sb("att", [P, 2, D])
        attT = sb("attT", [P, 2, KC, P])
        b_s, b_p, b_q, b_o, b_w = g["banks"][0:2], g["banks"][2:4], g["banks"][4], g["banks"][5], g["banks"][6]
        b_k = g["banks"][7]

        zero_done = sem("zero_done")
        kz_done = sem("kz_done")
        k_turned = sem("k_turned")
        kT_done = sem("kT_done")
        k_hi_done = sem("k_hi_done")
        q_hi_done = sem("q_hi_done")
        kbd_zero = sem("kbd_zero")
        kbd_done = sem("kbd_done")
        vb_done = sem("vb_done")
        qp_done = sem("q1p_done")
        qT_done = sem("q1T_done")
        s_done = sem("s1_done")
        sub_done = sem("sub_done")
        exp_done = sem("exp_done")
        p_turned = sem("p_turned")
        pT_done = sem("pT_done")
        av_done = sem("av_done")
        att_done = sem("att_done")
        att_turned = sem("att_turned")
        attT_done = sem("attT_done")
        wo_done = sem("wo_done")
        out_done = sem("out_done")
        stored = sem("stored")
        rec_done = sem("rec_done")
        fstep = sem("fstep")
        block = ctx.enter_context(nc.Block())
        ident = cst[:, _C["ident"][0]:_C["ident"][1]]
        low = cst[:, _C["lowkeys"][0]:_C["lowkeys"][1]]
        high = cst[:, _C["highkeys"][0]:_C["highkeys"][1]]
        out_v = out.rearrange("b (c p) d -> (b c) p d", p=P)

        def pairs_of_batches(eng, body):
            body(0, True, False)
            with eng.Fori(1, BATCH // 2 - 1) as i:
                body(i, False, False)
            body(BATCH // 2 - 1, False, True)


        @block.sync
        def _(sp):
            def body(i, first, last):
                for c in range(2 * BT):
                    n = i * (2 * BT) + c
                    sp.wait_ge(out_done, n + 1)
                    sp.dma_start(out_v[n], x_all[:, n, :]).then_inc(stored, 16)

            pairs_of_batches(sp, body)
            sp.wait_ge(stored, 16 * NT)

        @block.gpsimd
        def _(pool):
            pool.memset(zero[:, :], 0.0)
            pool.memset(vb[:, :, :, :], 0.0).then_inc(zero_done, 1)
            pool.wait_ge(zero_done, 1)
            for par in range(2):
                pool.tensor_scalar(vb[:, par, :, 16], vb[:, par, :, 16], low, None, ALU.add)
                pool.tensor_scalar(vb[:, par, :, 33], vb[:, par, :, 33], high, None, ALU.add)

            def body(i, first, last):
                for par in range(2):
                    b = 2 * i + par
                    kv = keys[:, bass.ds(b * 8, 8), :]
                    wait(pool, k_turned, b)
                    k_in = kv[:, :, 0:16].rearrange("p (k a) e -> p k a e", k=KC)
                    pool.tensor_tensor(kz[:, :, :, 0:16], k_in, low.unsqueeze(2).unsqueeze(3).broadcast_to(k_in.shape),
                                       ALU.mult)
                    pool.tensor_tensor(kz[:, :, :, 16:32], k_in,
                                       high.unsqueeze(2).unsqueeze(3).broadcast_to(k_in.shape),
                                       ALU.mult).then_inc(kz_done, 1)
                    wait(pool, av_done, (b - 1) * BT)
                    v_in = kv[:, :, 16:32]
                    pool.tensor_tensor(vb[:, par, :, 0:16], v_in, low.unsqueeze(2).broadcast_to(v_in.shape), ALU.mult)
                    pool.tensor_tensor(vb[:, par, :, 17:33], v_in, high.unsqueeze(2).broadcast_to(v_in.shape), ALU.mult)\
                        .then_inc(vb_done, 1)

            pairs_of_batches(pool, body)

        @block.scalar
        def _(act):
            def put_kT(b):
                act.wait_ge(k_turned, b + 1)
                wait(act, kbd_done, 2 * b)
                act.copy(kT[:, :, :], b_k[:, 0:256].rearrange("p (k t) -> p k t", k=KC)).then_inc(kT_done, 1)

            def round_keys(b, par, j):
                if isinstance(b, int) and b == 0:
                    act.wait_ge(kT_done, 1)
                    act.wait_ge(kbd_zero, 2)
                else:
                    act.wait_ge(kT_done, b + 1)
                wait(act, s_done, 2 * BT * (b - 1))
                for at, twin, slots, cols in KEY_PLACES[j]:
                    for to in (at, twin):
                        op = act.copy(kbd[to:to + 32, par, slots, 0, cols], kT[at:at + 32, :, :])
                op.then_inc(k_hi_done, 1)

            def put_q(q, par, k):
                act.wait_ge(qp_done, 2 * q + k + 1)
                act.activation(q_parts[0:64, par, 2 * k, :], b_q[0:64, :], ACT.Copy, scale=HD ** -0.5)
                act.activation(q_parts[64:P, par, 2 * k + 1, :], b_q[64:P, :], ACT.Copy,
                               scale=HD ** -0.5).then_inc(q_hi_done, 1)

            def exps(n, par):
                act.wait_ge(sub_done, 2 * n + 2)
                wait(act, p_turned, 2 * (n - 1))
                act.activation(p_sb[:, par, :, :], s_sb[:, par, :, :], ACT.Exp).then_inc(exp_done, 1)

            def put_pT(n, par):
                for hf in range(2):
                    act.wait_ge(p_turned, 2 * n + hf + 1)
                    wait(act, av_done, n - 1)
                    act.copy(pT[:, par, 4 * hf:4 * hf + 4, :], b_p[hf][:, :].rearrange("p (a t) -> p a t", a=4))\
                       .then_inc(pT_done, 1)

            def put_attT(n, par):
                act.wait_ge(att_turned, n + 1)
                wait(act, wo_done, n - 1)
                act.copy(attT[:, par, :, :], b_k[:, 256:512].rearrange("p (k t) -> p k t", k=KC))\
                   .then_inc(attT_done, 1)

            for k in range(KC):
                put_q(0, 0, k)
            put_kT(0)
            for j in range(2):
                round_keys(0, 0, j)
            exps(0, 0)

            def body(i, first, last):
                for c in range(2 * BT):
                    n = i * (2 * BT) + c
                    if c % BT == ST and not (last and c == BT + ST):
                        put_kT(2 * i + c // BT + 1)
                    if c % ST < KC and not (last and c >= 2 * BT - ST):
                        put_q(4 * i + c // ST + 1, (c // ST + 1) % 2, c % ST)
                    put_pT(n, c % 2)
                    if not (last and c == 2 * BT - 1):
                        exps(n + 1, (c + 1) % 2)
                    if not (first and c < 2):
                        put_attT(n - 2, c % 2)
                    if ST <= c % BT < ST + 2 and not (last and c >= BT):
                        round_keys(2 * i + c // BT + 1, (c // BT + 1) % 2, c % BT - ST)

            pairs_of_batches(act, body)
            put_attT(NT - 2, 0)
            put_attT(NT - 1, 1)

        @block.vector
        def _(dve):
            dve.wait_ge(zero_done, 1)
            for par in range(2):
                dve.tensor_copy(kbd[:, par, :, :, :].rearrange("p a b c -> p (a b c)"),
                                zero[:, :].broadcast_to([P, 16 * P])).then_inc(kbd_zero, 1)

            def rest_of_keys(b, par, j):
                dve.wait_ge(k_hi_done, 2 * b + j + 1)
                for at, twin, slots, cols in KEY_PLACES[j]:
                    rounded = kbd[at:at + 32, par, slots, 0, cols].bitcast(F32)
                    for to in (at, twin):
                        op = dve.tensor_tensor(kbd[to:to + 32, par, slots, 1, cols], kT[at:at + 32, :, :], rounded,
                                               ALU.subtract)
                op.then_inc(kbd_done, 1)

            def rest_of_q(q, par, k):
                dve.wait_ge(q_hi_done, 2 * q + k + 1)
                for j, (at, twin) in enumerate(((0, 64), (64, 0))):
                    slot = 2 * k + j
                    op = dve.scalar_tensor_tensor(out=q_parts[twin:twin + 64, par, slot, :], in0=b_q[at:at + 64, :],
                                                  scalar=HD ** -0.5, in1=q_parts[at:at + 64, par, slot, :].bitcast(F32),
                                                  op0=ALU.mult, op1=ALU.subtract)
                op.then_inc(qT_done, 1)

            def subtract_max(n, par, k):
                heads = slice(8 * k, 8 * k + 8)
                sc = b_s[k][:, :].rearrange("p (h j) -> p h j", j=TOPK)
                step = Chain(dve, fstep, 2 * n + k)
                dve.wait_ge(s_done, 2 * n + k + 1)
                step.mark(dve.tensor_reduce(smax[:, par, heads], sc, AX_X, ALU.max))
                step.wait()
                wait(dve, exp_done, n - 1)
                dve.tensor_tensor(s_sb[:, par, heads, :], sc, bcast(smax[:, par, heads], 2, TOPK),
                                  ALU.subtract).then_inc(sub_done, 1)

            def normalise(n, par):
                dve.wait_ge(av_done, n + 1)
                wait(dve, att_turned, n - 1)
                o = b_o[:, 0:272].rearrange("p (a x e) -> p a x e", a=8, x=2)
                dve.reciprocal(rden[:, par, :].rearrange("p (a x) -> p a x", x=2), o[:, :, :, 16]).then_inc(rec_done, 1)
                dve.wait_ge(rec_done, n + 1)
                dve.tensor_tensor(att[:, par, :].rearrange("p (a x e) -> p a x e", a=8, x=2), o[:, :, :, 0:16],
                                  bcast(rden[:, par, :].rearrange("p (a x) -> p a x", x=2), 3, 16),
                                  ALU.mult).then_inc(att_done, 1)

            def residual(n):
                dve.wait_ge(wo_done, n + 1)
                dve.tensor_tensor(x_all[:, n, :], x_all[:, n, :], b_w[:, 0:256], ALU.add).then_inc(out_done, 1)

            for k in range(KC):
                rest_of_q(0, 0, k)
            for j in range(2):
                rest_of_keys(0, 0, j)
            for k in range(2):
                subtract_max(0, 0, k)

            def body(i, first, last):
                for c in range(2 * BT):
                    n = i * (2 * BT) + c
                    if not (last and c == 2 * BT - 1):
                        for k in range(2):
                            subtract_max(n + 1, (c + 1) % 2, k)
                    if c % ST < KC and not (last and c >= 2 * BT - ST):
                        rest_of_q(4 * i + c // ST + 1, (c // ST + 1) % 2, c % ST)
                    if ST + 1 <= c % BT < ST + 3 and not (last and c >= BT):
                        rest_of_keys(2 * i + c // BT + 1, (c // BT + 1) % 2, c % BT - ST - 1)
                    if not (first and c == 0):
                        normalise(n - 1, (c + 1) % 2)
                    if not (first and c < 3):
                        residual(n - 3)

            pairs_of_batches(dve, body)
            normalise(NT - 1, 1)
            for n in range(NT - 3, NT):
                residual(n)

        @block.tensor
        def _(pe):
            def turn_keys(b):
                pe.wait_ge(kz_done, b + 1)
                wait(pe, kT_done, b)
                for k in range(KC):
                    op = pe.transpose(b_k[:, k * P:(k + 1) * P], kz[:, k, :, :], ident)
                op.then_inc(k_turned, 1)

            def project_q(q, k):
                wait(pe, qT_done, 2 * q + k)
                for kc in range(KC):
                    op = pe.matmul(b_q[:, :], wq[:, kc, k * P:(k + 1) * P], xnT[:, kc, bass.ds(q * 512, 512)],
                                   start=(kc == 0), stop=(kc == KC - 1))
                op.then_inc(qp_done, 1)

            def scores(n, c, bpar, q):
                if c % ST == 0:
                    pe.wait_ge(qT_done, 2 * q + 2)
                for k in range(KC):
                    wait(pe, sub_done, 2 * (n - 1) + k + 1)
                    for slot in (2 * k, 2 * k + 1):
                        for part in range(2):
                            op = pe.matmul(b_s[k][:, (slot % 2) * 256:(slot % 2 + 1) * 256],
                                           q_parts[:, c // ST % 2, slot, (c % ST) * P:(c % ST + 1) * P],
                                           kbd[:, bpar, slot, part, :], start=(part == 0), stop=(part == 1))
                    op.then_inc(s_done, 1)

            def turn_p(n, par):
                pe.wait_ge(exp_done, n + 1)
                for hf in range(2):
                    wait(pe, pT_done, 2 * (n - 1) + hf + 1)
                    for a in range(4):
                        h = 8 * hf + 2 * a
                        op = pe.transpose(b_p[hf][:, a * P:(a + 1) * P], p_sb[:, par, h:h + 2, :], ident)
                    op.then_inc(p_turned, 1)

            def attend(n, par, bpar):
                wait(pe, att_done, n)
                for hf in range(2):
                    pe.wait_ge(pT_done, 2 * n + hf + 1)
                    for a in range(4 * hf, 4 * hf + 4):
                        op = pe.matmul(b_o[:, 34 * a:34 * a + 34], pT[:, par, a, :], vb[:, bpar, a, :], start=True,
                                       stop=True)
                op.then_inc(av_done, 1)

            def turn_att(n, par):
                pe.wait_ge(att_done, n + 1)
                wait(pe, attT_done, n)
                for k in range(KC):
                    op = pe.transpose(b_k[:, 256 + k * P:256 + (k + 1) * P], att[:, par, k * P:(k + 1) * P], ident)
                op.then_inc(att_turned, 1)

            def output(n, par):
                pe.wait_ge(attT_done, n + 1)
                wait(pe, out_done, n)
                for k in range(KC):
                    op = pe.matmul(b_w[:, 0:256], attT[:, par, k, :], wo[:, k, :], start=(k == 0), stop=(k == KC - 1))
                op.then_inc(wo_done, 1)

            for k in range(KC):
                project_q(0, k)
            turn_keys(0)
            pe.wait_ge(kbd_done, 2)
            scores(0, 0, 0, 0)

            def body(i, first, last):
                for c in range(2 * BT):
                    n = i * (2 * BT) + c
                    if c % BT == ST and not (last and c == BT + ST):
                        pe.wait_ge(attT_done, n - 2)
                        turn_keys(2 * i + c // BT + 1)
                    if c % ST < KC and not (last and c >= 2 * BT - ST):
                        project_q(4 * i + c // ST + 1, c % ST)
                    if not (last and c == 2 * BT - 1):
                        d = (c + 1) % (2 * BT)
                        if d % BT == 0:
                            pe.wait_ge(kbd_done, 4 * i + 2 * ((c + 1) // BT) + 2)
                        scores(n + 1, d, d // BT, 4 * i + (c + 1) // ST)
                    turn_p(n, c % 2)
                    if not (first and c == 0):
                        attend(n - 1, (c + 1) % 2, (c + 2 * BT - 1) % (2 * BT) // BT)
                    if c % BT == 0:
                        pe.wait_ge(vb_done, 2 * i + c // BT + 1)
                    if not (first and c < 3):
                        output(n - 3, (c + 1) % 2)
                    if c % BT == ST and not (last and c == BT + ST):
                        pe.wait_ge(kT_done, 2 * i + c // BT + 2)
                    if not (first and c < 2):
                        turn_att(n - 2, c % 2)

            pairs_of_batches(pe, body)
            attend(NT - 1, 1, 1)
            output(NT - 3, 1)
            turn_att(NT - 2, 0)
            output(NT - 2, 0)
            turn_att(NT - 1, 1)
            output(NT - 1, 1)


def layers(nc, ins, out):
    with ExitStack() as ctx:
        def sb(name, shape, dt=F32):
            return ctx.enter_context(nc.sbuf_tensor(name, shape, dt))

        g = {"cst": sb("csts", [P, CW]), "x_all": sb("x_all", [P, NT, D]),
             "ln": {"ve": sb("ln_ve", [P, BT]), "r": sb("ln_r", [P, BT]), "t": sb("ln_t", [P, BT]),
                    "st": sb("ln_st", [P, BT, 6]), "mv": sb("ln_mv", [P, BT, 2]), "rstd": sb("ln_rstd", [P, NT]),
                    "nmr": sb("ln_nmr", [P, NT])},
             "banks": [ctx.enter_context(nc.psum_tensor(f"bank{i}", [P, 512], F32)) for i in range(8)]}
        dram = {"xrows": nc.dram_tensor("xrows", (ROWS, XW), F32).ap(),
                "x1": nc.dram_tensor("x1_sum", (ROWS, D), F32).ap(),
                "slots": nc.dram_tensor("slot_table", (NE * CAP,), F32).ap(),
                "kvrows": nc.dram_tensor("kvrows", (TOKENS * H, 2 * HD), F32).ap(),
                "scores": nc.dram_tensor("key_scores", (BATCH * H, SEQ), F32).ap()}
        with ExitStack() as c0:
            g["place"] = c0.enter_context(nc.sbuf_tensor("place", [P, NT, NE], F32))
            g["slot_rows"] = c0.enter_context(nc.sbuf_tensor("slot_rows", [P, 2 * NE], I32))
            layer0_dense(nc, g, ins, dram)
            expert_slots(nc, g, dram)
            routed_experts(nc, g, ins, dram)
        g["xnT_all"] = sb("xnT_all", [P, KC, TOKENS])
        g["keys"] = sb("keys", [P, NPAIR, 2 * HD])
        g["wq"], g["wo"] = sb("wq1_sb", [P, KC, D]), sb("wo1_sb", [P, KC, D])
        with ExitStack() as c1:
            for name, shape in (("wg", [P, KC, HID]), ("wu", [P, KC, HID]), ("wd", [P, MC, D])):
                g[name] = c1.enter_context(nc.sbuf_tensor(name, shape, F32R))
            layer1_project(nc, g, ins, dram)
            layer1_ffn_and_keys(nc, g, ins, dram)
        layer1_attention(nc, g, ins, out)


def kernel(**inputs):
    import concourse.bacc as bacc
    from concourse.bass_utils import run_bass_kernel_spmd

    a = {k: np.asarray(v) for k, v in inputs.items()}
    qk_w, qk_b = a["L0_attn_Wqk_w"], a["L0_attn_Wqk_b"]
    columns = [qk_w[D:], a["L0_attn_Wv_w"], qk_w[:D], a["L0_attn_Wn_w"], a["L0_ffn_gate_w"]]
    biases = [qk_b[D:], a["L0_attn_Wv_b"], qk_b[:D], a["L0_attn_Wn_b"], np.zeros(NE, np.float32)]
    arrays = {
        "x": a["L0_attn_x"],
        "cst": shape_constants(),
        "wproj": np.concatenate(columns).T,
        "bproj": np.tile(np.concatenate(biases), (P, 1)),
        "wo": a["L0_attn_Wo_w"].T,
        "bo": np.tile(a["L0_attn_Wo_b"], (P, 1)),
        "wsu": a["L0_ffn_shared_w_gate_up"],
        "wsd": a["L0_ffn_shared_w_down"],
        "wup": a["L0_ffn_w_gate_up"],
        "wdn": a["L0_ffn_w_down"],
        "wkv1": np.concatenate([a["L1_attn_Wk"], a["L1_attn_Wv"]]).T,
        "wsc": np.tile(a["L1_attn_w_score"], (P, 1)),
        "wq1": a["L1_attn_Wq"].T,
        "wo1": a["L1_attn_Wo"].T,
        "wg1": a["L1_ffn_w_gate"].T,
        "wu1": a["L1_ffn_w_up"].T,
        "wd1": a["L1_ffn_w_down"].T,
    }
    nc = bacc.Bacc("TRN2", target_bir_lowering=False, num_devices=1)
    feed, ins = {}, {}
    for name, v in arrays.items():
        v = np.ascontiguousarray(v)
        feed["in_" + name] = v
        ins[name] = nc.dram_tensor("in_" + name, v.shape, mybir.dt.from_np(v.dtype), kind="ExternalInput").ap()
    out = nc.dram_tensor("out", (BATCH, SEQ, D), F32, kind="ExternalOutput").ap()
    layers(nc, ins, out)
    r = run_bass_kernel_spmd(nc, [feed], core_ids=[0])
    return r.results[0]["out"]
```
